# Optimizing a Trainium2 kernel written in Bass

```python
import numpy as np
import jax
import jax.numpy as jnp

def _softmax(x, axis=-1):
    return jax.nn.softmax(x, axis=axis)

def _gelu(x):
    return jax.nn.gelu(x, approximate=True)

def _silu(x):
    return jax.nn.silu(x)

def _sigmoid(x):
    return jax.nn.sigmoid(x)

def _layernorm(x, axis=-1, eps=1e-05):
    m = jnp.mean(x, axis=axis, keepdims=True)
    v = jnp.var(x, axis=axis, keepdims=True)
    return (x - m) / jnp.sqrt(v + eps)

def _scatter_add(tgt, idx, src, axis=0):
    return tgt.at[idx].add(src)

def _segment_sum(src, seg, n):
    return jax.ops.segment_sum(src, seg, n)
kernel_name = 'mk_audio_tower_d1_tok_audfeat1024_r4_ddba73'

def setup_inputs(seed: int=0):
    np.random.seed(seed)
    _w = jnp.asarray

    def _rec_inputs():
        import jax
        import jax.numpy as jnp
        _rk = jax.random.key(seed)
        x = -0.000392918 + 0.999932 * jax.random.normal(jax.random.fold_in(_rk, 1), (16, 256, 128), jnp.float32)
        return x
    x = _rec_inputs()

    def _L0_tok_setup():
        import jax, jax.numpy as jnp
        import numpy as np
        CONTEXT = 5
        DILATION = 1
        EPS = 1e-05
        key = jax.random.key(seed)
        ks = jax.random.split(key, 6)
        B, T, D, O = (32, 1024, 128, 256)
        K = D * CONTEXT
        x = jax.random.normal(ks[0], (B, T, D), dtype=jnp.float32)
        W = jax.random.normal(ks[1], (O, K), dtype=jnp.float32) * 0.02
        b = jnp.zeros((O,), dtype=jnp.float32)
        gamma = jnp.ones((O,), dtype=jnp.float32)
        beta = jnp.zeros((O,), dtype=jnp.float32)
        running_mean = jax.random.normal(ks[2], (O,), dtype=jnp.float32) * 0.1
        running_var = jax.random.uniform(ks[3], (O,), dtype=jnp.float32, minval=0.5, maxval=1.5)
        return {'x': x, 'W': W, 'b': b, 'gamma': gamma, 'beta': beta, 'running_mean': running_mean, 'running_var': running_var}
    _L0_tok_all = _L0_tok_setup()
    _L0_tok_in = {k: v for k, v in _L0_tok_all.items() if k in ('W', 'b', 'gamma', 'beta', 'running_mean', 'running_var')}
    del _L0_tok_all

    def _L0_attn_setup():
        import jax, jax.numpy as jnp
        import numpy as np
        import math
        NUM_BUCKETS = 32
        MAX_DISTANCE = 128
        HEADS = 16
        D_MODEL = 256

        def _relative_position_bucket(rel_pos, num_buckets=NUM_BUCKETS, max_distance=MAX_DISTANCE):
            n = jnp.maximum(-rel_pos, 0)
            max_exact = num_buckets // 2
            is_small = n < max_exact
            val_large = max_exact + (jnp.log(jnp.maximum(n, 1).astype(jnp.float32) / max_exact) / math.log(max_distance / max_exact) * (num_buckets - max_exact)).astype(jnp.int32)
            val_large = jnp.minimum(val_large, num_buckets - 1)
            return jnp.where(is_small, n, val_large)
        key = jax.random.key(seed)
        ks = jax.random.split(key, 7)
        d = D_MODEL
        s = 1.0 / math.sqrt(d)
        x = jax.random.normal(ks[0], (2, 512, d), dtype=jnp.float32)
        Wq = jax.random.normal(ks[1], (d, d), dtype=jnp.float32) * s
        Wk = jax.random.normal(ks[2], (d, d), dtype=jnp.float32) * s
        Wv = jax.random.normal(ks[3], (d, d), dtype=jnp.float32) * s
        Wo = jax.random.normal(ks[4], (d, d), dtype=jnp.float32) * s
        bo = jnp.zeros((d,), dtype=jnp.float32)
        rel_emb = jax.random.normal(ks[5], (NUM_BUCKETS, HEADS), dtype=jnp.float32) * 0.02
        return {'x': x, 'Wq': Wq, 'Wk': Wk, 'Wv': Wv, 'Wo': Wo, 'bo': bo, 'rel_emb': rel_emb}
    _L0_attn_all = _L0_attn_setup()
    _L0_attn_in = {k: v for k, v in _L0_attn_all.items() if k in ('Wq', 'Wk', 'Wv', 'Wo', 'bo', 'rel_emb')}
    del _L0_attn_all

    def _L0_ffn_setup():
        import jax, jax.numpy as jnp
        import numpy as np
        BLOCK = 32
        W_BITS = 4
        ACT_BITS = 16

        def act_qdq(x):
            qmax = 2.0 ** (ACT_BITS - 1) - 1.0
            scale = jnp.maximum(jnp.max(jnp.abs(x)) / qmax, 1e-12)
            return jnp.clip(jnp.round(x / scale), -qmax - 1.0, qmax) * scale

        def fixed_qdq_u16(x):
            scale = 1.0 / 65536.0
            return jnp.clip(jnp.round(x / scale), 0.0, 65535.0) * scale

        def lpbq_dequant(w):
            O, I = w.shape
            qmax = 2.0 ** (W_BITS - 1) - 1.0
            wb = w.reshape(O, I // BLOCK, BLOCK)
            s = jnp.maximum(jnp.max(jnp.abs(wb), axis=-1, keepdims=True) / qmax, 1e-12)
            wq = jnp.clip(jnp.round(wb / s), -qmax - 1.0, qmax) * s
            return wq.reshape(O, I)
        key = jax.random.key(seed)
        k1, k2, k3, k4 = jax.random.split(key, 4)
        B, S, H, I = (2, 1024, 256, 768)
        x = jax.random.normal(k1, (B, S, H), jnp.float32)
        w_gate = jax.random.normal(k2, (I, H), jnp.float32) * 0.02
        w_up = jax.random.normal(k3, (I, H), jnp.float32) * 0.02
        w_down = jax.random.normal(k4, (H, I), jnp.float32) * 0.02
        return {'x': x, 'w_gate': w_gate, 'w_up': w_up, 'w_down': w_down}
    _L0_ffn_all = _L0_ffn_setup()
    _L0_ffn_in = {k: v for k, v in _L0_ffn_all.items() if k in ('w_gate', 'w_up', 'w_down')}
    del _L0_ffn_all
    return {'x': x, 'L0_tok_W': _L0_tok_in['W'], 'L0_tok_b': _L0_tok_in['b'], 'L0_tok_gamma': _L0_tok_in['gamma'], 'L0_tok_beta': _L0_tok_in['beta'], 'L0_tok_running_mean': _L0_tok_in['running_mean'], 'L0_tok_running_var': _L0_tok_in['running_var'], 'L0_attn_Wq': _L0_attn_in['Wq'], 'L0_attn_Wk': _L0_attn_in['Wk'], 'L0_attn_Wv': _L0_attn_in['Wv'], 'L0_attn_Wo': _L0_attn_in['Wo'], 'L0_attn_bo': _L0_attn_in['bo'], 'L0_attn_rel_emb': _L0_attn_in['rel_emb'], 'L0_ffn_w_gate': _L0_ffn_in['w_gate'], 'L0_ffn_w_up': _L0_ffn_in['w_up'], 'L0_ffn_w_down': _L0_ffn_in['w_down']}

def reference(x, L0_tok_W, L0_tok_b, L0_tok_gamma, L0_tok_beta, L0_tok_running_mean, L0_tok_running_var, L0_attn_Wq, L0_attn_Wk, L0_attn_Wv, L0_attn_Wo, L0_attn_bo, L0_attn_rel_emb, L0_ffn_w_gate, L0_ffn_w_up, L0_ffn_w_down):
    import jax
    import jax.numpy as jnp

    def _L0_tok_ref(x, W, b, gamma, beta, running_mean, running_var):
        import jax, jax.numpy as jnp
        import numpy as np
        CONTEXT = 5
        DILATION = 1
        EPS = 1e-05
        B, T, D = x.shape
        Tp = T - DILATION * (CONTEXT - 1)
        idx = jnp.arange(Tp)[:, None] + jnp.arange(CONTEXT)[None, :] * DILATION
        win = x[:, idx, :].reshape(B, Tp, CONTEXT * D)
        h = jnp.einsum('btk,ok->bto', win, W) + b
        h = jax.nn.relu(h)
        h = gamma * (h - running_mean) * jax.lax.rsqrt(running_var + EPS) + beta
        return h

    def _L0_attn_ref(x, Wq, Wk, Wv, Wo, bo, rel_emb):
        import jax, jax.numpy as jnp
        import numpy as np
        import math
        NUM_BUCKETS = 32
        MAX_DISTANCE = 128
        HEADS = 16
        D_MODEL = 256

        def _relative_position_bucket(rel_pos, num_buckets=NUM_BUCKETS, max_distance=MAX_DISTANCE):
            n = jnp.maximum(-rel_pos, 0)
            max_exact = num_buckets // 2
            is_small = n < max_exact
            val_large = max_exact + (jnp.log(jnp.maximum(n, 1).astype(jnp.float32) / max_exact) / math.log(max_distance / max_exact) * (num_buckets - max_exact)).astype(jnp.int32)
            val_large = jnp.minimum(val_large, num_buckets - 1)
            return jnp.where(is_small, n, val_large)
        b, n, d = x.shape
        h = HEADS
        dh = d // h
        scale = dh ** (-0.5)
        q = (x @ Wq).reshape(b, n, h, dh).transpose(0, 2, 1, 3)
        k = (x @ Wk).reshape(b, n, h, dh).transpose(0, 2, 1, 3)
        v = (x @ Wv).reshape(b, n, h, dh).transpose(0, 2, 1, 3)
        sim = jnp.einsum('bhid,bhjd->bhij', q, k) * scale
        pos = jnp.arange(n, dtype=jnp.int32)
        rel_pos = pos[None, :] - pos[:, None]
        buckets = _relative_position_bucket(rel_pos)
        bias = rel_emb[buckets]
        sim = sim + jnp.transpose(bias, (2, 0, 1))[None]
        mask_value = -jnp.finfo(sim.dtype).max
        causal_mask = jnp.triu(jnp.ones((n, n), dtype=bool), k=1)
        sim = jnp.where(causal_mask[None, None], mask_value, sim)
        attn = jax.nn.softmax(sim, axis=-1)
        out = jnp.einsum('bhij,bhjd->bhid', attn, v)
        out = out.transpose(0, 2, 1, 3).reshape(b, n, d)
        return out @ Wo + bo

    def _L0_ffn_ref(x, w_gate, w_up, w_down):
        import jax, jax.numpy as jnp
        import numpy as np
        BLOCK = 32
        W_BITS = 4
        ACT_BITS = 16

        def act_qdq(x):
            qmax = 2.0 ** (ACT_BITS - 1) - 1.0
            scale = jnp.maximum(jnp.max(jnp.abs(x)) / qmax, 1e-12)
            return jnp.clip(jnp.round(x / scale), -qmax - 1.0, qmax) * scale

        def fixed_qdq_u16(x):
            scale = 1.0 / 65536.0
            return jnp.clip(jnp.round(x / scale), 0.0, 65535.0) * scale

        def lpbq_dequant(w):
            O, I = w.shape
            qmax = 2.0 ** (W_BITS - 1) - 1.0
            wb = w.reshape(O, I // BLOCK, BLOCK)
            s = jnp.maximum(jnp.max(jnp.abs(wb), axis=-1, keepdims=True) / qmax, 1e-12)
            wq = jnp.clip(jnp.round(wb / s), -qmax - 1.0, qmax) * s
            return wq.reshape(O, I)
        x = act_qdq(x)
        up = act_qdq(x @ lpbq_dequant(w_up).T)
        gate = act_qdq(x @ lpbq_dequant(w_gate).T)
        sig = fixed_qdq_u16(jax.nn.sigmoid(gate))
        gate = act_qdq(gate * sig)
        o = act_qdq(gate * up)
        return o @ lpbq_dequant(w_down).T
    h = _L0_tok_ref(x, L0_tok_W, L0_tok_b, L0_tok_gamma, L0_tok_beta, L0_tok_running_mean, L0_tok_running_var)
    h = h + _L0_attn_ref(_layernorm(h, axis=-1), L0_attn_Wq, L0_attn_Wk, L0_attn_Wv, L0_attn_Wo, L0_attn_bo, L0_attn_rel_emb)
    h = h + _L0_ffn_ref(_layernorm(h, axis=-1), L0_ffn_w_gate, L0_ffn_w_up, L0_ffn_w_down)
    return h

_drawn_inputs = setup_inputs


def setup_inputs(seed=0):
    import zlib

    import numpy as np

    out = dict(_drawn_inputs(seed))
    spreads = {'L0_tok_b': (0.0, 0.1),
     'L0_tok_gamma': (1.0, 0.2),
     'L0_tok_beta': (0.0, 0.1),
     'L0_attn_bo': (0.0, 0.1)}
    factors = {'L0_attn_rel_emb': 8.0}
    for name, (base, spread) in spreads.items():
        noise = np.random.default_rng([zlib.crc32(name.encode()), seed]).standard_normal(out[name].shape)
        drawn = base * np.exp(spread * noise) if base else spread * noise
        out[name] = jnp.asarray(drawn.astype(out[name].dtype))
    for name, factor in factors.items():
        out[name] = (out[name] * factor).astype(out[name].dtype)
    return out
```

```python
import math
from contextlib import ExitStack

import numpy as np

import concourse.bass as bass
from concourse import mybir

F32, F16, BF16 = mybir.dt.float32, mybir.dt.float16, mybir.dt.bfloat16
I16, U16, I32 = mybir.dt.int16, mybir.dt.uint16, mybir.dt.int32
ALU = mybir.AluOpType
ACT = mybir.ActivationFunctionType
X = mybir.AxisListType.X
ABSMAX = bass.bass_isa.ReduceOp.absmax

B, T, D = 16, 256, 128
CTX = 5
N = T - CTX + 1
TT = N // 2
C = 256
H, DH = 16, 16
KT = C // 128
NP = 256
G = 4
INNER, MT = 768, 6
BUCKETS, MAXDIST = 32, 128
LINE = TT - 1 + N
MASKED = -3.0e38
EPS = 1e-5
QMAX, WQMAX, BLOCK = 32767.0, 7.0, 32
FLOOR = 1e-12
CH, UW = 8, 3 * 2 * N
HP = CTX - 1

W_CONV, W_Q, W_K, W_V, W_O, W_GATE, W_UP, W_DOWN = range(8)


def bucket_onehot():
    n = np.arange(-(TT - 1), N)
    large = BUCKETS // 2 + (np.log(np.maximum(n, 1) / (BUCKETS // 2)) / math.log(MAXDIST / (BUCKETS // 2))
                            * (BUCKETS - BUCKETS // 2)).astype(np.int64)
    bucket = np.where(n < BUCKETS // 2, n, np.minimum(large, BUCKETS - 1))
    hot = ((np.arange(BUCKETS)[:, None] == bucket[None, :]) & (n >= 0)[None, :]).astype(np.float32)
    return np.concatenate([hot, hot[:, ::-1]], axis=1)


def audio_tower(nc, x, cw, cb, gamma, beta, rmean, rvar, wq, wk, wv, wo, bo, rel, wg, wu, wd, hot, out):
    with ExitStack() as ctx:
        def sb(name, shape, dt=F32, scope=None):
            return (scope or ctx).enter_context(nc.sbuf_tensor(name, shape, dt))

        def sem(name):
            return ctx.enter_context(nc.semaphore(name))

        ps = ctx.enter_context(nc.psum_tensor("ps", [128, 8, 512], F32))

        line_t = nc.dram_tensor("line_t", (H, LINE), F32)
        line_n = nc.dram_tensor("line_n", (H, LINE), BF16)
        res = nc.dram_tensor("res", (B, TT, 2 * C), F32)
        up_raw = nc.dram_tensor("up_raw", (CH, 2, 128, UW), F32)

        identf = sb("identf", [128, 128])
        x2t = sb("x2t", [128, B, KT, N])
        wscale = sb("wscale", [128, 8])
        winv = sb("winv", [128, 8])
        wgT = sb("wgT", [128, 2, KT, INNER], F16)
        wuT = sb("wuT", [128, 2, KT, INNER], F16)
        wdT = sb("wdT", [128, 2, MT, C], F16)
        amax_x = sb("amax_x", [128, B])

        names = """nhalf_set w_loaded consts wamax wall wpow winv_s wdq_s wdq_i wdq_w wT_ps wT_hi wT_lo wabs lines_ps lines_sb
            lines_dram bias_in anti_r antib_r flipT_ps flipN_ps biasT_r biasN_r vec_ready vec_in ident pool_init dve_init act_init
            x_in xT_ps xh_r xl_r conv_ps u_r relu_r v1_r h_r hb_r bns_r mv_r ve_r rstd_r nb_r xn_r
            xnT_ps xnh_r xnl_r q_ps k_ps v_ps qh_r ql_r kh_r kl_r va_r stack_in
            p1_ps mx_r mT_ps mneg_r mneg_in p2_ps sb_r exp_r pv_ps osb_r oT_ps rc_r on_r onT_ps onh_r onl_r
            wo_ps h2_r spilled bns2_r mv2_r ve2_r rstd2_r nb2_r xn2_r x2T_ps x2_r ax_r
            one_r xi_r xqh_r xq_r ag_r ared par sc_r ap_r ao_r oq_r oh_r ol_r""".split()
        names += [n + str(i) for n in "g_ps g_r u_ps raw_r raw_out raw_in gq_r sig_r sq_r p_r au_r uq_r g2_r o_r".split()
                  for i in range(2)]
        names += [n + str(i) for n in "dn_ps h_in y_r y_out".split() for i in range(4)]
        S = {n: sem(n) for n in names}

        def wait(eng, name, count):
            if isinstance(count, int) and count <= 0:
                return
            eng.wait_ge(S[name], count)

        def from_zero(eng, end, body):
            body(0)
            with eng.Fori(1, end) as i:
                body(i)

        def unregistered(eng, b):
            if not isinstance(b, int):
                eng.wait_ge(S["ident"], 2)

        def valued(eng, count):
            return count if isinstance(count, int) else eng.compute_val(count)

        pa = ctx.enter_context(ExitStack())

        def sba(name, shape, dt=F32):
            return sb(name, shape, dt, pa)

        identb = sba("identb", [128, 128], BF16)
        wcT = sba("wcT", [128, 2, CTX, C], F16)
        wqT, wkT, wvT, woT = (sba(n, [128, 2, KT, C], F16) for n in ("wqT", "wkT", "wvT", "woT"))
        bc = sba("bc", [128, 4, C])
        biasT = sba("biasT", [128, H, N])
        biasN = sba("biasN", [128, H, N], BF16)
        nhalf = sba("nhalf", [128, 2])

        pw = ExitStack()
        flipT = sb("flipT", [128, H, N], F32, pw)
        flipN = sb("flipN", [128, H, N], BF16, pw)
        anti = sb("anti", [128, TT], F32, pw)
        antib = sb("antib", [128, TT], BF16, pw)
        cw_n = sb("cw_n", [128, 2, CTX * D], F32, pw)
        sq_n = sb("sq_n", [128, 4, KT, C], F32, pw)
        ff_n = sb("ff_n", [128, 3, MT * C], F32, pw)
        ff_i = sb("ff_i", [128, 3, MT * C], I16, pw)
        ff_s = sb("ff_s", [128, 3, MT * C // BLOCK], F32, pw)
        ff_r = sb("ff_r", [128, 3, MT * C // BLOCK], F32, pw)
        wam = sb("wam", [128, 8], F32, pw)
        wal = sb("wal", [128, 8], F32, pw)
        hot_s = sb("hot_s", [BUCKETS, 2 * LINE], F32, pw)
        rel_s = sb("rel_s", [BUCKETS, H], F32, pw)
        lt_s = sb("lt_s", [H, LINE], F32, pw)
        ln_s = sb("ln_s", [H, LINE], BF16, pw)
        vec = sb("vec", [128, 2, C], F32, pw)

        sq_dram = [wq, wk, wv, wo]
        ff_dram = [wg.rearrange("(m p) i -> p m i", p=128), wu.rearrange("(m p) i -> p m i", p=128),
                   wd.rearrange("(m p) i -> p m i", p=128)]
        vec_dram = [cb, gamma, beta, bo, rmean, rvar]

        def bcast(v):
            return bass.AP(v.tensor, v.offset, [[0, 128], [1, C]])

        def ff_view(i):
            return ff_n[:, i, :].rearrange("p (m c) -> p m c", m=MT if i < 2 else 2)

        blocks = []
        for c in range(CTX):
            for o in range(2):
                blocks.append((cw_n[:, o, c * D:(c + 1) * D], wcT, c, o, W_CONV))
        blocks += [None, None]
        for i, w, col in ((0, wgT, W_GATE), (1, wuT, W_UP)):
            for k in range(KT):
                for m in range(MT):
                    blocks.append((ff_view(i)[:, m, k * 128:(k + 1) * 128], w, k, m, col))
        for k in range(MT):
            for m in range(2):
                blocks.append((ff_view(2)[:, m, k * 128:(k + 1) * 128], wdT, k, m, W_DOWN))
        banks = [blocks[i:i + 4] for i in range(0, len(blocks), 4)]

        def bank_dst(group, part):
            n = sum(g is not None for g in group)
            _, w, k, m, _ = group[0]
            cols = w.shape[3]
            flat = w[:, part, :, :].rearrange("p k c -> p (k c)")
            at = k * cols + m * 128
            return flat[:, at:at + n * 128], n

        def heads(km, i):
            cols = sq_n[:, i, km // 2, km % 2 * 128:km % 2 * 128 + 128]
            return cols.rearrange("p (s r) -> p r s", s=8) if i < 2 else cols

        def square(w, part, km, i):
            cols = w[:, part, km // 2, km % 2 * 128:km % 2 * 128 + 128]
            return cols.rearrange("p (r s) -> p r s", s=8) if i < 2 else cols

        with nc.Block() as block:
            @block.sync
            def _(sp):
                sp.dma_start(cw_n[:], cw.rearrange("(o p) k -> p o k", p=128)).then_inc(S["w_loaded"], 16)
                for i, w in enumerate(sq_dram):
                    sp.dma_start(sq_n[:, i], w.rearrange("(k p) c -> p k c", p=128)).then_inc(S["w_loaded"], 16)
                for i, w in enumerate(ff_dram):
                    sp.dma_start(ff_view(i), w).then_inc(S["w_loaded"], 16)
                sp.dma_start(hot_s[:], hot).then_inc(S["consts"], 16)
                sp.dma_start(rel_s[:], rel).then_inc(S["consts"], 16)
                for i, v in enumerate(vec_dram):
                    dst = bc[:, i, :] if i < 4 else vec[:, i - 4, :]
                    sp.dma_start(dst, bcast(v)).then_inc(S["vec_in"], 16)
                sp.wait_ge(S["lines_sb"], 4)
                sp.dma_start(line_t.ap(), lt_s[:]).then_inc(S["lines_dram"], 16)
                sp.dma_start(line_n.ap(), ln_s[:]).then_inc(S["lines_dram"], 16)
                sp.wait_ge(S["lines_dram"], 32)
                sp.dma_start(flipT[0:TT], bass.AP(line_t, 0, [[1, TT], [LINE, H], [1, N]])).then_inc(S["bias_in"], 16)
                sp.dma_start(flipN[0:TT], bass.AP(line_n, 0, [[1, TT], [LINE, H], [1, N]])).then_inc(S["bias_in"], 16)

            @block.gpsimd
            def _(pool):
                nc.gpsimd.memset(identf[:], 0.0).then_inc(S["ident"], 1)
                pool.wait_ge(S["ident"], 1)
                nc.gpsimd.affine_select(out=identf[:], in_=identf[:], compare_op=ALU.not_equal, fill=1.0, base=0,
                                        pattern=[[1, 128]], channel_multiplier=-1).then_inc(S["ident"], 1)
                nc.gpsimd.memset(anti[:], 0.0).then_inc(S["anti_r"], 1)
                pool.wait_ge(S["anti_r"], 1)
                nc.gpsimd.affine_select(out=anti[:], in_=anti[:], compare_op=ALU.not_equal, fill=1.0, base=1 - TT,
                                        pattern=[[1, TT]], channel_multiplier=1).then_inc(S["anti_r"], 1)
                pool.wait_ge(S["wamax"], 8)
                nc.gpsimd.partition_all_reduce(wal[:], wam[:], 128, ABSMAX).then_inc(S["wall"], 1)
                pool.wait_ge(S["vec_in"], 96)
                nc.gpsimd.tensor_scalar(vec[:, 1, :], vec[:, 1, :], EPS, 1.0, ALU.add, ALU.mult
                                        ).then_inc(S["vec_ready"], 1)
                pool.wait_ge(S["nhalf_set"], 1)
                pool.wait_ge(S["vec_ready"], 1)
                nc.gpsimd.tensor_tensor(vec[:, 1, :], vec[:, 1, :], nhalf[:, 0:1].broadcast_to([128, C]), ALU.pow
                                        ).then_inc(S["vec_ready"], 1)
                pool.wait_ge(S["vec_ready"], 2)
                nc.gpsimd.tensor_tensor(bc[:, 1, :], bc[:, 1, :], vec[:, 1, :], ALU.mult).then_inc(S["vec_ready"], 1)
                pool.wait_ge(S["vec_ready"], 3)
                nc.gpsimd.tensor_tensor(vec[:, 0, :], vec[:, 0, :], bc[:, 1, :], ALU.mult).then_inc(S["vec_ready"], 1)
                pool.wait_ge(S["vec_ready"], 4)
                nc.gpsimd.tensor_tensor(bc[:, 2, :], bc[:, 2, :], vec[:, 0, :], ALU.subtract
                                        ).then_inc(S["vec_ready"], 1)

            @block.vector
            def _(dve):
                nc.vector.memset(nhalf[:], -0.5).then_inc(S["nhalf_set"], 1)
                dve.wait_ge(S["w_loaded"], 128)
                nc.vector.tensor_reduce(wam[:, 0:1], cw_n[:].rearrange("p a b -> p (a b)"), X, ALU.max,
                                        apply_absolute_value=True).then_inc(S["wamax"], 1)
                for i in range(4):
                    nc.vector.tensor_reduce(wam[:, 1 + i:2 + i], sq_n[:, i].rearrange("p a b -> p (a b)"), X,
                                            ALU.max, apply_absolute_value=True).then_inc(S["wamax"], 1)
                for i in range(3):
                    nc.vector.tensor_reduce(ff_s[:, i], ff_n[:, i].rearrange("p (a b) -> p a b", b=BLOCK), X,
                                            ALU.max, apply_absolute_value=True).then_inc(S["wabs"], 1)
                for i in range(3):
                    dve.wait_ge(S["wabs"], i + 1)
                    nc.vector.tensor_reduce(wam[:, 5 + i:6 + i], ff_s[:, i], X, ALU.max).then_inc(S["wamax"], 1)
                dve.wait_ge(S["wamax"], 8)
                nc.vector.tensor_scalar(ff_s[:], ff_s[:], 1.0 / WQMAX, FLOOR, ALU.mult, ALU.max
                                        ).then_inc(S["wdq_s"], 1)
                dve.wait_ge(S["wdq_s"], 1)
                nc.vector.reciprocal(ff_r[:], ff_s[:]).then_inc(S["wdq_s"], 1)
                dve.wait_ge(S["wdq_s"], 2)
                for i in range(3):
                    v = ff_n[:, i].rearrange("p (a b) -> p a b", b=BLOCK)
                    vi = ff_i[:, i].rearrange("p (a b) -> p a b", b=BLOCK)
                    nc.vector.tensor_tensor(vi, v, ff_r[:, i].unsqueeze(2).broadcast_to([128, 48, BLOCK]),
                                            ALU.mult).then_inc(S["wdq_i"], 1)
                    dve.wait_ge(S["wdq_i"], i + 1)
                    nc.vector.tensor_tensor(v, vi, ff_s[:, i].unsqueeze(2).broadcast_to([128, 48, BLOCK]),
                                            ALU.mult).then_inc(S["wdq_w"], 1)
                dve.wait_ge(S["wall"], 1)
                nc.vector.tensor_scalar(wal[:], wal[:], 1e-30, None, ALU.max).then_inc(S["wpow"], 1)
                dve.wait_ge(S["wpow"], 1)
                nc.vector.tensor_scalar(wal[:].bitcast(I32), wal[:].bitcast(I32), 0x7F800000, None,
                                        ALU.bitwise_and).then_inc(S["wpow"], 1)
                dve.wait_ge(S["wpow"], 2)
                nc.vector.tensor_scalar(wscale[:], wal[:], 1.0 / 64, None, ALU.mult).then_inc(S["wpow"], 1)
                dve.wait_ge(S["wpow"], 3)
                nc.vector.reciprocal(winv[:], wscale[:]).then_inc(S["winv_s"], 1)
                dve.wait_ge(S["winv_s"], 1)
                dve.wait_ge(S["ident"], 2)
                nc.vector.tensor_copy(identb[:], identf[:]).then_inc(S["dve_init"], 1)
                dve.wait_ge(S["anti_r"], 2)
                nc.vector.tensor_copy(antib[:], anti[:]).then_inc(S["antib_r"], 1)
                for i, w in enumerate((wqT, wkT, wvT, woT)):
                    dve.wait_ge(S["wT_hi"], 4 * i + 4)
                    for km in range(2 * KT):
                        nc.vector.scalar_tensor_tensor(square(w, 1, km, i), heads(km, i), winv[:, 1 + i:2 + i],
                                                       square(w, 0, km, i), ALU.mult, ALU.subtract
                                                       ).then_inc(S["wT_lo"], 1)
                dve.wait_ge(S["lines_ps"], 2)
                nc.vector.tensor_copy(lt_s[:, TT - 1:LINE], ps[0:H, 0, TT - 1:LINE]).then_inc(S["lines_sb"], 1)
                nc.vector.memset(lt_s[:, 0:TT - 1], MASKED).then_inc(S["lines_sb"], 1)
                nc.vector.tensor_copy(ln_s[:, 0:N], ps[0:H, 1, 0:N]).then_inc(S["lines_sb"], 1)
                nc.vector.memset(ln_s[:, N:LINE], MASKED).then_inc(S["lines_sb"], 1)
                for j, group in enumerate(banks):
                    hi, n = bank_dst(group, 0)
                    lo, _ = bank_dst(group, 1)
                    col = group[0][4]
                    dve.wait_ge(S["wT_hi"], 17 + j)
                    nc.vector.scalar_tensor_tensor(lo, ps[:, 2 + j % 4, 0:128 * n], winv[:, col:col + 1], hi,
                                                   ALU.mult, ALU.subtract).then_inc(S["wT_lo"], 1)
                for i in range(H // 2):
                    dve.wait_ge(S["flipN_ps"], i + 1)
                    nc.vector.tensor_copy(biasN[0:TT, 2 * i:2 * i + 2].rearrange("p h n -> p (h n)"),
                                          ps[0:TT, i % 2, 0:2 * N]).then_inc(S["biasN_r"], 1)

            @block.scalar
            def _(act):
                act.wait_ge(S["winv_s"], 1)
                for i, w in enumerate((wqT, wkT, wvT, woT)):
                    for km in range(2 * KT):
                        nc.scalar.activation(square(w, 0, km, i), heads(km, i), ACT.Copy,
                                             scale=winv[:, 1 + i:2 + i]).then_inc(S["wT_hi"], 1)
                for j, group in enumerate(banks):
                    hi, n = bank_dst(group, 0)
                    col = group[0][4]
                    act.wait_ge(S["wT_ps"], j + 1)
                    nc.scalar.activation(hi, ps[:, 2 + j % 4, 0:128 * n], ACT.Copy, scale=winv[:, col:col + 1]
                                         ).then_inc(S["wT_hi"], 1)
                for i in range(H // 2):
                    act.wait_ge(S["flipT_ps"], i + 1)
                    nc.scalar.activation(biasT[0:TT, 2 * i:2 * i + 2].rearrange("p h n -> p (h n)"),
                                         ps[0:TT, 6 + i % 2, 0:2 * N], ACT.Copy).then_inc(S["biasT_r"], 1)

            @block.tensor
            def _(pe):
                pe.wait_ge(S["consts"], 32)
                pe.wait_ge(S["ident"], 2)
                for i in range(2):
                    nc.tensor.matmul(ps[0:H, i, 0:LINE], rel_s[:], hot_s[:, i * LINE:(i + 1) * LINE],
                                     start=True, stop=True).then_inc(S["lines_ps"], 1)
                pe.wait_ge(S["wdq_w"], 3)
                pe.wait_ge(S["w_loaded"], 128)
                for j, group in enumerate(banks):
                    if j >= 4:
                        pe.wait_ge(S["wT_lo"], 16 + j - 3)
                    for n, g in enumerate(group):
                        if g is not None:
                            last = nc.tensor.transpose(ps[:, 2 + j % 4, n * 128:(n + 1) * 128], g[0], identf[:])
                    last.then_inc(S["wT_ps"], 1)
                pe.wait_ge(S["bias_in"], 32)
                pe.wait_ge(S["antib_r"], 1)
                pe.wait_ge(S["lines_sb"], 4)
                for i in range(H // 2):
                    pair = slice(2 * i, 2 * i + 2)
                    if i >= 2:
                        pe.wait_ge(S["biasT_r"], i - 1)
                        pe.wait_ge(S["biasN_r"], i - 1)
                    nc.tensor.matmul(ps[0:TT, 6 + i % 2, 0:2 * N], anti[0:TT], flipT[0:TT, pair], start=True, stop=True
                                     ).then_inc(S["flipT_ps"], 1)
                    nc.tensor.matmul(ps[0:TT, i % 2, 0:2 * N], antib[0:TT], flipN[0:TT, pair], start=True, stop=True
                                     ).then_inc(S["flipN_ps"], 1)
        pw.close()

        xin = sba("xin", [128, 2, D])
        xh, xl = sba("xh", [128, T], F16), sba("xl", [128, T], F16)
        u = sba("u", [128, 2, C])
        r1 = sba("r1", [128, 2, C])
        v1 = sba("v1", [128, 2, C])
        h = sba("h", [128, 2, C])
        hall = sba("hall", [128, B, 2 * C])
        bns, bns2 = sba("bns", [128, 2, 6]), sba("bns2", [128, 2, 6])
        mv, mv2 = sba("mv", [128, 2, 2]), sba("mv2", [128, 2, 2])
        ve, ve2 = sba("ve", [128, 2]), sba("ve2", [128, 2])
        rstd, rstd2 = sba("rstd", [128, 2]), sba("rstd2", [128, 2])
        nb, nb2 = sba("nb", [128, 2]), sba("nb2", [128, 2])
        xn, xn2 = sba("xn", [128, 2, C]), sba("xn2", [128, 2, C])
        xnh, xnl = sba("xnh", [128, KT, N], F16), sba("xnl", [128, KT, N], F16)
        qh, ql, kh, kl = (sba(n, [128, 2, NP], F16) for n in ("qh", "ql", "kh", "kl"))
        qS = [sba(f"qS{i}", [128, 8, NP], F16) for i in range(2)]
        kS = [sba(f"kS{i}", [128, 8, NP], F16) for i in range(2)]
        va = [sba(f"va{i}", [128, 2, H, 32]) for i in range(2)]
        mx = sba("mx", [128, 2, H])
        mneg = sba("mneg", [H, NP], F16)
        sbr = sba("sbr", [128, 4, 2 * N])
        pt = sba("pt", [128, 2, 3, 2 * N])
        osb = sba("osb", [128, G, N])
        rc = sba("rc", [128, 2, H])
        on = sba("on", [128, 2, C])
        onh, onl = sba("onh", [128, KT, N], F16), sba("onl", [128, KT, N], F16)

        OB, MB = 4, 6

        ORDER = [("xnT", 1), ("OT0", -1), ("OT1", -1), ("q", 1), ("k", 1), ("v", 1), ("P2", 0, 0), ("onT", -1),
                 ("P2", 0, 1), ("PV", 0, 0), ("xT", 2), ("wo", -1), ("P2", 0, 2), ("PV", 0, 1), ("P1", 1, 0),
                 ("conv", 2), ("P2", 0, 3), ("PV", 0, 2), ("P1", 1, 1), ("x2T", -1), ("P1", 1, 2), ("P1", 1, 3),
                 ("PV", 0, 3), ("mT", 1)]
        MISC = [("xnT", "xnl_r", 1, 1, 1), ("OT0", "on_r", 2, 1, -1), ("OT1", "on_r", 2, 2, -1),
                ("q", "ql_r", 1, 1, 1), ("k", "kl_r", 1, 1, 1), ("v", "va_r", 1, 1, 1), ("onT", "onl_r", 1, 1, -1),
                ("xT", "xl_r", 1, 1, 2), ("wo", "h2_r", 1, 1, -1), ("conv", "u_r", 1, 1, 2),
                ("x2T", "x2_r", 1, 1, -1), ("mT", "mneg_r", 1, 1, 1)]
        misc_at = {m[0]: i for i, m in enumerate(MISC)}
        misc_bank = {m[0]: MB + i % 2 for i, m in enumerate(MISC)}
        piece_at = {}
        PIECES = []
        for st in ORDER:
            if st[0] in ("P1", "P2"):
                piece_at[(st[0], st[2])] = len(PIECES)
                PIECES += [(st[0], st[1], 3 * st[2] + j) for j in range(3)]

        def runs(b, off):
            return not isinstance(b, int) or 0 <= b + off < B

        def misc_free(pe, stage, b):
            i = misc_at[stage] - 2
            for back in range(4):
                while i >= 0:
                    _, name, per, n, off = MISC[i]
                    if runs(b - back if isinstance(b, int) else b, off):
                        return wait(pe, name, per * (b - back + off) + n)
                    i -= 2
                i += len(MISC)

        def score_free(pe, idx, b):
            i = idx - 4
            for back in range(4):
                while i >= 0:
                    kind, off, n = PIECES[i]
                    if runs(b - back if isinstance(b, int) else b, off):
                        return wait(pe, "sb_r" if kind == "P2" else "mx_r", 12 * (b - back + off) + n + 1)
                    i -= 4
                i += len(PIECES)

        def three(out_ap, pairs):
            todo = []
            for (ah, al), (bh, bl) in pairs:
                todo += [(ah, bh), (al, bh), (ah, bl)]
            for i, (a, w) in enumerate(todo):
                last = nc.tensor.matmul(out_ap, a, w, start=(i == 0), stop=(i == len(todo) - 1))
            return last

        def pe_step(pe, b, par):
            odd = 1 - par
            for st in ORDER:
                name, off = st[0], st[1]
                if not runs(b, off):
                    continue
                c = b + off
                if name in misc_at:
                    bank = ps[:, misc_bank[name], :]
                if name == "xT":
                    wait(pe, "x_in", 16 * (c + 1))
                    misc_free(pe, name, b)
                    nc.tensor.transpose(bank[:, 0:128], xin[:, 0], identf[:])
                    nc.tensor.transpose(bank[:, 128:256], xin[:, 1], identf[:]).then_inc(S["xT_ps"], 1)
                elif name == "conv":
                    wait(pe, "xh_r", c + 1)
                    wait(pe, "xl_r", c + 1)
                    misc_free(pe, name, b)
                    for t in range(2):
                        last = three(bank[0:TT, t * C:(t + 1) * C],
                                     [((xh[:, t * TT + i:t * TT + i + TT], xl[:, t * TT + i:t * TT + i + TT]),
                                       (wcT[:, 0, i, :], wcT[:, 1, i, :])) for i in range(CTX)])
                    last.then_inc(S["conv_ps"], 1)
                elif name == "xnT":
                    wait(pe, "xn_r", 2 * (c + 1))
                    misc_free(pe, name, b)
                    for k in range(KT):
                        for t in range(2):
                            last = nc.tensor.transpose(bank[:, k * N + t * TT:k * N + (t + 1) * TT],
                                                       xn[0:TT, t, k * 128:(k + 1) * 128], identf[0:TT, 0:TT])
                    last.then_inc(S["xnT_ps"], 1)
                elif name in ("q", "k"):
                    w = wqT if name == "q" else wkT
                    wait(pe, "xnh_r", c + 1)
                    wait(pe, "xnl_r", c + 1)
                    misc_free(pe, name, b)
                    for m in range(2):
                        cols = slice(m * 128, (m + 1) * 128)
                        todo = [(w[:, 0, k, cols], xnh[:, k]) for k in range(KT)]
                        todo += [(w[:, 0, k, cols], xnl[:, k]) for k in range(KT)]
                        todo += [(w[:, 1, k, cols], xnh[:, k]) for k in range(KT)]
                        for i, (a, v) in enumerate(todo):
                            last = nc.tensor.matmul(bank[:, m * N:(m + 1) * N], a, v, start=(i == 0), stop=(i == 5))
                    last.then_inc(S[name + "_ps"], 1)
                elif name == "v":
                    misc_free(pe, name, b)
                    for t in range(2):
                        rows = slice(t * TT, (t + 1) * TT)
                        last = three(bank[0:TT, t * C:(t + 1) * C],
                                     [((xnh[:, k, rows], xnl[:, k, rows]), (wvT[:, 0, k], wvT[:, 1, k]))
                                      for k in range(KT)])
                    last.then_inc(S["v_ps"], 1)
                elif name == "P1":
                    g = st[2]
                    if g == 0:
                        wait(pe, "stack_in", 192 * (c + 1))
                    q, k = qS[odd], kS[odd]
                    rows = slice(64 * (g // 2), 64 * (g // 2) + 48)
                    for j in range(3):
                        idx = piece_at[("P1", g)] + j
                        score_free(pe, idx, b)
                        heads = range(4 * g, 4 * g + 4) if j == 2 else range(4 * g + 2 * j, 4 * g + 2 * j + 2)
                        w = TT if j == 2 else N
                        dst = ps[0:TT, idx % 4, 0:2 * N]
                        nc.tensor.matmul(dst, identb[0:TT, 0:TT], biasN[0:TT, heads[0]:heads[-1] + 1, N - w:N],
                                         start=True, stop=True)
                        for n, hd in enumerate(heads):
                            qt = slice(0, TT) if j == 2 else slice(TT, N)
                            last = nc.tensor.matmul(dst[:, n * w:(n + 1) * w], q[rows, hd % 8, qt],
                                                    k[rows, hd % 8, 0:w], start=False, stop=True,
                                                    skip_group_check=True)
                        last.then_inc(S["p1_ps"], 1)
                elif name == "mT":
                    wait(pe, "mx_r", 12 * (c + 1))
                    misc_free(pe, name, b)
                    for t in range(2):
                        last = nc.tensor.matmul(bank[0:H, t * TT:(t + 1) * TT], mx[0:TT, t, :], identf[0:TT, 0:TT],
                                                start=True, stop=True)
                    last.then_inc(S["mT_ps"], 1)
                elif name == "P2":
                    g = st[2]
                    if g == 0:
                        wait(pe, "mneg_in", 32 * (c + 1))
                    q, k = qS[par], kS[par]
                    rows = slice(64 * (g // 2), 64 * (g // 2) + 49)
                    for j in range(3):
                        idx = piece_at[("P2", g)] + j
                        score_free(pe, idx, b)
                        heads = range(4 * g, 4 * g + 4) if j == 2 else range(4 * g + 2 * j, 4 * g + 2 * j + 2)
                        w = TT if j == 2 else N
                        for n, hd in enumerate(heads):
                            kt = slice(TT, N) if j == 2 else slice(0, TT)
                            last = nc.tensor.matmul(ps[0:TT, idx % 4, n * w:(n + 1) * w], k[rows, hd % 8, kt],
                                                    q[rows, hd % 8, N - w:N], start=True, stop=True)
                        last.then_inc(S["p2_ps"], 1)
                elif name == "PV":
                    g = st[2]
                    wait(pe, "exp_r", 12 * c + 3 * (g + 1))
                    wait(pe, "va_r", c + 1)
                    wait(pe, "osb_r", 4 * c + g - 1)
                    p = pt[0:TT, g % 2]
                    for i in range(4):
                        nc.tensor.matmul(ps[32 * i:32 * i + 32, OB + g % 2, 0:N], va[par][0:TT, 0, 4 * g + i, :],
                                         p[:, i // 2, (i % 2) * N:(i % 2) * N + N], start=True, stop=True,
                                         skip_group_check=True)
                    for i in range(4):
                        last = nc.tensor.matmul(ps[32 * i:32 * i + 32, OB + g % 2, TT:N],
                                                va[par][0:TT, 1, 4 * g + i, :], p[:, 2, i * TT:(i + 1) * TT],
                                                start=False, stop=True, skip_group_check=True)
                    last.then_inc(S["pv_ps"], 1)
                elif name in ("OT0", "OT1"):
                    t = int(name[2])
                    wait(pe, "osb_r", 4 * (c + 1))
                    misc_free(pe, name, b)
                    for g in range(G):
                        last = nc.tensor.transpose(bank[0:TT, g * 128:(g + 1) * 128],
                                                   osb[:, g, t * TT:(t + 1) * TT], identf[:])
                    last.then_inc(S["oT_ps"], 1)
                elif name == "onT":
                    wait(pe, "on_r", 2 * (c + 1))
                    misc_free(pe, name, b)
                    for k in range(KT):
                        for t in range(2):
                            last = nc.tensor.transpose(bank[:, k * N + t * TT:k * N + (t + 1) * TT],
                                                       on[0:TT, t, k * 128:(k + 1) * 128], identf[0:TT, 0:TT])
                    last.then_inc(S["onT_ps"], 1)
                elif name == "wo":
                    wait(pe, "onh_r", c + 1)
                    wait(pe, "onl_r", c + 1)
                    misc_free(pe, name, b)
                    for t in range(2):
                        rows = slice(t * TT, (t + 1) * TT)
                        last = three(bank[0:TT, t * C:(t + 1) * C],
                                     [((onh[:, k, rows], onl[:, k, rows]), (woT[:, 0, k], woT[:, 1, k]))
                                      for k in range(KT)])
                    last.then_inc(S["wo_ps"], 1)
                elif name == "x2T":
                    wait(pe, "xn2_r", 2 * (c + 1))
                    misc_free(pe, name, b)
                    for k in range(KT):
                        for t in range(2):
                            last = nc.tensor.transpose(bank[:, k * N + t * TT:k * N + (t + 1) * TT],
                                                       xn2[0:TT, t, k * 128:(k + 1) * 128], identf[0:TT, 0:TT])
                    last.then_inc(S["x2T_ps"], 1)

        def split(stage, scale=None):
            return ps[:, misc_bank[stage], :]

        def dve_bias(dve, c, b, g):
            for j in range(3):
                n = 3 * g + j
                bank = ps[0:TT, (piece_at[("P2", g)] + j) % 4, 0:2 * N]
                wait(dve, "p2_ps", 12 * c + n + 1)
                wait(dve, "exp_r", 12 * c + n - 3)
                hs, w = (slice(4 * g, 4 * g + 4), TT) if j == 2 else (slice(4 * g + 2 * j, 4 * g + 2 * j + 2), N)
                nc.vector.tensor_tensor(sbr[0:TT, n % 4].rearrange("p (h w) -> p h w", w=w),
                                        bank.rearrange("p (h w) -> p h w", w=w), biasT[0:TT, hs, 0:w], ALU.add
                                        ).then_inc(S["sb_r"], 1)

        def dve_max(dve, c, b, g):
            if g == 0:
                wait(dve, "mT_ps", c)
            for j in range(3):
                n = 3 * g + j
                bank = ps[0:TT, (piece_at[("P1", g)] + j) % 4, 0:2 * N]
                wait(dve, "p1_ps", 12 * c + n + 1)
                hs, w = (slice(4 * g, 4 * g + 4), TT) if j == 2 else (slice(4 * g + 2 * j, 4 * g + 2 * j + 2), N)
                nc.vector.tensor_reduce(mx[0:TT, 0 if j == 2 else 1, hs], bank.rearrange("p (h w) -> p h w", w=w), X,
                                        ALU.max).then_inc(S["mx_r"], 1)

        def dve_stats(dve, c, src, st, m, v, sfx, ready):
            unregistered(dve, c)
            wait(dve, *ready)
            wait(dve, "xn" + sfx[:-2] + "_r" if sfx != "_r" else "xn_r", 2 * c)
            for t in range(2):
                nc.vector.bn_stats(st[0:TT, t], src(t)).then_inc(S["bns" + sfx], 1)
            for t in range(2):
                count = valued(dve, 2 * c + t + 1)
                unregistered(dve, c)
                wait(dve, "bns" + sfx, count)
                nc.vector.bn_aggr(m[0:TT, t], st[0:TT, t]).then_inc(S["mv" + sfx], 1)
            wait(dve, "mv" + sfx, 2 * (c + 1))
            nc.vector.tensor_scalar(v[0:TT], m[0:TT, :, 1], EPS, None, ALU.add).then_inc(S["ve" + sfx], 1)

        def dve_nb(dve, c, m, r, o, sfx):
            wait(dve, "rstd" + sfx, c + 1)
            nc.vector.scalar_tensor_tensor(o[0:TT], m[0:TT, :, 0], -1.0, r[0:TT], ALU.mult, ALU.mult
                                           ).then_inc(S["nb" + sfx], 1)

        def dve_step(dve, b, par):
            f1, f2, at, back = runs(b, 2), runs(b, 1), runs(b, 0), runs(b, -1)
            if f2:
                c = b + 1
                wait(dve, "xnh_r", c + 1)
                wait(dve, "v_ps", c)
                nc.vector.tensor_tensor(xnl[:].rearrange("p k n -> p (k n)"), split("xnT")[:, 0:2 * N],
                                        xnh[:].rearrange("p k n -> p (k n)"), ALU.subtract).then_inc(S["xnl_r"], 1)
            if back:
                c = b - 1
                for t in range(2):
                    src = split(f"OT{t}")[0:TT].rearrange("p (h e) -> p h e", e=32)
                    wait(dve, "oT_ps", 2 * c + t + 1)
                    wait(dve, "onT_ps", c)
                    nc.vector.reciprocal(rc[0:TT, t], src[:, :, DH]).then_inc(S["rc_r"], 1)
                    wait(dve, "rc_r", 2 * c + t + 1)
                    nc.vector.tensor_tensor(on[0:TT, t].rearrange("p (h e) -> p h e", e=DH), src[:, :, 0:DH],
                                            rc[0:TT, t].unsqueeze(2).broadcast_to([TT, H, DH]), ALU.mult
                                            ).then_inc(S["on_r"], 1)
            if f2:
                c = b + 1
                for nm, hi, lo, col in (("q", qh, ql, 1), ("k", kh, kl, 2)):
                    wait(dve, nm + "h_r", c + 1)
                    wait(dve, "stack_in", 192 * c)
                    nc.vector.scalar_tensor_tensor(
                        lo[:, :, 0:N], split(nm)[:, 0:2 * N].rearrange("p (m n) -> p m n", m=2), qks[:, col - 1:col],
                        hi[:, :, 0:N], ALU.mult, ALU.subtract).then_inc(S[nm + "l_r"], 1)
            if at:
                dve_bias(dve, b, b, 0)
            if back:
                c = b - 1
                wait(dve, "onh_r", c + 1)
                wait(dve, "wo_ps", c)
                nc.vector.tensor_tensor(onl[:].rearrange("p k n -> p (k n)"), split("onT")[:, 0:2 * N],
                                        onh[:].rearrange("p k n -> p (k n)"), ALU.subtract).then_inc(S["onl_r"], 1)
            if at:
                dve_bias(dve, b, b, 1)
            if f1:
                c = b + 2
                wait(dve, "xh_r", c + 1)
                wait(dve, "conv_ps", c)
                nc.vector.tensor_tensor(xl[:], split("xT")[:, 0:T], xh[:], ALU.subtract).then_inc(S["xl_r"], 1)
            if back:
                c = b - 1
                wait(dve, "wo_ps", c + 1)
                wait(dve, "hb_r", c + 1)
                hc = hall[0:TT, c, :] if isinstance(c, int) else hall[0:TT, bass.ds(c, 1), :].rearrange("p a n -> p (a n)")
                nc.vector.scalar_tensor_tensor(hc, split("wo")[0:TT], wscale[0:TT, W_O:W_O + 1], hc, ALU.mult,
                                               ALU.add).then_inc(S["h2_r"], 1)
                dve_stats(dve, c, lambda t: hc[:, t * C:(t + 1) * C], bns2, mv2, ve2, "2_r", ("h2_r", c + 1))
            if at:
                dve_bias(dve, b, b, 2)
            if back:
                dve_nb(dve, b - 1, mv2, rstd2, nb2, "2_r")
            if f2:
                dve_max(dve, b + 1, b, 0)
            if f1:
                c = b + 2
                wait(dve, "conv_ps", c + 1)
                wait(dve, "relu_r", c)
                nc.vector.scalar_tensor_tensor(
                    u[0:TT], split("conv")[0:TT].rearrange("p (t c) -> p t c", t=2), wscale[0:TT, 0:1],
                    bc[0:TT, 0:1, :].broadcast_to([TT, 2, C]), ALU.mult, ALU.add).then_inc(S["u_r"], 1)
            if at:
                dve_bias(dve, b, b, 3)
            if f2:
                dve_max(dve, b + 1, b, 1)
            if f1:
                dve_stats(dve, b + 2, lambda t: h[0:TT, t], bns, mv, ve, "_r", ("h_r", b + 3))
            if f2:
                dve_max(dve, b + 1, b, 2)
            if back:
                c = b - 1
                wait(dve, "x2_r", c + 1)
                src = x2t[:, c] if isinstance(c, int) else x2t[:, bass.ds(c, 1)].rearrange("p a k n -> p (a k) n")
                dst = amax_x[:, c:c + 1] if isinstance(c, int) else amax_x[:, bass.ds(c, 1)]
                nc.vector.tensor_reduce(dst, src, mybir.AxisListType.XY, ALU.max, apply_absolute_value=True
                                        ).then_inc(S["ax_r"], 1)
            if f1:
                dve_nb(dve, b + 2, mv, rstd, nb, "_r")
            if f2:
                dve_max(dve, b + 1, b, 3)
                c = b + 1
                wait(dve, "mT_ps", c + 1)
                wait(dve, "mneg_in", 32 * c)
                nc.vector.tensor_scalar(mneg[:, 0:N], split("mT")[0:H, 0:N], -1.0, None, ALU.mult
                                        ).then_inc(S["mneg_r"], 1)

        def act_exp(act, b, g):
            for j in range(3):
                n = 3 * g + j
                wait(act, "sb_r", 12 * b + n + 1)
                wait(act, "pv_ps", 4 * b + g - 1)
                nc.scalar.activation(pt[0:TT, g % 2, j], sbr[0:TT, n % 4], ACT.Exp).then_inc(S["exp_r"], 1)

        def act_o(act, b, g):
            wait(act, "pv_ps", 4 * b + g + 1)
            if g == 0:
                wait(act, "oT_ps", 2 * b)
            nc.scalar.activation(osb[:, g], ps[:, OB + g % 2, 0:N], ACT.Copy).then_inc(S["osb_r"], 1)

        def act_norm(act, c, src, dst, r, o, sfx, read):
            wait(act, "nb" + sfx, c + 1)
            wait(act, read, c)
            for t in range(2):
                nc.scalar.activation(dst[0:TT, t], src(t), ACT.Identity, bias=o[0:TT, t:t + 1],
                                     scale=r[0:TT, t:t + 1]).then_inc(S["xn" + sfx], 1)

        def act_step(act, b, par):
            odd = 1 - par
            f1, f2, at, back = runs(b, 2), runs(b, 1), runs(b, 0), runs(b, -1)
            if f2:
                c = b + 1
                wait(act, "xnT_ps", c + 1)
                wait(act, "v_ps", c)
                nc.scalar.activation(xnh[:].rearrange("p k n -> p (k n)"), split("xnT")[:, 0:2 * N], ACT.Copy
                                     ).then_inc(S["xnh_r"], 1)
                for nm, hi, col in (("q", qh, 0), ("k", kh, 1)):
                    wait(act, nm + "_ps", c + 1)
                    wait(act, "stack_in", 192 * c)
                    nc.scalar.activation(hi[:, :, 0:N], split(nm)[:, 0:2 * N].rearrange("p (m n) -> p m n", m=2),
                                         ACT.Copy, scale=qks[:, col:col + 1]).then_inc(S[nm + "h_r"], 1)
                wait(act, "v_ps", c + 1)
                wait(act, "pv_ps", 4 * (c - 1))
                nc.scalar.activation(va[odd][0:TT, :, :, 0:DH],
                                     split("v")[0:TT].rearrange("p (t h e) -> p t h e", t=2, h=H), ACT.Copy,
                                     scale=wscale[0:TT, W_V:W_V + 1]).then_inc(S["va_r"], 1)
            if at:
                act_exp(act, b, 0)
            if back:
                c = b - 1
                wait(act, "onT_ps", c + 1)
                wait(act, "wo_ps", c)
                nc.scalar.activation(onh[:].rearrange("p k n -> p (k n)"), split("onT")[:, 0:2 * N], ACT.Copy
                                     ).then_inc(S["onh_r"], 1)
            if at:
                act_exp(act, b, 1)
                act_o(act, b, 0)
            if f1:
                c = b + 2
                wait(act, "xT_ps", c + 1)
                wait(act, "conv_ps", c)
                nc.scalar.activation(xh[:], split("xT")[:, 0:T], ACT.Copy).then_inc(S["xh_r"], 1)
            if at:
                act_exp(act, b, 2)
                act_o(act, b, 1)
            if back:
                c = b - 1
                hc = hall[0:TT, c, :] if isinstance(c, int) else hall[0:TT, bass.ds(c, 1), :].rearrange("p a n -> p (a n)")
                act_norm(act, c, lambda t: hc[:, t * C:(t + 1) * C], xn2, rstd2, nb2, "2_r", "x2T_ps")
            if f1:
                c = b + 2
                wait(act, "u_r", c + 1)
                wait(act, "v1_r", c)
                nc.scalar.activation(r1[0:TT], u[0:TT], ACT.Relu).then_inc(S["relu_r"], 1)
            if at:
                act_exp(act, b, 3)
                act_o(act, b, 2)
            if back:
                c = b - 1
                wait(act, "x2T_ps", c + 1)
                dst = x2t[:, c] if isinstance(c, int) else x2t[:, bass.ds(c, 1)].rearrange("p a k n -> p (a k) n")
                nc.scalar.activation(dst, split("x2T")[:, 0:2 * N].rearrange("p (k n) -> p k n", k=KT), ACT.Copy
                                     ).then_inc(S["x2_r"], 1)
            if f1:
                act_norm(act, b + 2, lambda t: h[0:TT, t], xn, rstd, nb, "_r", "xnT_ps")
            if at:
                act_o(act, b, 3)

        def pool_step(pool, b, par):
            if runs(b, -1):
                c = b - 1
                wait(pool, "ve2_r", c + 1)
                wait(pool, "xn2_r", 2 * c)
                nc.gpsimd.tensor_tensor(rstd2[0:TT], ve2[0:TT], nhalf[0:TT], ALU.pow).then_inc(S["rstd2_r"], 1)
            if runs(b, 2):
                c = b + 2
                wait(pool, "relu_r", c + 1)
                wait(pool, "h_r", c)
                nc.gpsimd.tensor_tensor(v1[0:TT], r1[0:TT], bc[0:TT, 1:2, :].broadcast_to([TT, 2, C]), ALU.mult
                                        ).then_inc(S["v1_r"], 1)
                wait(pool, "v1_r", c + 1)
                wait(pool, "xn_r", 2 * c)
                wait(pool, "hb_r", c)
                nc.gpsimd.tensor_tensor(h[0:TT], v1[0:TT], bc[0:TT, 2:3, :].broadcast_to([TT, 2, C]), ALU.add
                                        ).then_inc(S["h_r"], 1)
                wait(pool, "h_r", c + 1)
                hc = (hall[0:TT, c, :] if isinstance(c, int) else
                      hall[0:TT, bass.ds(c, 1), :].rearrange("p a n -> p (a n)")).rearrange("p (t c) -> p t c", t=2)
                nc.gpsimd.tensor_tensor(hc, h[0:TT], bc[0:TT, 3:4, :].broadcast_to([TT, 2, C]), ALU.add
                                        ).then_inc(S["hb_r"], 1)
                wait(pool, "ve_r", c + 1)
                nc.gpsimd.tensor_tensor(rstd[0:TT], ve[0:TT], nhalf[0:TT], ALU.pow).then_inc(S["rstd_r"], 1)

        def load_x(sp, c):
            unregistered(sp, c)
            wait(sp, "xT_ps", c)
            src = x[c] if isinstance(c, int) else x[bass.ds(c, 1)].rearrange("a t d -> (a t) d")
            sp.dma_start(xin[:], src.rearrange("(a p) d -> p a d", p=128)).then_inc(S["x_in"], 16)

        def sp_step(sp, b, par):
            odd = 1 - par
            if runs(b, 1):
                c = b + 1
                for nm, dst, parts in (("q", qS[odd], (qh, ql, qh)), ("k", kS[odd], (kh, kh, kl))):
                    done = valued(sp, 12 * (c - 1))
                    wait(sp, nm + "h_r", c + 1)
                    wait(sp, nm + "l_r", c + 1)
                    wait(sp, "p2_ps", done)
                    for i, src in enumerate(parts):
                        for m in range(2):
                            row = 64 * m + 16 * i
                            sp.dma_start(dst[row:row + DH], src[:, m, :]).then_inc(S["stack_in"], 16)
            if runs(b, 3):
                load_x(sp, b + 3)
            if runs(b, -1):
                c = b - 1
                unregistered(sp, c)
                wait(sp, "h2_r", c + 1)
                if isinstance(c, int):
                    sp.dma_start(res.ap()[c], hall[0:TT, c, :]).then_inc(S["spilled"], 16)
                else:
                    sp.dma_start(res.ap()[bass.ds(c, 1)].rearrange("a p n -> (a p) n"),
                                 hall[0:TT, bass.ds(c, 1), :].rearrange("p a n -> p (a n)")).then_inc(S["spilled"], 16)
            if runs(b, 1):
                c = b + 1
                wait(sp, "mneg_r", c + 1)
                for m in range(2):
                    sp.dma_start(qS[odd][64 * m + 48:64 * m + 49], mneg[8 * m:8 * m + 8, :]).then_inc(S["mneg_in"], 16)

        INIT = 3 + 4 + 2 + 4 + 1
        qks = sba("qks", [128, 2])

        with nc.Block() as block:
            @block.tensor
            def _(pe):
                pe.wait_ge(S["dve_init"], INIT)
                for b in (-2, -1, 0, 1):
                    pe_step(pe, b, b % 2)
                with pe.Fori(1, 7) as k:
                    for par in range(2):
                        pe_step(pe, 2 * k + par, par)
                for b in (14, 15, 16):
                    pe_step(pe, b, b % 2)

            @block.vector
            def _(dve):
                nc.vector.tensor_scalar(qks[:, 0:1], wscale[:, W_Q:W_Q + 1], DH ** -0.5, None, ALU.mult
                                        ).then_inc(S["dve_init"], 1)
                nc.vector.tensor_copy(qks[:, 1:2], wscale[:, W_K:W_K + 1]).then_inc(S["dve_init"], 1)
                for t in kS:
                    for m in range(2):
                        nc.vector.memset(t[64 * m + 32:64 * m + 64], 1.0).then_inc(S["dve_init"], 1)
                for t in va:
                    nc.vector.memset(t[:], 1.0).then_inc(S["dve_init"], 1)
                for t in (qh, ql, kh, kl):
                    nc.vector.memset(t[:, :, N:NP], 0.0).then_inc(S["dve_init"], 1)
                nc.vector.memset(mneg[:, N:NP], 0.0).then_inc(S["dve_init"], 1)
                dve.wait_ge(S["dve_init"], INIT)
                for b in (-2, -1, 0, 1):
                    dve_step(dve, b, b % 2)
                with dve.Fori(1, 7) as k:
                    for par in range(2):
                        dve_step(dve, 2 * k + par, par)
                for b in (14, 15, 16):
                    dve_step(dve, b, b % 2)

            @block.scalar
            def _(act):
                act.wait_ge(S["dve_init"], INIT)
                for b in (-2, -1, 0, 1):
                    act_step(act, b, b % 2)
                with act.Fori(1, 7) as k:
                    for par in range(2):
                        act_step(act, 2 * k + par, par)
                for b in (14, 15, 16):
                    act_step(act, b, b % 2)

            @block.gpsimd
            def _(pool):
                for b in (-2, -1, 0, 1):
                    pool_step(pool, b, b % 2)
                with pool.Fori(1, 7) as k:
                    for par in range(2):
                        pool_step(pool, 2 * k + par, par)
                for b in (14, 15, 16):
                    pool_step(pool, b, b % 2)

            @block.sync
            def _(sp):
                sp.wait_ge(S["dve_init"], INIT)
                load_x(sp, 0)
                for b in (-2, -1, 0, 1):
                    sp_step(sp, b, b % 2)
                with sp.Fori(1, 6) as k:
                    for par in range(2):
                        sp_step(sp, 2 * k + par, par)
                for b in (12, 13, 14, 15, 16):
                    sp_step(sp, b, b % 2)
                sp.wait_ge(S["spilled"], 16 * B)
        pa.close()

        gat = sb("gat", [128, 2 * CH, UW])
        amax = sb("amax", [128, 4, 2 * CH])
        scalars = """ax pax ag pag au pau ap pap ao pao one t t2
            step_x inv_x unit_g unit_u step_g inv_g size_g step_u inv_u size_u unit_p step_p inv_p size_p
            unit_o step_o inv_o size_o size_y""".split()
        sc = sb("sc", [128, len(scalars)])
        col = {n: sc[:, i:i + 1] for i, n in enumerate(scalars)}
        done = [0]

        def small(dve, ins):
            done[0] += 1
            ins.then_inc(S["sc_r"], 1)
            dve.wait_ge(S["sc_r"], done[0])

        def step_of(dve, name, unit, s, inv, size=None):
            small(dve, nc.vector.reciprocal(col["t"], col[unit]))
            small(dve, nc.vector.tensor_scalar(col["t2"], col["t"], FLOOR, None, ALU.mult))
            small(dve, nc.vector.tensor_scalar(col[s], col[name], 1.0 / QMAX, col["t2"], ALU.mult, ALU.max))
            small(dve, nc.vector.reciprocal(col[inv], col[s]))
            if size:
                small(dve, nc.vector.tensor_tensor(col[size], col[s], col[unit], ALU.mult))

        def over_partitions(pool, n, src, dst):
            pool.wait_ge(S["ared"], n)
            nc.gpsimd.partition_all_reduce(col[dst], col[src], 128, ABSMAX).then_inc(S["par"], 1)

        def unit(u):
            return gat[:, bass.ds(u, 1), :].rearrange("p a n -> p (a n)")

        def amax_at(i, u):
            return amax[:, i, bass.ds(u, 1)]

        XC = 2 * KT * N
        xf = x2t[:].rearrange("p b k n -> p (b k n)")
        xq = xf.bitcast(F16)

        def product(w, c, hf):
            for j in range(3):
                m = slice((3 * hf + j) * 128, (3 * hf + j + 1) * 128)
                i = 0
                for wp, xp in ((0, 0), (0, 1), (1, 0)):
                    for k in range(KT):
                        rhs = xq[:, bass.ds(c * 2 * XC + xp * XC + k * 2 * N, 2 * N)]
                        last = nc.tensor.matmul(ps[:, 3 * hf + j, 0:2 * N], w[:, wp, k, m], rhs,
                                                start=(i == 0), stop=(i == 5))
                        i += 1
            return last

        def banks_of(hf):
            return ps[:, 3 * hf:3 * hf + 3, 0:2 * N]

        def three_rows(ap):
            return ap.rearrange("p (j n) -> p j n", j=3)

        pf = ctx.enter_context(ExitStack())
        raw = [sb(f"raw{i}", [128, UW], F32, pf) for i in range(2)]
        gq = [sb(f"gq{i}", [128, UW], I16, pf) for i in range(2)]
        sig = [sb(f"sig{i}", [128, UW], F32, pf) for i in range(2)]
        sq = [sb(f"sq{i}", [128, UW], U16, pf) for i in range(2)]
        g2 = [sb(f"g2{i}", [128, UW], I16, pf) for i in range(2)]
        xi = sb("xi", [128, XC], I16, pf)

        with nc.Block() as block:
            @block.tensor
            def _(pe):
                def body(c):
                    for hf in range(2):
                        wait(pe, "xq_r", c + 1)
                        wait(pe, f"g_r{hf}", c)
                        product(wgT, c, hf).then_inc(S[f"g_ps{hf}"], 1)

                from_zero(pe, CH, body)

            @block.vector
            def _(dve):
                nc.vector.memset(col["one"], 1.0).then_inc(S["one_r"], 1)
                nc.vector.tensor_reduce(col["ax"], amax_x[:], X, ALU.max).then_inc(S["ared"], 1)
                wait(dve, "par", 1)
                wait(dve, "one_r", 1)
                step_of(dve, "pax", "one", "step_x", "inv_x")
                small(dve, nc.vector.tensor_tensor(col["unit_g"], col["step_x"], wscale[:, W_GATE:W_GATE + 1],
                                                   ALU.mult))
                small(dve, nc.vector.tensor_tensor(col["unit_u"], col["step_x"], wscale[:, W_UP:W_UP + 1],
                                                   ALU.mult))

                def integers(c):
                    wait(dve, "xq_r", c)
                    nc.vector.tensor_scalar(xi[:].rearrange("p (k b n) -> p k b n", k=KT, b=2),
                                            x2t[:, bass.ds(2 * c, 2)].rearrange("p b k n -> p k b n"),
                                            col["inv_x"], None, ALU.mult).then_inc(S["xi_r"], 1)
                    wait(dve, "xqh_r", c + 1)
                    nc.vector.tensor_tensor(xq[:, bass.ds(c * 2 * XC + XC, XC)], xi[:],
                                            xq[:, bass.ds(c * 2 * XC, XC)], ALU.subtract).then_inc(S["xq_r"], 1)

                def largest(c):
                    for hf in range(2):
                        wait(dve, f"g_r{hf}", c + 1)
                        nc.vector.tensor_reduce(amax_at(0, 2 * c + hf), unit(2 * c + hf), X, ALU.max,
                                                apply_absolute_value=True).then_inc(S["ag_r"], 1)

                integers(0)
                def body(c):
                    integers(c + 1)
                    largest(c)

                from_zero(dve, CH - 1, body)
                largest(CH - 1)
                wait(dve, "ag_r", 2 * CH)
                nc.vector.tensor_reduce(col["ag"], amax[:, 0], X, ALU.max).then_inc(S["ared"], 1)
                wait(dve, "par", 2)
                step_of(dve, "pag", "unit_g", "step_g", "inv_g", "size_g")

            @block.scalar
            def _(act):
                def high(c):
                    wait(act, "xi_r", c + 1)
                    nc.scalar.activation(xq[:, bass.ds(c * 2 * XC, XC)], xi[:], ACT.Copy).then_inc(S["xqh_r"], 1)

                def keep(c):
                    for hf in range(2):
                        wait(act, f"g_ps{hf}", c + 1)
                        nc.scalar.activation(three_rows(unit(2 * c + hf)), banks_of(hf), ACT.Copy
                                             ).then_inc(S[f"g_r{hf}"], 1)

                high(0)
                def body(c):
                    high(c + 1)
                    keep(c)

                from_zero(act, CH - 1, body)
                keep(CH - 1)

            @block.gpsimd
            def _(pool):
                over_partitions(pool, 1, "ax", "pax")
                over_partitions(pool, 2, "ag", "pag")

        with nc.Block() as block:
            @block.tensor
            def _(pe):
                def body(c):
                    for hf in range(2):
                        wait(pe, f"raw_r{hf}", c)
                        product(wuT, c, hf).then_inc(S[f"u_ps{hf}"], 1)

                from_zero(pe, CH, body)

            @block.scalar
            def _(act):
                def body(c):
                    for hf in range(2):
                        wait(act, f"p_r{hf}", c)
                        nc.scalar.activation(gq[hf][:], unit(2 * c + hf), ACT.Copy, scale=col["inv_g"]
                                             ).then_inc(S[f"gq_r{hf}"], 1)
                        wait(act, f"gq_r{hf}", c + 1)
                        wait(act, f"sq_r{hf}", c)
                        nc.scalar.activation(sig[hf][:], gq[hf][:], ACT.Sigmoid, scale=col["size_g"]
                                             ).then_inc(S[f"sig_r{hf}"], 1)
                        wait(act, f"u_ps{hf}", c + 1)
                        wait(act, f"au_r{hf}", c)
                        wait(act, f"raw_out{hf}", 16 * c)
                        nc.scalar.activation(three_rows(raw[hf][:]), banks_of(hf), ACT.Copy
                                             ).then_inc(S[f"raw_r{hf}"], 1)

                from_zero(act, CH, body)

            @block.vector
            def _(dve):
                def body(c):
                    for hf in range(2):
                        wait(dve, f"sig_r{hf}", c + 1)
                        wait(dve, f"p_r{hf}", c)
                        nc.vector.tensor_scalar(sq[hf][:], sig[hf][:], 65536.0, 65535.0, ALU.mult, ALU.min
                                                ).then_inc(S[f"sq_r{hf}"], 1)
                        wait(dve, f"sq_r{hf}", c + 1)
                        wait(dve, f"gq_r{hf}", c + 1)
                        nc.vector.tensor_tensor(unit(2 * c + hf), gq[hf][:], sq[hf][:], ALU.mult
                                                ).then_inc(S[f"p_r{hf}"], 1)
                        wait(dve, f"raw_r{hf}", c + 1)
                        nc.vector.tensor_reduce(amax_at(1, 2 * c + hf), raw[hf][:], X, ALU.max,
                                                apply_absolute_value=True).then_inc(S[f"au_r{hf}"], 1)
                        wait(dve, f"p_r{hf}", c + 1)
                        nc.vector.tensor_reduce(amax_at(2, 2 * c + hf), unit(2 * c + hf), X, ALU.max,
                                                apply_absolute_value=True).then_inc(S["ap_r"], 1)

                from_zero(dve, CH, body)
                for hf in range(2):
                    wait(dve, f"au_r{hf}", CH)
                wait(dve, "ap_r", 2 * CH)
                nc.vector.tensor_reduce(col["au"], amax[:, 1], X, ALU.max).then_inc(S["ared"], 1)
                nc.vector.tensor_reduce(col["ap"], amax[:, 2], X, ALU.max).then_inc(S["ared"], 1)
                small(dve, nc.vector.tensor_scalar(col["unit_p"], col["size_g"], 1.0 / 65536, None, ALU.mult))
                wait(dve, "par", 4)
                step_of(dve, "pau", "unit_u", "step_u", "inv_u", "size_u")
                step_of(dve, "pap", "unit_p", "step_p", "inv_p", "size_p")
                small(dve, nc.vector.tensor_tensor(col["unit_o"], col["size_u"], col["size_p"], ALU.mult))

            @block.gpsimd
            def _(pool):
                over_partitions(pool, 3, "au", "pau")
                over_partitions(pool, 4, "ap", "pap")

            @block.sync
            def _(sp):
                def body(c):
                    for hf in range(2):
                        wait(sp, f"raw_r{hf}", c + 1)
                        sp.dma_start(up_raw.ap()[bass.ds(c, 1), hf].rearrange("a p n -> (a p) n"), raw[hf][:]
                                     ).then_inc(S[f"raw_out{hf}"], 16)

                from_zero(sp, CH, body)
                for hf in range(2):
                    wait(sp, f"raw_out{hf}", 16 * CH)

        with nc.Block() as block:
            @block.sync
            def _(sp):
                def body(c):
                    for hf in range(2):
                        wait(sp, f"uq_r{hf}", c)
                        sp.dma_start(raw[hf][:], up_raw.ap()[bass.ds(c, 1), hf].rearrange("a p n -> (a p) n")
                                     ).then_inc(S[f"raw_in{hf}"], 16)

                from_zero(sp, CH, body)

            @block.gpsimd
            def _(pool):
                def body(c):
                    for hf in range(2):
                        count = valued(pool, 16 * (c + 1))
                        unregistered(pool, c)
                        wait(pool, f"raw_in{hf}", count)
                        wait(pool, f"o_r{hf}", c)
                        nc.gpsimd.tensor_scalar(gq[hf][:], raw[hf][:], col["inv_u"], 0.0, ALU.mult, ALU.add
                                                ).then_inc(S[f"uq_r{hf}"], 1)

                from_zero(pool, CH, body)
                over_partitions(pool, 5, "ao", "pao")

            @block.scalar
            def _(act):
                def body(c):
                    for hf in range(2):
                        wait(act, f"o_r{hf}", c)
                        nc.scalar.activation(g2[hf][:], unit(2 * c + hf), ACT.Copy, scale=col["inv_p"]
                                             ).then_inc(S[f"g2_r{hf}"], 1)

                from_zero(act, CH, body)

            @block.vector
            def _(dve):
                def body(c):
                    for hf in range(2):
                        wait(dve, f"uq_r{hf}", c + 1)
                        wait(dve, f"g2_r{hf}", c + 1)
                        nc.vector.tensor_tensor(unit(2 * c + hf), g2[hf][:], gq[hf][:], ALU.mult
                                                ).then_inc(S[f"o_r{hf}"], 1)
                        wait(dve, f"o_r{hf}", c + 1)
                        nc.vector.tensor_reduce(amax_at(3, 2 * c + hf), unit(2 * c + hf), X, ALU.max,
                                                apply_absolute_value=True).then_inc(S["ao_r"], 1)

                from_zero(dve, CH, body)
                wait(dve, "ao_r", 2 * CH)
                nc.vector.tensor_reduce(col["ao"], amax[:, 3], X, ALU.max).then_inc(S["ared"], 1)
                wait(dve, "par", 5)
                step_of(dve, "pao", "unit_o", "step_o", "inv_o", "size_o")
                small(dve, nc.vector.tensor_tensor(col["size_y"], col["size_o"], wscale[:, W_DOWN:W_DOWN + 1],
                                                   ALU.mult))
        pf.close()

        oq = sb("oq", [128, MT, 2 * N], I16)
        oh = [sb(f"oh{i}", [128, MT, 2 * N], F16) for i in range(2)]
        ol = [sb(f"ol{i}", [128, MT, 2 * N], F16) for i in range(2)]
        hin = [sb(f"hin{i}", [128, 2 * C]) for i in range(4)]
        y = [sb(f"y{i}", [128, 2 * C]) for i in range(4)]
        SLOTS = [(par, bb) for par in range(2) for bb in range(2)]

        with nc.Block() as block:
            @block.scalar
            def _(act):
                def body(k):
                    for par in range(2):
                        c = 2 * k + par
                        wait(act, "ol_r", c)
                        chunk = gat[:, bass.ds(2 * c, 2), :].rearrange("p a n -> p (a n)")
                        nc.scalar.activation(oq[:].rearrange("p m n -> p (m n)"), chunk, ACT.Copy,
                                             scale=col["inv_o"]).then_inc(S["oq_r"], 1)
                        wait(act, "oq_r", c + 1)
                        for bb in range(2):
                            wait(act, f"dn_ps{2 * par + bb}", k)
                        nc.scalar.activation(oh[par][:], oq[:], ACT.Copy).then_inc(S["oh_r"], 1)

                from_zero(act, CH // 2, body)

            @block.vector
            def _(dve):
                def low(k, par):
                    c = 2 * k + par
                    wait(dve, "oh_r", c + 1)
                    for bb in range(2):
                        wait(dve, f"dn_ps{2 * par + bb}", k)
                    nc.vector.tensor_tensor(ol[par][:], oq[:], oh[par][:], ALU.subtract).then_inc(S["ol_r"], 1)

                def finish(k, par):
                    for bb in range(2):
                        s = 2 * par + bb
                        wait(dve, f"dn_ps{s}", k + 1)
                        wait(dve, f"h_in{s}", 16 * (k + 1))
                        wait(dve, f"y_out{s}", 16 * k)
                        nc.vector.scalar_tensor_tensor(y[s][0:TT], ps[0:TT, s, :], col["size_y"][0:TT],
                                                       hin[s][0:TT], ALU.mult, ALU.add).then_inc(S[f"y_r{s}"], 1)

                low(0, 0)
                def body(k):
                    low(k, 1)
                    finish(k, 0)
                    low(k + 1, 0)
                    finish(k, 1)

                from_zero(dve, CH // 2 - 1, body)
                low(CH // 2 - 1, 1)
                finish(CH // 2 - 1, 0)
                finish(CH // 2 - 1, 1)

            @block.tensor
            def _(pe):
                def body(k):
                    for par in range(2):
                        wait(pe, "ol_r", 2 * k + par + 1)
                        for bb in range(2):
                            s = 2 * par + bb
                            wait(pe, f"y_r{s}", k)
                            for t in range(2):
                                rows = slice(bb * N + t * TT, bb * N + (t + 1) * TT)
                                last = three(ps[0:TT, s, t * C:(t + 1) * C],
                                             [((oh[par][:, m, rows], ol[par][:, m, rows]),
                                               (wdT[:, 0, m], wdT[:, 1, m])) for m in range(MT)])
                            last.then_inc(S[f"dn_ps{s}"], 1)

                from_zero(pe, CH // 2, body)

            @block.sync
            def _(sp):
                def load(k, s):
                    sp.dma_start(hin[s][0:TT], res.ap()[bass.ds(4 * k + s, 1)].rearrange("a p n -> (a p) n")
                                 ).then_inc(S[f"h_in{s}"], 16)

                def store(k, s):
                    count = valued(sp, k + 1)
                    dst = out[bass.ds(4 * k + s, 1)].rearrange("a (t p) c -> p (a t) c", p=TT)
                    unregistered(sp, k)
                    wait(sp, f"y_r{s}", count)
                    sp.dma_start(dst, y[s][0:TT].rearrange("p (t c) -> p t c", t=2)).then_inc(S[f"y_out{s}"], 16)

                for s in range(4):
                    load(0, s)
                def body(k):
                    for s in range(4):
                        store(k, s)
                        load(k + 1, s)

                from_zero(sp, CH // 2 - 1, body)
                for s in range(4):
                    store(CH // 2 - 1, s)
                for s in range(4):
                    wait(sp, f"y_out{s}", 16 * (CH // 2))


def kernel(x, L0_tok_W, L0_tok_b, L0_tok_gamma, L0_tok_beta, L0_tok_running_mean, L0_tok_running_var, L0_attn_Wq,
           L0_attn_Wk, L0_attn_Wv, L0_attn_Wo, L0_attn_bo, L0_attn_rel_emb, L0_ffn_w_gate, L0_ffn_w_up,
           L0_ffn_w_down):
    import concourse.bacc as bacc
    from concourse.bass_utils import run_bass_kernel_spmd

    nc = bacc.Bacc("TRN2", target_bir_lowering=False, num_devices=1)
    given = dict(x=x, cw=L0_tok_W, cb=L0_tok_b, gamma=L0_tok_gamma, beta=L0_tok_beta, rmean=L0_tok_running_mean,
                 rvar=L0_tok_running_var, wq=L0_attn_Wq, wk=L0_attn_Wk, wv=L0_attn_Wv, wo=L0_attn_Wo, bo=L0_attn_bo,
                 rel=L0_attn_rel_emb, wg=L0_ffn_w_gate, wu=L0_ffn_w_up, wd=L0_ffn_w_down, hot=bucket_onehot())
    arrays, args = {}, {}
    for name, a in given.items():
        arrays["in_" + name] = np.ascontiguousarray(a)
        args[name] = nc.dram_tensor("in_" + name, arrays["in_" + name].shape, F32, kind="ExternalInput").ap()
    out = nc.dram_tensor("out", (B, N, C), F32, kind="ExternalOutput").ap()
    audio_tower(nc, out=out, **args)
    r = run_bass_kernel_spmd(nc, [arrays], core_ids=[0])
    return r.results[0]["out"]
```

```python
import math
from contextlib import ExitStack

import numpy as np

import concourse.bass as bass
from concourse import mybir

F32, F16, BF16 = mybir.dt.float32, mybir.dt.float16, mybir.dt.bfloat16
I16, U16, I32 = mybir.dt.int16, mybir.dt.uint16, mybir.dt.int32
ALU = mybir.AluOpType
ACT = mybir.ActivationFunctionType
X = mybir.AxisListType.X
ABSMAX = bass.bass_isa.ReduceOp.absmax

B, T, D = 16, 256, 128
CTX = 5
N = T - CTX + 1
TT = N // 2
C = 256
H, DH = 16, 16
KT = C // 128
NP = 256
G = 4
INNER, MT = 768, 6
BUCKETS, MAXDIST = 32, 128
LINE = TT - 1 + N
MASKED = -3.0e38
EPS = 1e-5
QMAX, WQMAX, BLOCK = 32767.0, 7.0, 32
FLOOR = 1e-12
CH, UW = 8, 3 * 2 * N
HP = CTX - 1

W_CONV, W_Q, W_K, W_V, W_O, W_GATE, W_UP, W_DOWN = range(8)


def bucket_onehot():
    n = np.arange(-(TT - 1), N)
    large = BUCKETS // 2 + (np.log(np.maximum(n, 1) / (BUCKETS // 2)) / math.log(MAXDIST / (BUCKETS // 2))
                            * (BUCKETS - BUCKETS // 2)).astype(np.int64)
    bucket = np.where(n < BUCKETS // 2, n, np.minimum(large, BUCKETS - 1))
    hot = ((np.arange(BUCKETS)[:, None] == bucket[None, :]) & (n >= 0)[None, :]).astype(np.float32)
    return np.concatenate([hot, hot[:, ::-1]], axis=1)


def audio_tower(nc, x, cw, cb, gamma, beta, rmean, rvar, wq, wk, wv, wo, bo, rel, wg, wu, wd, hot, out):
    with ExitStack() as ctx:
        def sb(name, shape, dt=F32, scope=None):
            return (scope or ctx).enter_context(nc.sbuf_tensor(name, shape, dt))

        def sem(name):
            return ctx.enter_context(nc.semaphore(name))

        ps = ctx.enter_context(nc.psum_tensor("ps", [128, 8, 512], F32))

        line_t = nc.dram_tensor("line_t", (H, LINE), F32)
        line_n = nc.dram_tensor("line_n", (H, LINE), BF16)
        res = nc.dram_tensor("res", (B, TT, 2 * C), F32)
        up_raw = nc.dram_tensor("up_raw", (CH, 2, 128, UW), F32)

        identf = sb("identf", [128, 128])
        x2t = sb("x2t", [128, B, KT, N])
        wscale = sb("wscale", [128, 8])
        winv = sb("winv", [128, 8])
        wgT = sb("wgT", [128, 2, KT, INNER], F16)
        wuT = sb("wuT", [128, 2, KT, INNER], F16)
        wdT = sb("wdT", [128, 2, MT, C], F16)
        amax_x = sb("amax_x", [128, B])

        names = """nhalf_set w_loaded consts wamax wall wpow winv_s wdq_s wdq_i wdq_w wT_ps wT_hi wT_lo wabs lines_ps lines_sb
            lines_dram bias_in anti_r antib_r flipT_ps flipN_ps biasT_r biasN_r vec_ready vec_in ident pool_init dve_init act_init
            x_in xT_ps xh_r xl_r conv_ps u_r relu_r v1_r h_r hb_r bns_r mv_r ve_r rstd_r nb_r xn_r
            xnT_ps xnh_r xnl_r q_ps k_ps v_ps qh_r ql_r kh_r kl_r va_r stack_in
            p1_ps mx_r mT_ps mneg_r mneg_in p2_ps sb_r exp_r pv_ps osb_r oT_ps rc_r on_r onT_ps onh_r onl_r
            wo_ps h2_r spilled bns2_r mv2_r ve2_r rstd2_r nb2_r nm2_r nm_r xn2_r x2T_ps x2_r ax_r
            one_r xi_r xqh_r xq_r ag_r ared par sc_r ap_r ao_r oq_r oh_r ol_r""".split()
        names += [n + str(i) for n in "g_ps g_r u_ps raw_r raw_out raw_in gq_r sig_r sq_r p_r au_r uq_r g2_r o_r".split()
                  for i in range(2)]
        names += [n + str(i) for n in "dn_ps h_in y_r y_out".split() for i in range(4)]
        S = {n: sem(n) for n in names}

        def wait(eng, name, count):
            if isinstance(count, int) and count <= 0:
                return
            eng.wait_ge(S[name], count)

        def from_zero(eng, end, body):
            body(0)
            with eng.Fori(1, end) as i:
                body(i)

        def unregistered(eng, b):
            if not isinstance(b, int):
                eng.wait_ge(S["ident"], 2)

        def valued(eng, count):
            return count if isinstance(count, int) else eng.compute_val(count)

        pa = ctx.enter_context(ExitStack())

        def sba(name, shape, dt=F32):
            return sb(name, shape, dt, pa)

        identb = sba("identb", [128, 128], BF16)
        wcT = sba("wcT", [128, 2, CTX, C], F16)
        wqT, wkT, wvT, woT = (sba(n, [128, 2, KT, C], F16) for n in ("wqT", "wkT", "wvT", "woT"))
        bc = sba("bc", [128, 4, C])
        biasT = sba("biasT", [128, H, N])
        biasN = sba("biasN", [128, H, N], BF16)
        nhalf = sba("nhalf", [128, 2])
        epsc, minus = sba("epsc", [128, 2]), sba("minus", [128, 2])

        pw = ExitStack()
        flipT = sb("flipT", [128, H, N], F32, pw)
        flipN = sb("flipN", [128, H, N], BF16, pw)
        anti = sb("anti", [128, TT], F32, pw)
        antib = sb("antib", [128, TT], BF16, pw)
        cw_n = sb("cw_n", [128, 2, CTX * D], F32, pw)
        sq_n = sb("sq_n", [128, 4, KT, C], F32, pw)
        ff_n = sb("ff_n", [128, 3, MT * C], F32, pw)
        ff_i = sb("ff_i", [128, 3, MT * C], I16, pw)
        ff_s = sb("ff_s", [128, 3, MT * C // BLOCK], F32, pw)
        ff_r = sb("ff_r", [128, 3, MT * C // BLOCK], F32, pw)
        wam = sb("wam", [128, 8], F32, pw)
        wal = sb("wal", [128, 8], F32, pw)
        hot_s = sb("hot_s", [BUCKETS, 2 * LINE], F32, pw)
        rel_s = sb("rel_s", [BUCKETS, H], F32, pw)
        lt_s = sb("lt_s", [H, LINE], F32, pw)
        ln_s = sb("ln_s", [H, LINE], BF16, pw)
        vec = sb("vec", [128, 2, C], F32, pw)

        sq_dram = [wq, wk, wv, wo]
        ff_dram = [wg.rearrange("(m p) i -> p m i", p=128), wu.rearrange("(m p) i -> p m i", p=128),
                   wd.rearrange("(m p) i -> p m i", p=128)]
        vec_dram = [cb, gamma, beta, bo, rmean, rvar]

        def bcast(v):
            return bass.AP(v.tensor, v.offset, [[0, 128], [1, C]])

        def ff_view(i):
            return ff_n[:, i, :].rearrange("p (m c) -> p m c", m=MT if i < 2 else 2)

        blocks = []
        for c in range(CTX):
            for o in range(2):
                blocks.append((cw_n[:, o, c * D:(c + 1) * D], wcT, c, o, W_CONV))
        blocks += [None, None]
        for i, w, col in ((0, wgT, W_GATE), (1, wuT, W_UP)):
            for k in range(KT):
                for m in range(MT):
                    blocks.append((ff_view(i)[:, m, k * 128:(k + 1) * 128], w, k, m, col))
        for k in range(MT):
            for m in range(2):
                blocks.append((ff_view(2)[:, m, k * 128:(k + 1) * 128], wdT, k, m, W_DOWN))
        banks = [blocks[i:i + 4] for i in range(0, len(blocks), 4)]

        def bank_dst(group, part):
            n = sum(g is not None for g in group)
            _, w, k, m, _ = group[0]
            cols = w.shape[3]
            flat = w[:, part, :, :].rearrange("p k c -> p (k c)")
            at = k * cols + m * 128
            return flat[:, at:at + n * 128], n

        def heads(km, i):
            if i < 2:
                return sq_n[:, i, km // 2, :].rearrange("p (s m r) -> p m r s", s=8, m=2)[:, km % 2]
            return sq_n[:, i, km // 2, km % 2 * 128:km % 2 * 128 + 128]

        def square(w, part, km, i):
            cols = w[:, part, km // 2, km % 2 * 128:km % 2 * 128 + 128]
            return cols.rearrange("p (r s) -> p r s", s=8) if i < 2 else cols

        with nc.Block() as block:
            @block.sync
            def _(sp):
                sp.dma_start(cw_n[:], cw.rearrange("(o p) k -> p o k", p=128)).then_inc(S["w_loaded"], 16)
                for i, w in enumerate(sq_dram):
                    sp.dma_start(sq_n[:, i], w.rearrange("(k p) c -> p k c", p=128)).then_inc(S["w_loaded"], 16)
                for i, w in enumerate(ff_dram):
                    sp.dma_start(ff_view(i), w).then_inc(S["w_loaded"], 16)
                sp.dma_start(hot_s[:], hot).then_inc(S["consts"], 16)
                sp.dma_start(rel_s[:], rel).then_inc(S["consts"], 16)
                for i, v in enumerate(vec_dram):
                    dst = bc[:, i, :] if i < 4 else vec[:, i - 4, :]
                    sp.dma_start(dst, bcast(v)).then_inc(S["vec_in"], 16)
                sp.wait_ge(S["lines_sb"], 4)
                sp.dma_start(line_t.ap(), lt_s[:]).then_inc(S["lines_dram"], 16)
                sp.dma_start(line_n.ap(), ln_s[:]).then_inc(S["lines_dram"], 16)
                sp.wait_ge(S["lines_dram"], 32)
                sp.dma_start(flipT[0:TT], bass.AP(line_t, 0, [[1, TT], [LINE, H], [1, N]])).then_inc(S["bias_in"], 16)
                sp.dma_start(flipN[0:TT], bass.AP(line_n, 0, [[1, TT], [LINE, H], [1, N]])).then_inc(S["bias_in"], 16)

            @block.gpsimd
            def _(pool):
                nc.gpsimd.memset(identf[:], 0.0).then_inc(S["ident"], 1)
                pool.wait_ge(S["ident"], 1)
                nc.gpsimd.affine_select(out=identf[:], in_=identf[:], compare_op=ALU.not_equal, fill=1.0, base=0,
                                        pattern=[[1, 128]], channel_multiplier=-1).then_inc(S["ident"], 1)
                nc.gpsimd.memset(anti[:], 0.0).then_inc(S["anti_r"], 1)
                pool.wait_ge(S["anti_r"], 1)
                nc.gpsimd.affine_select(out=anti[:], in_=anti[:], compare_op=ALU.not_equal, fill=1.0, base=1 - TT,
                                        pattern=[[1, TT]], channel_multiplier=1).then_inc(S["anti_r"], 1)
                pool.wait_ge(S["wamax"], 8)
                nc.gpsimd.partition_all_reduce(wal[:], wam[:], 128, ABSMAX).then_inc(S["wall"], 1)
                pool.wait_ge(S["vec_in"], 96)
                nc.gpsimd.tensor_scalar(vec[:, 1, :], vec[:, 1, :], EPS, 1.0, ALU.add, ALU.mult
                                        ).then_inc(S["vec_ready"], 1)
                pool.wait_ge(S["nhalf_set"], 3)
                pool.wait_ge(S["vec_ready"], 1)
                nc.gpsimd.tensor_tensor(vec[:, 1, :], vec[:, 1, :], nhalf[:, 0:1].broadcast_to([128, C]), ALU.pow
                                        ).then_inc(S["vec_ready"], 1)
                pool.wait_ge(S["vec_ready"], 2)
                nc.gpsimd.tensor_tensor(bc[:, 1, :], bc[:, 1, :], vec[:, 1, :], ALU.mult).then_inc(S["vec_ready"], 1)
                pool.wait_ge(S["vec_ready"], 3)
                nc.gpsimd.tensor_tensor(vec[:, 0, :], vec[:, 0, :], bc[:, 1, :], ALU.mult).then_inc(S["vec_ready"], 1)
                pool.wait_ge(S["vec_ready"], 4)
                nc.gpsimd.tensor_tensor(bc[:, 2, :], bc[:, 2, :], vec[:, 0, :], ALU.subtract
                                        ).then_inc(S["vec_ready"], 1)

            @block.vector
            def _(dve):
                nc.vector.memset(nhalf[:], -0.5).then_inc(S["nhalf_set"], 1)
                nc.vector.memset(epsc[:], EPS).then_inc(S["nhalf_set"], 1)
                nc.vector.memset(minus[:], -1.0).then_inc(S["nhalf_set"], 1)
                dve.wait_ge(S["w_loaded"], 128)
                nc.vector.tensor_reduce(wam[:, 0:1], cw_n[:].rearrange("p a b -> p (a b)"), X, ALU.max,
                                        apply_absolute_value=True).then_inc(S["wamax"], 1)
                for i in range(4):
                    nc.vector.tensor_reduce(wam[:, 1 + i:2 + i], sq_n[:, i].rearrange("p a b -> p (a b)"), X,
                                            ALU.max, apply_absolute_value=True).then_inc(S["wamax"], 1)
                for i in range(3):
                    nc.vector.tensor_reduce(ff_s[:, i], ff_n[:, i].rearrange("p (a b) -> p a b", b=BLOCK), X,
                                            ALU.max, apply_absolute_value=True).then_inc(S["wabs"], 1)
                for i in range(3):
                    dve.wait_ge(S["wabs"], i + 1)
                    nc.vector.tensor_reduce(wam[:, 5 + i:6 + i], ff_s[:, i], X, ALU.max).then_inc(S["wamax"], 1)
                dve.wait_ge(S["wamax"], 8)
                nc.vector.tensor_scalar(ff_s[:], ff_s[:], 1.0 / WQMAX, FLOOR, ALU.mult, ALU.max
                                        ).then_inc(S["wdq_s"], 1)
                dve.wait_ge(S["wdq_s"], 1)
                nc.vector.reciprocal(ff_r[:], ff_s[:]).then_inc(S["wdq_s"], 1)
                dve.wait_ge(S["wdq_s"], 2)
                for i in range(3):
                    v = ff_n[:, i].rearrange("p (a b) -> p a b", b=BLOCK)
                    vi = ff_i[:, i].rearrange("p (a b) -> p a b", b=BLOCK)
                    nc.vector.tensor_tensor(vi, v, ff_r[:, i].unsqueeze(2).broadcast_to([128, 48, BLOCK]),
                                            ALU.mult).then_inc(S["wdq_i"], 1)
                    dve.wait_ge(S["wdq_i"], i + 1)
                    nc.vector.tensor_tensor(v, vi, ff_s[:, i].unsqueeze(2).broadcast_to([128, 48, BLOCK]),
                                            ALU.mult).then_inc(S["wdq_w"], 1)
                dve.wait_ge(S["wall"], 1)
                nc.vector.tensor_scalar(wal[:], wal[:], 1e-30, None, ALU.max).then_inc(S["wpow"], 1)
                dve.wait_ge(S["wpow"], 1)
                nc.vector.tensor_scalar(wal[:].bitcast(I32), wal[:].bitcast(I32), 0x7F800000, None,
                                        ALU.bitwise_and).then_inc(S["wpow"], 1)
                dve.wait_ge(S["wpow"], 2)
                nc.vector.tensor_scalar(wscale[:], wal[:], 1.0 / 64, None, ALU.mult).then_inc(S["wpow"], 1)
                dve.wait_ge(S["wpow"], 3)
                nc.vector.reciprocal(winv[:], wscale[:]).then_inc(S["winv_s"], 1)
                dve.wait_ge(S["winv_s"], 1)
                dve.wait_ge(S["ident"], 2)
                nc.vector.tensor_copy(identb[:], identf[:]).then_inc(S["dve_init"], 1)
                dve.wait_ge(S["anti_r"], 2)
                nc.vector.tensor_copy(antib[:], anti[:]).then_inc(S["antib_r"], 1)
                for i, w in enumerate((wqT, wkT, wvT, woT)):
                    dve.wait_ge(S["wT_hi"], 4 * i + 4)
                    for km in range(2 * KT):
                        nc.vector.scalar_tensor_tensor(square(w, 1, km, i), heads(km, i), winv[:, 1 + i:2 + i],
                                                       square(w, 0, km, i), ALU.mult, ALU.subtract
                                                       ).then_inc(S["wT_lo"], 1)
                dve.wait_ge(S["lines_ps"], 2)
                nc.vector.tensor_copy(lt_s[:, TT - 1:LINE], ps[0:H, 0, TT - 1:LINE]).then_inc(S["lines_sb"], 1)
                nc.vector.memset(lt_s[:, 0:TT - 1], MASKED).then_inc(S["lines_sb"], 1)
                nc.vector.tensor_copy(ln_s[:, 0:N], ps[0:H, 1, 0:N]).then_inc(S["lines_sb"], 1)
                nc.vector.memset(ln_s[:, N:LINE], MASKED).then_inc(S["lines_sb"], 1)
                for j, group in enumerate(banks):
                    hi, n = bank_dst(group, 0)
                    lo, _ = bank_dst(group, 1)
                    col = group[0][4]
                    dve.wait_ge(S["wT_hi"], 17 + j)
                    nc.vector.scalar_tensor_tensor(lo, ps[:, 2 + j % 4, 0:128 * n], winv[:, col:col + 1], hi,
                                                   ALU.mult, ALU.subtract).then_inc(S["wT_lo"], 1)
                for i in range(H // 2):
                    dve.wait_ge(S["flipN_ps"], i + 1)
                    nc.vector.tensor_copy(biasN[0:TT, 2 * i:2 * i + 2].rearrange("p h n -> p (h n)"),
                                          ps[0:TT, i % 2, 0:2 * N]).then_inc(S["biasN_r"], 1)

            @block.scalar
            def _(act):
                act.wait_ge(S["winv_s"], 1)
                for i, w in enumerate((wqT, wkT, wvT, woT)):
                    for km in range(2 * KT):
                        nc.scalar.activation(square(w, 0, km, i), heads(km, i), ACT.Copy,
                                             scale=winv[:, 1 + i:2 + i]).then_inc(S["wT_hi"], 1)
                for j, group in enumerate(banks):
                    hi, n = bank_dst(group, 0)
                    col = group[0][4]
                    act.wait_ge(S["wT_ps"], j + 1)
                    nc.scalar.activation(hi, ps[:, 2 + j % 4, 0:128 * n], ACT.Copy, scale=winv[:, col:col + 1]
                                         ).then_inc(S["wT_hi"], 1)
                for i in range(H // 2):
                    act.wait_ge(S["flipT_ps"], i + 1)
                    nc.scalar.activation(biasT[0:TT, 2 * i:2 * i + 2].rearrange("p h n -> p (h n)"),
                                         ps[0:TT, 6 + i % 2, 0:2 * N], ACT.Copy).then_inc(S["biasT_r"], 1)

            @block.tensor
            def _(pe):
                pe.wait_ge(S["consts"], 32)
                pe.wait_ge(S["ident"], 2)
                for i in range(2):
                    nc.tensor.matmul(ps[0:H, i, 0:LINE], rel_s[:], hot_s[:, i * LINE:(i + 1) * LINE],
                                     start=True, stop=True).then_inc(S["lines_ps"], 1)
                pe.wait_ge(S["wdq_w"], 3)
                pe.wait_ge(S["w_loaded"], 128)
                for j, group in enumerate(banks):
                    if j >= 4:
                        pe.wait_ge(S["wT_lo"], 16 + j - 3)
                    for n, g in enumerate(group):
                        if g is not None:
                            last = nc.tensor.transpose(ps[:, 2 + j % 4, n * 128:(n + 1) * 128], g[0], identf[:])
                    last.then_inc(S["wT_ps"], 1)
                pe.wait_ge(S["bias_in"], 32)
                pe.wait_ge(S["antib_r"], 1)
                pe.wait_ge(S["lines_sb"], 4)
                for i in range(H // 2):
                    pair = slice(2 * i, 2 * i + 2)
                    if i >= 2:
                        pe.wait_ge(S["biasT_r"], i - 1)
                        pe.wait_ge(S["biasN_r"], i - 1)
                    nc.tensor.matmul(ps[0:TT, 6 + i % 2, 0:2 * N], anti[0:TT], flipT[0:TT, pair], start=True, stop=True
                                     ).then_inc(S["flipT_ps"], 1)
                    nc.tensor.matmul(ps[0:TT, i % 2, 0:2 * N], antib[0:TT], flipN[0:TT, pair], start=True, stop=True
                                     ).then_inc(S["flipN_ps"], 1)
        pw.close()

        xin = sba("xin", [128, 2, D])
        xh, xl = sba("xh", [128, T], F16), sba("xl", [128, T], F16)
        u = sba("u", [128, 2, C])
        r1 = sba("r1", [128, 2, C])
        v1 = sba("v1", [128, 2, C])
        h = sba("h", [128, 2, C])
        hall = sba("hall", [128, B, 2 * C])
        bns, bns2 = sba("bns", [128, 2, 6]), sba("bns2", [128, 2, 6])
        mv, mv2 = sba("mv", [128, 2, 2]), sba("mv2", [128, 2, 2])
        ve, ve2 = sba("ve", [128, 2]), sba("ve2", [128, 2])
        rstd, rstd2 = sba("rstd", [128, 2]), sba("rstd2", [128, 2])
        nb, nb2 = sba("nb", [128, 2]), sba("nb2", [128, 2])
        xn, xn2 = sba("xn", [128, 2, C]), sba("xn2", [128, 2, C])
        xnh, xnl = sba("xnh", [128, KT, N], F16), sba("xnl", [128, KT, N], F16)
        qh, ql, kh, kl = (sba(n, [128, 2, NP], F16) for n in ("qh", "ql", "kh", "kl"))
        q_st, k_st = sba("q_st", [128, H, NP], F16), sba("k_st", [128, H, NP], F16)
        qS = [q_st[0:64], q_st[64:128]]
        kS = [k_st[0:64], k_st[64:128]]
        va = [sba(f"va{i}", [128, 2, H, 32]) for i in range(2)]
        mx = sba("mx", [128, 2, H])
        mneg = sba("mneg", [H, NP], F16)
        sbr = sba("sbr", [128, 4, 2 * N])
        pt = sba("pt", [128, 2, 3, 2 * N])
        osb = sba("osb", [128, G, N])
        rc = sba("rc", [128, 2, H])
        on = sba("on", [128, 2, C])
        onh, onl = sba("onh", [128, KT, N], F16), sba("onl", [128, KT, N], F16)

        OB, MB = 4, 6

        def pieces(kind, off, first, end):
            return [(kind, off, n) for n in range(first, end)]

        P2, P1 = pieces("P2", 0, 0, 12), pieces("P1", 1, 0, 12)
        PE_ORDER = [P2[0], ("k", 1, 0), P2[1], ("k", 1, 1), ("conv", 2, 0), P2[2], ("PV", -1, 3), P2[3],
                    ("conv", 2, 1), P2[4], ("conv", 2, 2), P2[5], ("OT0", -1, 0), ("conv", 2, 3), P1[0],
                    ("OT1", -1, 0), ("conv", 2, 4), P1[1], ("PV", 0, 0), ("conv", 2, 5), P1[2], P1[3],
                    ("onT", -1, 0), P1[4], ("v", 1, 0), P1[5], ("PV", 0, 1), P1[6], ("wo", -1, 0), P1[7],
                    ("wo", -1, 1), P1[8], ("v", 1, 1), P1[9], P1[10], ("xT", 3, 0), P1[11], P2[6], P2[7],
                    ("xnT", 2, 0), ("mT", 1, 0), P2[8], P2[9], ("x2T", -1, 0), P2[10], ("q", 2, 0), P2[11],
                    ("q", 2, 1), ("PV", 0, 2)]
        DVE_ORDER = [P2[0], P2[1], ("kl", 1), P2[2], P2[3], P2[4], P2[5], ("on", -1, 0), P1[0], ("on", -1, 1),
                     P1[1], ("u", 2), P1[2], P1[3], P1[4], ("onl", -1), P1[5], P1[6], P1[7],
                     ("stats", 2), P1[8], ("h2", -1), P1[9], ("stats2", -1), P1[10], ("xl", 3), P1[11], P2[6],
                     P2[7], ("mneg", 1), P2[8], ("xnl", 2), P2[9], ("ax", -1), P2[10], ("ql", 2), P2[11]]
        ACT_ORDER = [P2[0], ("kh", 1), P2[1], P2[2], ("osb", -1, 3), P2[3], P2[4], P2[5], ("osb", 0, 0),
                     ("relu", 2), ("onh", -1), ("osb", 0, 1), ("va", 1), ("xn", 2), ("xh", 3), ("xn2", -1), P2[6],
                     P2[7], ("xnh", 2), P2[8], ("x2", -1), P2[9], ("qh", 2), P2[10], ("osb", 0, 2), P2[11]]
        MISC = [[("conv", "u_r", 1, 1, 2), ("v", "va_r", 1, 1, 1), ("xnT", "xnl_r", 1, 1, 2),
                 ("q", "ql_r", 1, 1, 2)],
                [("k", "kl_r", 1, 1, 1), ("OT0", "on_r", 2, 1, -1), ("OT1", "on_r", 2, 2, -1),
                 ("onT", "onl_r", 1, 1, -1), ("wo", "h2_r", 1, 1, -1), ("xT", "xl_r", 1, 1, 3),
                 ("mT", "mneg_r", 1, 1, 1), ("x2T", "x2_r", 1, 1, -1)]]
        misc_at = {m[0]: (r, i) for r, ring in enumerate(MISC) for i, m in enumerate(ring)}
        misc_bank = {name: MB + r for name, (r, i) in misc_at.items()}
        PIECES = [st for st in PE_ORDER if st[0] in ("P1", "P2")]
        score_bank = {(kind, n): i % 4 for i, (kind, off, n) in enumerate(PIECES)}

        def runs(b, off):
            return not isinstance(b, int) or 0 <= b + off < B

        def misc_free(pe, stage, b):
            r, i = misc_at[stage]
            i -= 1
            for back in range(5):
                while i >= 0:
                    _, name, per, n, off = MISC[r][i]
                    if runs(b - back if isinstance(b, int) else b, off):
                        return wait(pe, name, per * (b - back + off) + n)
                    i -= 1
                i += len(MISC[r])

        def score_free(pe, st, b):
            i = PIECES.index(st) - 4
            for back in range(5):
                while i >= 0:
                    kind, off, n = PIECES[i]
                    if runs(b - back if isinstance(b, int) else b, off):
                        return wait(pe, "sb_r" if kind == "P2" else "mx_r", 12 * (b - back + off) + n + 1)
                    i -= 4
                i += len(PIECES)

        def piece_heads(n):
            g, j = n // 3, n % 3
            if j == 2:
                return range(4 * g, 4 * g + 4), TT
            return range(4 * g + 2 * j, 4 * g + 2 * j + 2), N

        def three(out_ap, pairs):
            todo = []
            for (ah, al), (bh, bl) in pairs:
                todo += [(ah, bh), (al, bh), (ah, bl)]
            for i, (a, w) in enumerate(todo):
                last = nc.tensor.matmul(out_ap, a, w, start=(i == 0), stop=(i == len(todo) - 1))
            return last

        def pe_step(pe, b, par):
            odd = 1 - par
            for st in PE_ORDER:
                name, off, part = st
                if not runs(b, off):
                    continue
                c = b + off
                if name in misc_at:
                    bank = ps[:, misc_bank[name], :]
                if name == "xT":
                    wait(pe, "x_in", 16 * (c + 1))
                    misc_free(pe, name, b)
                    nc.tensor.transpose(bank[:, 0:128], xin[:, 0], identf[:])
                    nc.tensor.transpose(bank[:, 128:256], xin[:, 1], identf[:]).then_inc(S["xT_ps"], 1)
                elif name == "conv":
                    if part == 0:
                        wait(pe, "xh_r", c + 1)
                        wait(pe, "xl_r", c + 1)
                        misc_free(pe, name, b)
                    t = part // 3
                    products = []
                    for i in range(CTX):
                        rows = slice(t * TT + i, t * TT + i + TT)
                        products += [(xh[:, rows], wcT[:, 0, i, :]), (xl[:, rows], wcT[:, 0, i, :]),
                                     (xh[:, rows], wcT[:, 1, i, :])]
                    for i in range(part % 3 * 5, part % 3 * 5 + 5):
                        last = nc.tensor.matmul(bank[0:TT, t * C:(t + 1) * C], *products[i], start=(i == 0),
                                                stop=(i == 14))
                    if part == 5:
                        last.then_inc(S["conv_ps"], 1)
                elif name == "xnT":
                    wait(pe, "xn_r", 2 * (c + 1))
                    misc_free(pe, name, b)
                    for k in range(KT):
                        for t in range(2):
                            last = nc.tensor.transpose(bank[:, k * N + t * TT:k * N + (t + 1) * TT],
                                                       xn[0:TT, t, k * 128:(k + 1) * 128], identf[0:TT, 0:TT])
                    last.then_inc(S["xnT_ps"], 1)
                elif name in ("q", "k"):
                    w = wqT if name == "q" else wkT
                    if part == 0:
                        wait(pe, "xnh_r", c + 1)
                        wait(pe, "xnl_r", c + 1)
                        misc_free(pe, name, b)
                    cols = slice(part * 128, (part + 1) * 128)
                    todo = [(w[:, 0, k, cols], xnh[:, k]) for k in range(KT)]
                    todo += [(w[:, 0, k, cols], xnl[:, k]) for k in range(KT)]
                    todo += [(w[:, 1, k, cols], xnh[:, k]) for k in range(KT)]
                    for i, (a, v) in enumerate(todo):
                        last = nc.tensor.matmul(bank[:, part * N:(part + 1) * N], a, v, start=(i == 0),
                                                stop=(i == 5))
                    if part == 1:
                        last.then_inc(S[name + "_ps"], 1)
                elif name == "v":
                    if part == 0:
                        misc_free(pe, name, b)
                    rows = slice(part * TT, (part + 1) * TT)
                    last = three(bank[0:TT, part * C:(part + 1) * C],
                                 [((xnh[:, k, rows], xnl[:, k, rows]), (wvT[:, 0, k], wvT[:, 1, k]))
                                  for k in range(KT)])
                    if part == 1:
                        last.then_inc(S["v_ps"], 1)
                elif name == "P1":
                    if part == 0:
                        wait(pe, "stack_in", 96 * (c + 1))
                    score_free(pe, st, b)
                    heads, w = piece_heads(part)
                    qt = slice(0, TT) if w == TT else slice(TT, N)
                    dst = ps[0:TT, score_bank[name, part], 0:2 * N]
                    nc.tensor.matmul(dst, identb[0:TT, 0:TT], biasN[0:TT, heads[0]:heads[-1] + 1, N - w:N],
                                     start=True, stop=True)
                    for n, hd in enumerate(heads):
                        last = nc.tensor.matmul(dst[:, n * w:(n + 1) * w], qS[odd][0:48, hd, qt],
                                                kS[odd][0:48, hd, 0:w], start=False, stop=True,
                                                skip_group_check=True)
                    last.then_inc(S["p1_ps"], 1)
                elif name == "mT":
                    wait(pe, "mx_r", 12 * (c + 1))
                    misc_free(pe, name, b)
                    for t in range(2):
                        last = nc.tensor.matmul(bank[0:H, t * TT:(t + 1) * TT], mx[0:TT, t, :], identf[0:TT, 0:TT],
                                                start=True, stop=True)
                    last.then_inc(S["mT_ps"], 1)
                elif name == "P2":
                    if part == 0:
                        wait(pe, "mneg_in", 16 * (c + 1))
                    score_free(pe, st, b)
                    heads, w = piece_heads(part)
                    kt = slice(TT, N) if w == TT else slice(0, TT)
                    for n, hd in enumerate(heads):
                        last = nc.tensor.matmul(ps[0:TT, score_bank[name, part], n * w:(n + 1) * w],
                                                kS[par][0:49, hd, kt], qS[par][0:49, hd, N - w:N],
                                                start=True, stop=True)
                    last.then_inc(S["p2_ps"], 1)
                elif name == "PV":
                    g, vc = part, va[odd if off else par]
                    wait(pe, "exp_r", 12 * c + 3 * (g + 1))
                    wait(pe, "va_r", c + 1)
                    wait(pe, "osb_r", 4 * c + g - 1)
                    p = pt[0:TT, g % 2]
                    for i in range(4):
                        nc.tensor.matmul(ps[32 * i:32 * i + 32, OB + g % 2, 0:N], vc[0:TT, 0, 4 * g + i, :],
                                         p[:, i // 2, (i % 2) * N:(i % 2) * N + N], start=True, stop=True,
                                         skip_group_check=True)
                    for i in range(4):
                        last = nc.tensor.matmul(ps[32 * i:32 * i + 32, OB + g % 2, TT:N],
                                                vc[0:TT, 1, 4 * g + i, :], p[:, 2, i * TT:(i + 1) * TT],
                                                start=False, stop=True, skip_group_check=True)
                    last.then_inc(S["pv_ps"], 1)
                elif name in ("OT0", "OT1"):
                    t = int(name[2])
                    wait(pe, "osb_r", 4 * (c + 1))
                    misc_free(pe, name, b)
                    for g in range(G):
                        last = nc.tensor.transpose(bank[0:TT, g * 128:(g + 1) * 128],
                                                   osb[:, g, t * TT:(t + 1) * TT], identf[:])
                    last.then_inc(S["oT_ps"], 1)
                elif name == "onT":
                    wait(pe, "on_r", 2 * (c + 1))
                    misc_free(pe, name, b)
                    for k in range(KT):
                        for t in range(2):
                            last = nc.tensor.transpose(bank[:, k * N + t * TT:k * N + (t + 1) * TT],
                                                       on[0:TT, t, k * 128:(k + 1) * 128], identf[0:TT, 0:TT])
                    last.then_inc(S["onT_ps"], 1)
                elif name == "wo":
                    if part == 0:
                        wait(pe, "onh_r", c + 1)
                        wait(pe, "onl_r", c + 1)
                        misc_free(pe, name, b)
                    rows = slice(part * TT, (part + 1) * TT)
                    last = three(bank[0:TT, part * C:(part + 1) * C],
                                 [((onh[:, k, rows], onl[:, k, rows]), (woT[:, 0, k], woT[:, 1, k]))
                                  for k in range(KT)])
                    if part == 1:
                        last.then_inc(S["wo_ps"], 1)
                elif name == "x2T":
                    wait(pe, "xn2_r", 2 * (c + 1))
                    misc_free(pe, name, b)
                    for k in range(KT):
                        for t in range(2):
                            last = nc.tensor.transpose(bank[:, k * N + t * TT:k * N + (t + 1) * TT],
                                                       xn2[0:TT, t, k * 128:(k + 1) * 128], identf[0:TT, 0:TT])
                    last.then_inc(S["x2T_ps"], 1)

        def misc(stage):
            return ps[:, misc_bank[stage], :]

        def whole(ap):
            return ap[:].rearrange("p k n -> p (k n)")

        def hall_of(c):
            return hall[0:TT, c, :] if isinstance(c, int) else hall[0:TT, bass.ds(c, 1), :].rearrange("p a n -> p (a n)")

        def x2t_of(c):
            return x2t[:, c] if isinstance(c, int) else x2t[:, bass.ds(c, 1)].rearrange("p a k n -> p (a k) n")

        def dve_step(dve, b, par):
            for st in DVE_ORDER:
                name, off = st[0], st[1]
                if not runs(b, off):
                    continue
                c = b + off
                if name == "P2":
                    n = st[2]
                    heads, w = piece_heads(n)
                    wait(dve, "p2_ps", 12 * c + n + 1)
                    wait(dve, "exp_r", 12 * c + n - 3)
                    nc.vector.tensor_tensor(sbr[0:TT, n % 4].rearrange("p (h w) -> p h w", w=w),
                                            ps[0:TT, score_bank[name, n], 0:2 * N].rearrange("p (h w) -> p h w", w=w),
                                            biasT[0:TT, heads[0]:heads[-1] + 1, 0:w], ALU.add).then_inc(S["sb_r"], 1)
                elif name == "P1":
                    n = st[2]
                    heads, w = piece_heads(n)
                    wait(dve, "p1_ps", 12 * c + n + 1)
                    if n == 0:
                        wait(dve, "mT_ps", c)
                    nc.vector.tensor_reduce(mx[0:TT, 0 if w == TT else 1, heads[0]:heads[-1] + 1],
                                            ps[0:TT, score_bank[name, n], 0:2 * N].rearrange("p (h w) -> p h w", w=w),
                                            X, ALU.max).then_inc(S["mx_r"], 1)
                elif name == "xl":
                    wait(dve, "xh_r", c + 1)
                    wait(dve, "conv_ps", c)
                    nc.vector.tensor_tensor(xl[:], misc("xT")[:, 0:T], xh[:], ALU.subtract).then_inc(S["xl_r"], 1)
                elif name == "u":
                    wait(dve, "conv_ps", c + 1)
                    wait(dve, "relu_r", c)
                    nc.vector.scalar_tensor_tensor(
                        u[0:TT], misc("conv")[0:TT].rearrange("p (t c) -> p t c", t=2), wscale[0:TT, 0:1],
                        bc[0:TT, 0:1, :].broadcast_to([TT, 2, C]), ALU.mult, ALU.add).then_inc(S["u_r"], 1)
                elif name in ("stats", "stats2"):
                    if name == "stats":
                        src, m, s6, sfx, ready = h, mv, bns, "", "h_r"
                    else:
                        src, m, s6, sfx, ready = hall_of(c).rearrange("p (t c) -> p t c", t=2), mv2, bns2, "2", "h2_r"
                    unregistered(dve, c)
                    wait(dve, ready, c + 1)
                    wait(dve, f"nb{sfx}_r", c)
                    for t in range(2):
                        nc.vector.bn_stats(s6[0:TT, t], src[0:TT, t]).then_inc(S[f"bns{sfx}_r"], 1)
                    for t in range(2):
                        count = valued(dve, 2 * c + t + 1)
                        unregistered(dve, c)
                        wait(dve, f"bns{sfx}_r", count)
                        nc.vector.bn_aggr(m[0:TT, t], s6[0:TT, t]).then_inc(S[f"mv{sfx}_r"], 1)
                elif name == "xnl":
                    wait(dve, "xnh_r", c + 1)
                    wait(dve, "v_ps", c)
                    nc.vector.tensor_tensor(whole(xnl), misc("xnT")[:, 0:2 * N], whole(xnh), ALU.subtract
                                            ).then_inc(S["xnl_r"], 1)
                elif name in ("ql", "kl"):
                    hi, lo, col = (qh, ql, 0) if name == "ql" else (kh, kl, 1)
                    wait(dve, name[0] + "h_r", c + 1)
                    wait(dve, "stack_in", 96 * c)
                    nc.vector.scalar_tensor_tensor(
                        lo[:, :, 0:N], misc(name[0])[:, 0:2 * N].rearrange("p (m n) -> p m n", m=2),
                        qks[:, col:col + 1], hi[:, :, 0:N], ALU.mult, ALU.subtract).then_inc(S[name + "_r"], 1)
                elif name == "mneg":
                    wait(dve, "mT_ps", c + 1)
                    wait(dve, "mneg_in", 16 * c)
                    nc.vector.tensor_scalar(mneg[:, 0:N], misc("mT")[0:H, 0:N], -1.0, None, ALU.mult
                                            ).then_inc(S["mneg_r"], 1)
                elif name == "on":
                    t = st[2]
                    src = misc(f"OT{t}")[0:TT].rearrange("p (h e) -> p h e", e=32)
                    wait(dve, "oT_ps", 2 * c + t + 1)
                    wait(dve, "onT_ps", c)
                    nc.vector.reciprocal(rc[0:TT, t], src[:, :, DH]).then_inc(S["rc_r"], 1)
                    wait(dve, "rc_r", 2 * c + t + 1)
                    nc.vector.tensor_tensor(on[0:TT, t].rearrange("p (h e) -> p h e", e=DH), src[:, :, 0:DH],
                                            rc[0:TT, t].unsqueeze(2).broadcast_to([TT, H, DH]), ALU.mult
                                            ).then_inc(S["on_r"], 1)
                elif name == "onl":
                    wait(dve, "onh_r", c + 1)
                    wait(dve, "wo_ps", c)
                    nc.vector.tensor_tensor(whole(onl), misc("onT")[:, 0:2 * N], whole(onh), ALU.subtract
                                            ).then_inc(S["onl_r"], 1)
                elif name == "h2":
                    wait(dve, "wo_ps", c + 1)
                    wait(dve, "hb_r", c + 1)
                    nc.vector.scalar_tensor_tensor(hall_of(c), misc("wo")[0:TT], wscale[0:TT, W_O:W_O + 1], hall_of(c),
                                                   ALU.mult, ALU.add).then_inc(S["h2_r"], 1)
                elif name == "ax":
                    wait(dve, "x2_r", c + 1)
                    dst = amax_x[:, c:c + 1] if isinstance(c, int) else amax_x[:, bass.ds(c, 1)]
                    nc.vector.tensor_reduce(dst, x2t_of(c), mybir.AxisListType.XY, ALU.max, apply_absolute_value=True
                                            ).then_inc(S["ax_r"], 1)

        def act_step(act, b, par):
            odd = 1 - par
            for st in ACT_ORDER:
                name, off = st[0], st[1]
                if not runs(b, off):
                    continue
                c = b + off
                if name == "P2":
                    n = st[2]
                    wait(act, "sb_r", 12 * c + n + 1)
                    wait(act, "pv_ps", 4 * c + n // 3 - 1)
                    nc.scalar.activation(pt[0:TT, n // 3 % 2, n % 3], sbr[0:TT, n % 4], ACT.Exp
                                         ).then_inc(S["exp_r"], 1)
                elif name == "osb":
                    g = st[2]
                    wait(act, "pv_ps", 4 * c + g + 1)
                    if g == 0:
                        wait(act, "oT_ps", 2 * c)
                    nc.scalar.activation(osb[:, g], ps[:, OB + g % 2, 0:N], ACT.Copy).then_inc(S["osb_r"], 1)
                elif name == "xh":
                    wait(act, "xT_ps", c + 1)
                    wait(act, "conv_ps", c)
                    nc.scalar.activation(xh[:], misc("xT")[:, 0:T], ACT.Copy).then_inc(S["xh_r"], 1)
                elif name == "relu":
                    wait(act, "u_r", c + 1)
                    wait(act, "v1_r", c)
                    nc.scalar.activation(r1[0:TT], u[0:TT], ACT.Relu).then_inc(S["relu_r"], 1)
                elif name in ("xn", "xn2"):
                    if name == "xn":
                        src, dst, r, o, sfx, read = h, xn, rstd, nb, "", "xnT_ps"
                    else:
                        src, dst, r, o, sfx, read = (hall_of(c).rearrange("p (t c) -> p t c", t=2), xn2, rstd2, nb2, "2",
                                                     "x2T_ps")
                    wait(act, f"nb{sfx}_r", c + 1)
                    wait(act, read, c)
                    for t in range(2):
                        nc.scalar.activation(dst[0:TT, t], src[0:TT, t], ACT.Identity, bias=o[0:TT, t:t + 1],
                                             scale=r[0:TT, t:t + 1]).then_inc(S[f"xn{sfx}_r"], 1)
                elif name == "xnh":
                    wait(act, "xnT_ps", c + 1)
                    wait(act, "v_ps", c)
                    nc.scalar.activation(whole(xnh), misc("xnT")[:, 0:2 * N], ACT.Copy).then_inc(S["xnh_r"], 1)
                elif name in ("qh", "kh"):
                    hi, col = (qh, 0) if name == "qh" else (kh, 1)
                    wait(act, name[0] + "_ps", c + 1)
                    wait(act, "stack_in", 96 * c)
                    nc.scalar.activation(hi[:, :, 0:N], misc(name[0])[:, 0:2 * N].rearrange("p (m n) -> p m n", m=2),
                                         ACT.Copy, scale=qks[:, col:col + 1]).then_inc(S[name + "_r"], 1)
                elif name == "va":
                    wait(act, "v_ps", c + 1)
                    wait(act, "pv_ps", 4 * (c - 1))
                    nc.scalar.activation(va[odd][0:TT, :, :, 0:DH],
                                         misc("v")[0:TT].rearrange("p (t h e) -> p t h e", t=2, h=H), ACT.Copy,
                                         scale=wscale[0:TT, W_V:W_V + 1]).then_inc(S["va_r"], 1)
                elif name == "onh":
                    wait(act, "onT_ps", c + 1)
                    wait(act, "wo_ps", c)
                    nc.scalar.activation(whole(onh), misc("onT")[:, 0:2 * N], ACT.Copy).then_inc(S["onh_r"], 1)
                elif name == "x2":
                    wait(act, "x2T_ps", c + 1)
                    nc.scalar.activation(x2t_of(c), misc("x2T")[:, 0:2 * N].rearrange("p (k n) -> p k n", k=KT),
                                         ACT.Copy).then_inc(S["x2_r"], 1)

        def pool_norm(pool, c, m, v, r, o, sfx):
            wait(pool, f"mv{sfx}_r", 2 * (c + 1))
            wait(pool, f"xn{sfx}_r", 2 * c)
            nc.gpsimd.tensor_tensor(v[0:TT], m[0:TT, :, 1], epsc[0:TT], ALU.add).then_inc(S[f"ve{sfx}_r"], 1)
            nc.gpsimd.tensor_tensor(o[0:TT], m[0:TT, :, 0], minus[0:TT], ALU.mult).then_inc(S[f"nm{sfx}_r"], 1)
            wait(pool, f"ve{sfx}_r", c + 1)
            nc.gpsimd.tensor_tensor(r[0:TT], v[0:TT], nhalf[0:TT], ALU.pow).then_inc(S[f"rstd{sfx}_r"], 1)
            wait(pool, f"rstd{sfx}_r", c + 1)
            wait(pool, f"nm{sfx}_r", c + 1)
            nc.gpsimd.tensor_tensor(o[0:TT], o[0:TT], r[0:TT], ALU.mult).then_inc(S[f"nb{sfx}_r"], 1)

        def pool_step(pool, b, par):
            if runs(b, 2):
                c = b + 2
                wait(pool, "relu_r", c + 1)
                wait(pool, "h_r", c)
                nc.gpsimd.tensor_tensor(v1[0:TT], r1[0:TT], bc[0:TT, 1:2, :].broadcast_to([TT, 2, C]), ALU.mult
                                        ).then_inc(S["v1_r"], 1)
                wait(pool, "v1_r", c + 1)
                wait(pool, "xn_r", 2 * c)
                wait(pool, "hb_r", c)
                nc.gpsimd.tensor_tensor(h[0:TT], v1[0:TT], bc[0:TT, 2:3, :].broadcast_to([TT, 2, C]), ALU.add
                                        ).then_inc(S["h_r"], 1)
            if runs(b, 2):
                pool_norm(pool, c, mv, ve, rstd, nb, "")
                wait(pool, "h_r", c + 1)
                hc = hall_of(c).rearrange("p (t c) -> p t c", t=2)
                nc.gpsimd.tensor_tensor(hc, h[0:TT], bc[0:TT, 3:4, :].broadcast_to([TT, 2, C]), ALU.add
                                        ).then_inc(S["hb_r"], 1)
            if runs(b, -1):
                pool_norm(pool, b - 1, mv2, ve2, rstd2, nb2, "2")

        def load_x(sp, c):
            unregistered(sp, c)
            wait(sp, "xT_ps", c)
            src = x[c] if isinstance(c, int) else x[bass.ds(c, 1)].rearrange("a t d -> (a t) d")
            sp.dma_start(xin[:], src.rearrange("(a p) d -> p a d", p=128)).then_inc(S["x_in"], 16)

        def sp_step(sp, b, par):
            odd = 1 - par
            if runs(b, 1):
                c = b + 1
                for nm, dst, parts in (("q", qS[odd], ((qh, (0, 2)), (ql, (1,)))),
                                       ("k", kS[odd], ((kh, (0, 1)), (kl, (2,))))):
                    done = valued(sp, 12 * (c - 1))
                    for (src, rows), ready in zip(parts, ("h_r", "l_r")):
                        wait(sp, nm + ready, c + 1)
                        if ready == "h_r":
                            wait(sp, "p2_ps", done)
                        for i in rows:
                            sp.dma_start(dst[16 * i:16 * i + DH], src[:]).then_inc(S["stack_in"], 16)
            if runs(b, 3):
                load_x(sp, b + 3)
            if runs(b, -1):
                c = b - 1
                unregistered(sp, c)
                wait(sp, "h2_r", c + 1)
                if isinstance(c, int):
                    sp.dma_start(res.ap()[c], hall[0:TT, c, :]).then_inc(S["spilled"], 16)
                else:
                    sp.dma_start(res.ap()[bass.ds(c, 1)].rearrange("a p n -> (a p) n"),
                                 hall[0:TT, bass.ds(c, 1), :].rearrange("p a n -> p (a n)")).then_inc(S["spilled"], 16)
            if runs(b, 1):
                c = b + 1
                wait(sp, "mneg_r", c + 1)
                sp.dma_start(qS[odd][48:49], mneg[:]).then_inc(S["mneg_in"], 16)

        INIT = 3 + 2 + 2 + 4 + 1
        qks = sba("qks", [128, 2])

        with nc.Block() as block:
            @block.tensor
            def _(pe):
                pe.wait_ge(S["dve_init"], INIT)
                for b in range(-3, 2):
                    pe_step(pe, b, b % 2)
                with pe.Fori(1, 6) as k:
                    for par in range(2):
                        pe_step(pe, 2 * k + par, par)
                for b in range(12, 17):
                    pe_step(pe, b, b % 2)

            @block.vector
            def _(dve):
                nc.vector.tensor_scalar(qks[:, 0:1], wscale[:, W_Q:W_Q + 1], DH ** -0.5, None, ALU.mult
                                        ).then_inc(S["dve_init"], 1)
                nc.vector.tensor_copy(qks[:, 1:2], wscale[:, W_K:W_K + 1]).then_inc(S["dve_init"], 1)
                for t in kS:
                    nc.vector.memset(t[32:64], 1.0).then_inc(S["dve_init"], 1)
                for t in va:
                    nc.vector.memset(t[:], 1.0).then_inc(S["dve_init"], 1)
                for t in (qh, ql, kh, kl):
                    nc.vector.memset(t[:, :, N:NP], 0.0).then_inc(S["dve_init"], 1)
                nc.vector.memset(mneg[:, N:NP], 0.0).then_inc(S["dve_init"], 1)
                dve.wait_ge(S["dve_init"], INIT)
                for b in range(-3, 2):
                    dve_step(dve, b, b % 2)
                with dve.Fori(1, 6) as k:
                    for par in range(2):
                        dve_step(dve, 2 * k + par, par)
                for b in range(12, 17):
                    dve_step(dve, b, b % 2)

            @block.scalar
            def _(act):
                act.wait_ge(S["dve_init"], INIT)
                for b in range(-3, 2):
                    act_step(act, b, b % 2)
                with act.Fori(1, 6) as k:
                    for par in range(2):
                        act_step(act, 2 * k + par, par)
                for b in range(12, 17):
                    act_step(act, b, b % 2)

            @block.gpsimd
            def _(pool):
                for b in range(-3, 2):
                    pool_step(pool, b, b % 2)
                with pool.Fori(1, 6) as k:
                    for par in range(2):
                        pool_step(pool, 2 * k + par, par)
                for b in range(12, 17):
                    pool_step(pool, b, b % 2)

            @block.sync
            def _(sp):
                sp.wait_ge(S["dve_init"], INIT)
                for b in range(-3, 2):
                    sp_step(sp, b, b % 2)
                with sp.Fori(1, 6) as k:
                    for par in range(2):
                        sp_step(sp, 2 * k + par, par)
                for b in range(12, 17):
                    sp_step(sp, b, b % 2)
                sp.wait_ge(S["spilled"], 16 * B)
        pa.close()

        gat = sb("gat", [128, 2 * CH, UW])
        amax = sb("amax", [128, 4, 2 * CH])
        scalars = """ax pax ag pag au pau ap pap ao pao one t t2
            step_x inv_x unit_g unit_u step_g inv_g size_g step_u inv_u size_u unit_p step_p inv_p size_p
            unit_o step_o inv_o size_o size_y""".split()
        sc = sb("sc", [128, len(scalars)])
        col = {n: sc[:, i:i + 1] for i, n in enumerate(scalars)}
        done = [0]

        def small(dve, ins):
            done[0] += 1
            ins.then_inc(S["sc_r"], 1)
            dve.wait_ge(S["sc_r"], done[0])

        def step_of(dve, name, unit, s, inv, size=None):
            small(dve, nc.vector.reciprocal(col["t"], col[unit]))
            small(dve, nc.vector.tensor_scalar(col["t2"], col["t"], FLOOR, None, ALU.mult))
            small(dve, nc.vector.tensor_scalar(col[s], col[name], 1.0 / QMAX, col["t2"], ALU.mult, ALU.max))
            small(dve, nc.vector.reciprocal(col[inv], col[s]))
            if size:
                small(dve, nc.vector.tensor_tensor(col[size], col[s], col[unit], ALU.mult))

        def over_partitions(pool, n, src, dst):
            pool.wait_ge(S["ared"], n)
            nc.gpsimd.partition_all_reduce(col[dst], col[src], 128, ABSMAX).then_inc(S["par"], 1)

        def unit(u):
            return gat[:, bass.ds(u, 1), :].rearrange("p a n -> p (a n)")

        def amax_at(i, u):
            return amax[:, i, bass.ds(u, 1)]

        XC = 2 * KT * N
        xf = x2t[:].rearrange("p b k n -> p (b k n)")
        xq = xf.bitcast(F16)

        def product(w, c, hf):
            for j in range(3):
                m = slice((3 * hf + j) * 128, (3 * hf + j + 1) * 128)
                i = 0
                for wp, xp in ((0, 0), (0, 1), (1, 0)):
                    for k in range(KT):
                        rhs = xq[:, bass.ds(c * 2 * XC + xp * XC + k * 2 * N, 2 * N)]
                        last = nc.tensor.matmul(ps[:, 3 * hf + j, 0:2 * N], w[:, wp, k, m], rhs,
                                                start=(i == 0), stop=(i == 5))
                        i += 1
            return last

        def banks_of(hf):
            return ps[:, 3 * hf:3 * hf + 3, 0:2 * N]

        def three_rows(ap):
            return ap.rearrange("p (j n) -> p j n", j=3)

        pf = ctx.enter_context(ExitStack())
        raw = [sb(f"raw{i}", [128, UW], F32, pf) for i in range(2)]
        gq = [sb(f"gq{i}", [128, UW], I16, pf) for i in range(2)]
        sig = [sb(f"sig{i}", [128, UW], F32, pf) for i in range(2)]
        sq = [sb(f"sq{i}", [128, UW], U16, pf) for i in range(2)]
        g2 = [sb(f"g2{i}", [128, UW], I16, pf) for i in range(2)]
        xi = sb("xi", [128, XC], I16, pf)

        with nc.Block() as block:
            @block.tensor
            def _(pe):
                def body(c):
                    for hf in range(2):
                        wait(pe, "xq_r", c + 1)
                        wait(pe, f"g_r{hf}", c)
                        product(wgT, c, hf).then_inc(S[f"g_ps{hf}"], 1)

                from_zero(pe, CH, body)

            @block.vector
            def _(dve):
                nc.vector.memset(col["one"], 1.0).then_inc(S["one_r"], 1)
                nc.vector.tensor_reduce(col["ax"], amax_x[:], X, ALU.max).then_inc(S["ared"], 1)
                wait(dve, "par", 1)
                wait(dve, "one_r", 1)
                step_of(dve, "pax", "one", "step_x", "inv_x")
                small(dve, nc.vector.tensor_tensor(col["unit_g"], col["step_x"], wscale[:, W_GATE:W_GATE + 1],
                                                   ALU.mult))
                small(dve, nc.vector.tensor_tensor(col["unit_u"], col["step_x"], wscale[:, W_UP:W_UP + 1],
                                                   ALU.mult))

                def integers(c):
                    wait(dve, "xq_r", c)
                    nc.vector.tensor_scalar(xi[:].rearrange("p (k b n) -> p k b n", k=KT, b=2),
                                            x2t[:, bass.ds(2 * c, 2)].rearrange("p b k n -> p k b n"),
                                            col["inv_x"], None, ALU.mult).then_inc(S["xi_r"], 1)
                    wait(dve, "xqh_r", c + 1)
                    nc.vector.tensor_tensor(xq[:, bass.ds(c * 2 * XC + XC, XC)], xi[:],
                                            xq[:, bass.ds(c * 2 * XC, XC)], ALU.subtract).then_inc(S["xq_r"], 1)

                def largest(c):
                    for hf in range(2):
                        wait(dve, f"g_r{hf}", c + 1)
                        nc.vector.tensor_reduce(amax_at(0, 2 * c + hf), unit(2 * c + hf), X, ALU.max,
                                                apply_absolute_value=True).then_inc(S["ag_r"], 1)

                integers(0)
                def body(c):
                    integers(c + 1)
                    largest(c)

                from_zero(dve, CH - 1, body)
                largest(CH - 1)
                wait(dve, "ag_r", 2 * CH)
                nc.vector.tensor_reduce(col["ag"], amax[:, 0], X, ALU.max).then_inc(S["ared"], 1)
                wait(dve, "par", 2)
                step_of(dve, "pag", "unit_g", "step_g", "inv_g", "size_g")

            @block.scalar
            def _(act):
                def high(c):
                    wait(act, "xi_r", c + 1)
                    nc.scalar.activation(xq[:, bass.ds(c * 2 * XC, XC)], xi[:], ACT.Copy).then_inc(S["xqh_r"], 1)

                def keep(c):
                    for hf in range(2):
                        wait(act, f"g_ps{hf}", c + 1)
                        nc.scalar.activation(three_rows(unit(2 * c + hf)), banks_of(hf), ACT.Copy
                                             ).then_inc(S[f"g_r{hf}"], 1)

                high(0)
                def body(c):
                    high(c + 1)
                    keep(c)

                from_zero(act, CH - 1, body)
                keep(CH - 1)

            @block.gpsimd
            def _(pool):
                over_partitions(pool, 1, "ax", "pax")
                over_partitions(pool, 2, "ag", "pag")

        with nc.Block() as block:
            @block.tensor
            def _(pe):
                def body(c):
                    for hf in range(2):
                        wait(pe, f"raw_r{hf}", c)
                        product(wuT, c, hf).then_inc(S[f"u_ps{hf}"], 1)

                from_zero(pe, CH, body)

            @block.scalar
            def _(act):
                def body(c):
                    for hf in range(2):
                        wait(act, f"p_r{hf}", c)
                        nc.scalar.activation(gq[hf][:], unit(2 * c + hf), ACT.Copy, scale=col["inv_g"]
                                             ).then_inc(S[f"gq_r{hf}"], 1)
                        wait(act, f"gq_r{hf}", c + 1)
                        wait(act, f"sq_r{hf}", c)
                        nc.scalar.activation(sig[hf][:], gq[hf][:], ACT.Sigmoid, scale=col["size_g"]
                                             ).then_inc(S[f"sig_r{hf}"], 1)
                        wait(act, f"u_ps{hf}", c + 1)
                        wait(act, f"au_r{hf}", c)
                        wait(act, f"raw_out{hf}", 16 * c)
                        nc.scalar.activation(three_rows(raw[hf][:]), banks_of(hf), ACT.Copy
                                             ).then_inc(S[f"raw_r{hf}"], 1)

                from_zero(act, CH, body)

            @block.vector
            def _(dve):
                def body(c):
                    for hf in range(2):
                        wait(dve, f"sig_r{hf}", c + 1)
                        wait(dve, f"p_r{hf}", c)
                        nc.vector.tensor_scalar(sq[hf][:], sig[hf][:], 65536.0, 65535.0, ALU.mult, ALU.min
                                                ).then_inc(S[f"sq_r{hf}"], 1)
                        wait(dve, f"sq_r{hf}", c + 1)
                        wait(dve, f"gq_r{hf}", c + 1)
                        nc.vector.tensor_tensor(unit(2 * c + hf), gq[hf][:], sq[hf][:], ALU.mult
                                                ).then_inc(S[f"p_r{hf}"], 1)
                        wait(dve, f"raw_r{hf}", c + 1)
                        nc.vector.tensor_reduce(amax_at(1, 2 * c + hf), raw[hf][:], X, ALU.max,
                                                apply_absolute_value=True).then_inc(S[f"au_r{hf}"], 1)
                        wait(dve, f"p_r{hf}", c + 1)
                        nc.vector.tensor_reduce(amax_at(2, 2 * c + hf), unit(2 * c + hf), X, ALU.max,
                                                apply_absolute_value=True).then_inc(S["ap_r"], 1)

                from_zero(dve, CH, body)
                for hf in range(2):
                    wait(dve, f"au_r{hf}", CH)
                wait(dve, "ap_r", 2 * CH)
                nc.vector.tensor_reduce(col["au"], amax[:, 1], X, ALU.max).then_inc(S["ared"], 1)
                nc.vector.tensor_reduce(col["ap"], amax[:, 2], X, ALU.max).then_inc(S["ared"], 1)
                small(dve, nc.vector.tensor_scalar(col["unit_p"], col["size_g"], 1.0 / 65536, None, ALU.mult))
                wait(dve, "par", 4)
                step_of(dve, "pau", "unit_u", "step_u", "inv_u", "size_u")
                step_of(dve, "pap", "unit_p", "step_p", "inv_p", "size_p")
                small(dve, nc.vector.tensor_tensor(col["unit_o"], col["size_u"], col["size_p"], ALU.mult))

            @block.gpsimd
            def _(pool):
                over_partitions(pool, 3, "au", "pau")
                over_partitions(pool, 4, "ap", "pap")

            @block.sync
            def _(sp):
                def body(c):
                    for hf in range(2):
                        wait(sp, f"raw_r{hf}", c + 1)
                        sp.dma_start(up_raw.ap()[bass.ds(c, 1), hf].rearrange("a p n -> (a p) n"), raw[hf][:]
                                     ).then_inc(S[f"raw_out{hf}"], 16)

                from_zero(sp, CH, body)
                for hf in range(2):
                    wait(sp, f"raw_out{hf}", 16 * CH)

        with nc.Block() as block:
            @block.sync
            def _(sp):
                def body(c):
                    for hf in range(2):
                        wait(sp, f"uq_r{hf}", c)
                        sp.dma_start(raw[hf][:], up_raw.ap()[bass.ds(c, 1), hf].rearrange("a p n -> (a p) n")
                                     ).then_inc(S[f"raw_in{hf}"], 16)

                from_zero(sp, CH, body)

            @block.gpsimd
            def _(pool):
                def body(c):
                    for hf in range(2):
                        count = valued(pool, 16 * (c + 1))
                        unregistered(pool, c)
                        wait(pool, f"raw_in{hf}", count)
                        wait(pool, f"o_r{hf}", c)
                        nc.gpsimd.tensor_scalar(gq[hf][:], raw[hf][:], col["inv_u"], 0.0, ALU.mult, ALU.add
                                                ).then_inc(S[f"uq_r{hf}"], 1)

                from_zero(pool, CH, body)
                over_partitions(pool, 5, "ao", "pao")

            @block.scalar
            def _(act):
                def body(c):
                    for hf in range(2):
                        wait(act, f"o_r{hf}", c)
                        nc.scalar.activation(g2[hf][:], unit(2 * c + hf), ACT.Copy, scale=col["inv_p"]
                                             ).then_inc(S[f"g2_r{hf}"], 1)

                from_zero(act, CH, body)

            @block.vector
            def _(dve):
                def body(c):
                    for hf in range(2):
                        wait(dve, f"uq_r{hf}", c + 1)
                        wait(dve, f"g2_r{hf}", c + 1)
                        nc.vector.tensor_tensor(unit(2 * c + hf), g2[hf][:], gq[hf][:], ALU.mult
                                                ).then_inc(S[f"o_r{hf}"], 1)
                        wait(dve, f"o_r{hf}", c + 1)
                        nc.vector.tensor_reduce(amax_at(3, 2 * c + hf), unit(2 * c + hf), X, ALU.max,
                                                apply_absolute_value=True).then_inc(S["ao_r"], 1)

                from_zero(dve, CH, body)
                wait(dve, "ao_r", 2 * CH)
                nc.vector.tensor_reduce(col["ao"], amax[:, 3], X, ALU.max).then_inc(S["ared"], 1)
                wait(dve, "par", 5)
                step_of(dve, "pao", "unit_o", "step_o", "inv_o", "size_o")
                small(dve, nc.vector.tensor_tensor(col["size_y"], col["size_o"], wscale[:, W_DOWN:W_DOWN + 1],
                                                   ALU.mult))
        pf.close()

        oq = sb("oq", [128, MT, 2 * N], I16)
        oh = [sb(f"oh{i}", [128, MT, 2 * N], F16) for i in range(2)]
        ol = [sb(f"ol{i}", [128, MT, 2 * N], F16) for i in range(2)]
        hin = [sb(f"hin{i}", [128, 2 * C]) for i in range(4)]
        y = [sb(f"y{i}", [128, 2 * C]) for i in range(4)]
        SLOTS = [(par, bb) for par in range(2) for bb in range(2)]

        with nc.Block() as block:
            @block.scalar
            def _(act):
                def body(k):
                    for par in range(2):
                        c = 2 * k + par
                        wait(act, "ol_r", c)
                        chunk = gat[:, bass.ds(2 * c, 2), :].rearrange("p a n -> p (a n)")
                        nc.scalar.activation(oq[:].rearrange("p m n -> p (m n)"), chunk, ACT.Copy,
                                             scale=col["inv_o"]).then_inc(S["oq_r"], 1)
                        wait(act, "oq_r", c + 1)
                        for bb in range(2):
                            wait(act, f"dn_ps{2 * par + bb}", k)
                        nc.scalar.activation(oh[par][:], oq[:], ACT.Copy).then_inc(S["oh_r"], 1)

                from_zero(act, CH // 2, body)

            @block.vector
            def _(dve):
                def low(k, par):
                    c = 2 * k + par
                    wait(dve, "oh_r", c + 1)
                    for bb in range(2):
                        wait(dve, f"dn_ps{2 * par + bb}", k)
                    nc.vector.tensor_tensor(ol[par][:], oq[:], oh[par][:], ALU.subtract).then_inc(S["ol_r"], 1)

                def finish(k, par):
                    for bb in range(2):
                        s = 2 * par + bb
                        wait(dve, f"dn_ps{s}", k + 1)
                        wait(dve, f"h_in{s}", 16 * (k + 1))
                        wait(dve, f"y_out{s}", 16 * k)
                        nc.vector.scalar_tensor_tensor(y[s][0:TT], ps[0:TT, s, :], col["size_y"][0:TT],
                                                       hin[s][0:TT], ALU.mult, ALU.add).then_inc(S[f"y_r{s}"], 1)

                low(0, 0)
                def body(k):
                    low(k, 1)
                    finish(k, 0)
                    low(k + 1, 0)
                    finish(k, 1)

                from_zero(dve, CH // 2 - 1, body)
                low(CH // 2 - 1, 1)
                finish(CH // 2 - 1, 0)
                finish(CH // 2 - 1, 1)

            @block.tensor
            def _(pe):
                def body(k):
                    for par in range(2):
                        wait(pe, "ol_r", 2 * k + par + 1)
                        for bb in range(2):
                            s = 2 * par + bb
                            wait(pe, f"y_r{s}", k)
                            for t in range(2):
                                rows = slice(bb * N + t * TT, bb * N + (t + 1) * TT)
                                last = three(ps[0:TT, s, t * C:(t + 1) * C],
                                             [((oh[par][:, m, rows], ol[par][:, m, rows]),
                                               (wdT[:, 0, m], wdT[:, 1, m])) for m in range(MT)])
                            last.then_inc(S[f"dn_ps{s}"], 1)

                from_zero(pe, CH // 2, body)

            @block.sync
            def _(sp):
                def load(k, s):
                    sp.dma_start(hin[s][0:TT], res.ap()[bass.ds(4 * k + s, 1)].rearrange("a p n -> (a p) n")
                                 ).then_inc(S[f"h_in{s}"], 16)

                def store(k, s):
                    count = valued(sp, k + 1)
                    dst = out[bass.ds(4 * k + s, 1)].rearrange("a (t p) c -> p (a t) c", p=TT)
                    unregistered(sp, k)
                    wait(sp, f"y_r{s}", count)
                    sp.dma_start(dst, y[s][0:TT].rearrange("p (t c) -> p t c", t=2)).then_inc(S[f"y_out{s}"], 16)

                for s in range(4):
                    load(0, s)
                def body(k):
                    for s in range(4):
                        store(k, s)
                        load(k + 1, s)

                from_zero(sp, CH // 2 - 1, body)
                for s in range(4):
                    store(CH // 2 - 1, s)
                for s in range(4):
                    wait(sp, f"y_out{s}", 16 * (CH // 2))


def kernel(x, L0_tok_W, L0_tok_b, L0_tok_gamma, L0_tok_beta, L0_tok_running_mean, L0_tok_running_var, L0_attn_Wq,
           L0_attn_Wk, L0_attn_Wv, L0_attn_Wo, L0_attn_bo, L0_attn_rel_emb, L0_ffn_w_gate, L0_ffn_w_up,
           L0_ffn_w_down):
    import concourse.bacc as bacc
    from concourse.bass_utils import run_bass_kernel_spmd

    nc = bacc.Bacc("TRN2", target_bir_lowering=False, num_devices=1)
    given = dict(x=x, cw=L0_tok_W, cb=L0_tok_b, gamma=L0_tok_gamma, beta=L0_tok_beta, rmean=L0_tok_running_mean,
                 rvar=L0_tok_running_var, wq=L0_attn_Wq, wk=L0_attn_Wk, wv=L0_attn_Wv, wo=L0_attn_Wo, bo=L0_attn_bo,
                 rel=L0_attn_rel_emb, wg=L0_ffn_w_gate, wu=L0_ffn_w_up, wd=L0_ffn_w_down, hot=bucket_onehot())
    arrays, args = {}, {}
    for name, a in given.items():
        arrays["in_" + name] = np.ascontiguousarray(a)
        args[name] = nc.dram_tensor("in_" + name, arrays["in_" + name].shape, F32, kind="ExternalInput").ap()
    out = nc.dram_tensor("out", (B, N, C), F32, kind="ExternalOutput").ap()
    audio_tower(nc, out=out, **args)
    r = run_bass_kernel_spmd(nc, [arrays], core_ids=[0])
    return r.results[0]["out"]
```

```python
import math
from contextlib import ExitStack

import numpy as np

import concourse.bass as bass
from concourse import mybir

F32, F16, BF16 = mybir.dt.float32, mybir.dt.float16, mybir.dt.bfloat16
I16, U16, I32 = mybir.dt.int16, mybir.dt.uint16, mybir.dt.int32
ALU = mybir.AluOpType
ACT = mybir.ActivationFunctionType
X = mybir.AxisListType.X
ABSMAX = bass.bass_isa.ReduceOp.absmax

B, T, D = 16, 256, 128
CTX = 5
N = T - CTX + 1
TT = N // 2
C = 256
H, DH = 16, 16
KT = C // 128
NP = 256
G = 4
INNER, MT = 768, 6
BUCKETS, MAXDIST = 32, 128
LINE = TT - 1 + N
MASKED = -3.0e38
EPS = 1e-5
QMAX, WQMAX, BLOCK = 32767.0, 7.0, 32
FLOOR = 1e-12
CH, UW = 8, 3 * 2 * N
TWO_ONES = float(np.ones(2, np.float16).view(np.float32)[0])

W_CONV, W_Q, W_K, W_V, W_O, W_GATE, W_UP, W_DOWN = range(8)


def bucket_onehot():
    n = np.arange(-(TT - 1), N)
    large = BUCKETS // 2 + (np.log(np.maximum(n, 1) / (BUCKETS // 2)) / math.log(MAXDIST / (BUCKETS // 2))
                            * (BUCKETS - BUCKETS // 2)).astype(np.int64)
    bucket = np.where(n < BUCKETS // 2, n, np.minimum(large, BUCKETS - 1))
    hot = ((np.arange(BUCKETS)[:, None] == bucket[None, :]) & (n >= 0)[None, :]).astype(np.float32)
    return np.concatenate([hot, hot[:, ::-1]], axis=1)


def audio_tower(nc, x, cw, cb, gamma, beta, rmean, rvar, wq, wk, wv, wo, bo, rel, wg, wu, wd, hot, out):
    with ExitStack() as ctx:
        def sb(name, shape, dt=F32, scope=None):
            return (scope or ctx).enter_context(nc.sbuf_tensor(name, shape, dt))

        def sem(name):
            return ctx.enter_context(nc.semaphore(name))

        ps = ctx.enter_context(nc.psum_tensor("ps", [128, 8, 512], F32))

        line_t = nc.dram_tensor("line_t", (H, LINE), F32)
        line_n = nc.dram_tensor("line_n", (H, LINE), BF16)
        res = nc.dram_tensor("res", (B, TT, 2 * C), F32)
        up_raw = nc.dram_tensor("up_raw", (CH, 2, 128, UW), F32)

        identf = sb("identf", [128, 128])
        x2t = sb("x2t", [128, B, KT, N])
        wscale = sb("wscale", [128, 8])
        winv = sb("winv", [128, 8])
        wgT = sb("wgT", [128, 2, KT, INNER], F16)
        wuT = sb("wuT", [128, 2, KT, INNER], F16)
        wdT = sb("wdT", [128, 2, MT, C], F16)
        amax_x = sb("amax_x", [128, B])

        names = """nhalf_set w_loaded ff_in var_in rstd_out ffT_ps ff_hi ff_lo consts wamax wall wpow winv_s wdq_s wdq_i wdq_w wT_ps wT_hi wT_lo wabs lines_ps lines_sb
            lines_dram bias_in anti_r antib_r flipT_ps flipN_ps biasT_r biasN_r vec_ready vec_in ident pool_init dve_init act_init
            x_in xT_ps xh_r xl_r conv_ps u_r relu_r v1_r h_r hb_r bns_r mv_r ve_r rstd_r nb_r xn_r
            xnT_ps xnh_r xnl_r q_ps k_ps v_ps qh_r ql_r kh_r kl_r va_r stack_in
            p1_ps mx_r mT_ps mneg_r mneg_in p2_ps sb_r exp_r pv_ps osb_r oT_ps rc_r on_r onT_ps onh_r onl_r
            wo_ps h2_r spilled bns2_r mv2_r ve2_r rstd2_r nb2_r nm2_r nm_r xn2_r x2T_ps x2_r ax_r
            xi_r xqh_r xq_r ag_r ared par sc_r ap_r ao_r oq_r oh_r ol_r""".split()
        names += [n + str(i) for n in "g_ps g_r u_ps raw_r raw_out raw_in gq_r sig_r sq_r p_r au_r uq_r g2_r o_r".split()
                  for i in range(2)]
        names += [n + str(i) for n in "dn_ps h_in y_r y_out".split() for i in range(4)]
        S = {n: sem(n) for n in names}

        def wait(eng, name, count):
            if isinstance(count, int) and count <= 0:
                return
            eng.wait_ge(S[name], count)

        def from_zero(eng, end, body):
            body(0)
            with eng.Fori(1, end) as i:
                body(i)

        def unregistered(eng, b):
            if not isinstance(b, int):
                eng.wait_ge(S["ident"], 2)

        def valued(eng, count):
            return count if isinstance(count, int) else eng.compute_val(count)

        pa = ctx.enter_context(ExitStack())

        def sba(name, shape, dt=F32):
            return sb(name, shape, dt, pa)

        identb = sba("identb", [128, 128], BF16)
        wcT = sba("wcT", [128, 2, CTX, C], F16)
        wqT, wkT, wvT, woT = (sba(n, [128, 2, KT, C], F16) for n in ("wqT", "wkT", "wvT", "woT"))
        bc = sba("bc", [128, 4, C])
        biasT = sba("biasT", [128, H, N])
        biasN = sba("biasN", [128, H, N], BF16)
        nhalf = sba("nhalf", [128, 2])
        epsc, minus = sba("epsc", [128, 2]), sba("minus", [128, 2])

        q_st, k_st = sba("q_st", [128, H, NP], F16), sba("k_st", [128, H, NP], F16)
        qS = [q_st[0:64], q_st[64:128]]
        kS = [k_st[0:64], k_st[64:128]]
        va = [sba(f"va{i}", [128, 2, H, 32]) for i in range(2)]
        qh, ql, kh, kl = (sba(n, [128, 2, NP], F16) for n in ("qh", "ql", "kh", "kl"))
        mneg = sba("mneg", [H, NP], F16)
        qks = sba("qks", [128, 2])
        wam = sba("wam", [128, 8])
        wal = sba("wal", [128, 8])
        x2_flat = x2t[:].rearrange("p b k n -> p (b k n)")
        FF, NB = MT * C, MT * C // BLOCK
        ff_n = x2_flat[:, 0:3 * FF].rearrange("p (i c) -> p i c", i=3)
        ff_i = x2_flat[:, 3 * FF:9 * FF // 2].bitcast(I16).rearrange("p (i c) -> p i c", i=3)
        ff_s = x2_flat[:, 9 * FF // 2:9 * FF // 2 + 3 * NB].rearrange("p (i c) -> p i c", i=3)
        ff_r = x2_flat[:, 9 * FF // 2 + 3 * NB:9 * FF // 2 + 6 * NB].rearrange("p (i c) -> p i c", i=3)

        pw = ExitStack()
        flipT = sb("flipT", [128, H, N], F32, pw)
        flipN = sb("flipN", [128, H, N], BF16, pw)
        anti = sb("anti", [128, TT], F32, pw)
        antib = sb("antib", [128, TT], BF16, pw)
        cw_n = sb("cw_n", [128, 2, CTX * D], F32, pw)
        sq_n = sb("sq_n", [128, 4, KT, C], F32, pw)
        hot_s = sb("hot_s", [BUCKETS, 2 * LINE], F32, pw)
        rel_s = sb("rel_s", [BUCKETS, H], F32, pw)
        lt_s = sb("lt_s", [H, LINE], F32, pw)
        ln_s = sb("ln_s", [H, LINE], BF16, pw)
        var = sb("var", [128, 2], F32, pw)
        vec = sb("vec", [128, 2, C], F32, pw)

        sq_dram = [wq, wk, wv, wo]
        ff_dram = [wg.rearrange("(m p) i -> p m i", p=128), wu.rearrange("(m p) i -> p m i", p=128),
                   wd.rearrange("(m p) i -> p m i", p=128)]
        vec_dram = [cb, gamma, beta, bo, rmean]
        rstd_line = nc.dram_tensor("rstd_line", (C,), F32)

        def bcast(v):
            return bass.AP(v.tensor, v.offset, [[0, 128], [1, C]])

        def ff_view(i):
            return ff_n[:, i, :].rearrange("p (m c) -> p m c", m=MT if i < 2 else 2)

        blocks = []
        for c in range(CTX):
            for o in range(2):
                blocks.append((cw_n[:, o, c * D:(c + 1) * D], wcT, c, o, W_CONV))
        ff_blocks = []
        for i, w, col in ((0, wgT, W_GATE), (1, wuT, W_UP)):
            for k in range(KT):
                for m in range(MT):
                    ff_blocks.append((ff_view(i)[:, m, k * 128:(k + 1) * 128], w, k, m, col))
        for k in range(MT):
            for m in range(2):
                ff_blocks.append((ff_view(2)[:, m, k * 128:(k + 1) * 128], wdT, k, m, W_DOWN))
        banks = [blocks[i:i + 4] for i in range(0, len(blocks), 4)]
        ff_banks = [ff_blocks[i:i + 4] for i in range(0, len(ff_blocks), 4)]

        def bank_dst(group, part):
            n = len(group)
            _, w, k, m, _ = group[0]
            cols = w.shape[3]
            flat = w[:, part, :, :].rearrange("p k c -> p (k c)")
            at = k * cols + m * 128
            return flat[:, at:at + n * 128], n

        def heads(km, i):
            if i < 2:
                return sq_n[:, i, km // 2, :].rearrange("p (s m r) -> p m r s", s=8, m=2)[:, km % 2]
            return sq_n[:, i, km // 2, km % 2 * 128:km % 2 * 128 + 128]

        def square(w, part, km, i):
            cols = w[:, part, km // 2, km % 2 * 128:km % 2 * 128 + 128]
            return cols.rearrange("p (r s) -> p r s", s=8) if i < 2 else cols

        def power(dve, cols, nth):
            dve.wait_ge(S["wall"], nth)
            nc.vector.tensor_scalar(wal[:, cols], wal[:, cols], 1e-30, None, ALU.max).then_inc(S["wpow"], 1)
            dve.wait_ge(S["wpow"], 3 * nth - 2)
            nc.vector.tensor_scalar(wal[:, cols].bitcast(I32), wal[:, cols].bitcast(I32), 0x7F800000, None,
                                    ALU.bitwise_and).then_inc(S["wpow"], 1)
            dve.wait_ge(S["wpow"], 3 * nth - 1)
            nc.vector.tensor_scalar(wscale[:, cols], wal[:, cols], 1.0 / 64, None, ALU.mult).then_inc(S["wpow"], 1)
            dve.wait_ge(S["wpow"], 3 * nth)
            nc.vector.reciprocal(winv[:, cols], wscale[:, cols]).then_inc(S["winv_s"], 1)

        with nc.Block() as block:
            @block.sync
            def _(sp):
                sp.dma_start(hot_s[:], hot).then_inc(S["consts"], 16)
                sp.dma_start(rel_s[:], rel).then_inc(S["consts"], 16)
                sp.dma_start(cw_n[:], cw.rearrange("(o p) k -> p o k", p=128)).then_inc(S["w_loaded"], 16)
                for i, w in enumerate(sq_dram):
                    sp.dma_start(sq_n[:, i], w.rearrange("(k p) c -> p k c", p=128)).then_inc(S["w_loaded"], 16)
                sp.wait_ge(S["lines_sb"], 4)
                sp.dma_start(line_t.ap(), lt_s[:]).then_inc(S["lines_dram"], 16)
                sp.dma_start(line_n.ap(), ln_s[:]).then_inc(S["lines_dram"], 16)
                sp.wait_ge(S["lines_dram"], 32)
                sp.dma_start(flipT[0:TT], bass.AP(line_t, 0, [[1, TT], [LINE, H], [1, N]])).then_inc(S["bias_in"], 16)
                sp.dma_start(flipN[0:TT], bass.AP(line_n, 0, [[1, TT], [LINE, H], [1, N]])).then_inc(S["bias_in"], 16)

            @block.gpsimd
            def _(pool):
                nc.gpsimd.memset(identf[:], 0.0).then_inc(S["ident"], 1)
                pool.wait_ge(S["ident"], 1)
                nc.gpsimd.affine_select(out=identf[:], in_=identf[:], compare_op=ALU.not_equal, fill=1.0, base=0,
                                        pattern=[[1, 128]], channel_multiplier=-1).then_inc(S["ident"], 1)
                nc.gpsimd.memset(anti[:], 0.0).then_inc(S["anti_r"], 1)
                pool.wait_ge(S["anti_r"], 1)
                nc.gpsimd.affine_select(out=anti[:], in_=anti[:], compare_op=ALU.not_equal, fill=1.0, base=1 - TT,
                                        pattern=[[1, TT]], channel_multiplier=1).then_inc(S["anti_r"], 1)
                pool.wait_ge(S["var_in"], 16)
                nc.gpsimd.tensor_scalar(var[:], var[:], EPS, 1.0, ALU.add, ALU.mult).then_inc(S["vec_ready"], 1)
                pool.wait_ge(S["nhalf_set"], 3)
                pool.wait_ge(S["vec_ready"], 1)
                nc.gpsimd.tensor_tensor(var[:], var[:], nhalf[:], ALU.pow).then_inc(S["vec_ready"], 1)
                pool.wait_ge(S["wamax"], 5)
                nc.gpsimd.partition_all_reduce(wal[:, 0:5], wam[:, 0:5], 128, ABSMAX).then_inc(S["wall"], 1)
                pool.wait_ge(S["vec_in"], 96)
                nc.gpsimd.tensor_tensor(bc[:, 1, :], bc[:, 1, :], vec[:, 1, :], ALU.mult).then_inc(S["vec_ready"], 1)
                pool.wait_ge(S["vec_ready"], 3)
                nc.gpsimd.tensor_tensor(vec[:, 0, :], vec[:, 0, :], bc[:, 1, :], ALU.mult).then_inc(S["vec_ready"], 1)
                pool.wait_ge(S["vec_ready"], 4)
                nc.gpsimd.tensor_tensor(bc[:, 2, :], bc[:, 2, :], vec[:, 0, :], ALU.subtract
                                        ).then_inc(S["vec_ready"], 1)

            @block.vector
            def _(dve):
                nc.vector.memset(nhalf[:], -0.5).then_inc(S["nhalf_set"], 1)
                nc.vector.memset(epsc[:], EPS).then_inc(S["nhalf_set"], 1)
                nc.vector.memset(minus[:], -1.0).then_inc(S["nhalf_set"], 1)
                nc.vector.memset(lt_s[:, 0:TT - 1], MASKED).then_inc(S["lines_sb"], 1)
                nc.vector.memset(ln_s[:, N:LINE], MASKED).then_inc(S["lines_sb"], 1)
                dve.wait_ge(S["lines_ps"], 2)
                nc.vector.tensor_copy(lt_s[:, TT - 1:LINE], ps[0:H, 0, TT - 1:LINE]).then_inc(S["lines_sb"], 1)
                nc.vector.tensor_copy(ln_s[:, 0:N], ps[0:H, 1, 0:N]).then_inc(S["lines_sb"], 1)
                dve.wait_ge(S["w_loaded"], 80)
                nc.vector.tensor_reduce(wam[:, 0:1], cw_n[:].rearrange("p a b -> p (a b)"), X, ALU.max,
                                        apply_absolute_value=True).then_inc(S["wamax"], 1)
                for i in range(4):
                    nc.vector.tensor_reduce(wam[:, 1 + i:2 + i], sq_n[:, i].rearrange("p a b -> p (a b)"), X,
                                            ALU.max, apply_absolute_value=True).then_inc(S["wamax"], 1)
                for t in kS:
                    nc.vector.memset(t[32:64].rearrange("p h n -> p (h n)").bitcast(F32), TWO_ONES
                                     ).then_inc(S["dve_init"], 1)
                for t in va:
                    nc.vector.memset(t[:, :, :, DH:32], 1.0).then_inc(S["dve_init"], 1)
                for t in (qh, ql, kh, kl):
                    nc.vector.memset(t[:, :, N:NP], 0.0).then_inc(S["dve_init"], 1)
                nc.vector.memset(mneg[:, N:NP], 0.0).then_inc(S["dve_init"], 1)
                dve.wait_ge(S["ident"], 2)
                nc.vector.tensor_copy(identb[:], identf[:]).then_inc(S["dve_init"], 1)
                dve.wait_ge(S["anti_r"], 2)
                nc.vector.tensor_copy(antib[:], anti[:]).then_inc(S["antib_r"], 1)
                power(dve, slice(0, 5), 1)
                dve.wait_ge(S["winv_s"], 1)
                nc.vector.tensor_scalar(qks[:, 0:1], wscale[:, W_Q:W_Q + 1], DH ** -0.5, None, ALU.mult
                                        ).then_inc(S["dve_init"], 1)
                nc.vector.tensor_copy(qks[:, 1:2], wscale[:, W_K:W_K + 1]).then_inc(S["dve_init"], 1)
                for j, group in enumerate(banks):
                    hi, n = bank_dst(group, 0)
                    lo, _ = bank_dst(group, 1)
                    col = group[0][4]
                    dve.wait_ge(S["wT_hi"], j + 1)
                    nc.vector.scalar_tensor_tensor(lo, ps[:, 2 + j, 0:128 * n], winv[:, col:col + 1], hi,
                                                   ALU.mult, ALU.subtract).then_inc(S["wT_lo"], 1)
                for i, w in enumerate((wqT, wkT, wvT, woT)):
                    dve.wait_ge(S["wT_hi"], len(banks) + 4 * i + 4)
                    for km in range(2 * KT):
                        nc.vector.scalar_tensor_tensor(square(w, 1, km, i), heads(km, i), winv[:, 1 + i:2 + i],
                                                       square(w, 0, km, i), ALU.mult, ALU.subtract
                                                       ).then_inc(S["wT_lo"], 1)
                for i in range(H // 2):
                    dve.wait_ge(S["flipN_ps"], i + 1)
                    nc.vector.tensor_copy(biasN[0:TT, 2 * i:2 * i + 2].rearrange("p h n -> p (h n)"),
                                          ps[0:TT, i % 2, 0:2 * N]).then_inc(S["biasN_r"], 1)

            @block.scalar
            def _(act):
                act.dma_start(var[:], rvar.rearrange("(p k) -> p k", p=128)).then_inc(S["var_in"], 16)
                for i, v in enumerate(vec_dram):
                    dst = bc[:, i, :] if i < 4 else vec[:, i - 4, :]
                    act.dma_start(dst, bcast(v)).then_inc(S["vec_in"], 16)
                act.wait_ge(S["vec_ready"], 2)
                act.dma_start(rstd_line.ap().rearrange("(p k) -> p k", p=128), var[:]).then_inc(S["rstd_out"], 16)
                act.wait_ge(S["rstd_out"], 16)
                act.dma_start(vec[:, 1, :], bcast(rstd_line.ap())).then_inc(S["vec_in"], 16)
                act.wait_ge(S["winv_s"], 1)
                for j, group in enumerate(banks):
                    hi, n = bank_dst(group, 0)
                    col = group[0][4]
                    act.wait_ge(S["wT_ps"], j + 1)
                    nc.scalar.activation(hi, ps[:, 2 + j, 0:128 * n], ACT.Copy, scale=winv[:, col:col + 1]
                                         ).then_inc(S["wT_hi"], 1)
                for i, w in enumerate((wqT, wkT, wvT, woT)):
                    for km in range(2 * KT):
                        nc.scalar.activation(square(w, 0, km, i), heads(km, i), ACT.Copy,
                                             scale=winv[:, 1 + i:2 + i]).then_inc(S["wT_hi"], 1)
                for i in range(H // 2):
                    act.wait_ge(S["flipT_ps"], i + 1)
                    nc.scalar.activation(biasT[0:TT, 2 * i:2 * i + 2].rearrange("p h n -> p (h n)"),
                                         ps[0:TT, 6 + i % 2, 0:2 * N], ACT.Copy).then_inc(S["biasT_r"], 1)

            @block.tensor
            def _(pe):
                pe.wait_ge(S["consts"], 32)
                for i in range(2):
                    nc.tensor.matmul(ps[0:H, i, 0:LINE], rel_s[:], hot_s[:, i * LINE:(i + 1) * LINE],
                                     start=True, stop=True).then_inc(S["lines_ps"], 1)
                pe.wait_ge(S["ident"], 2)
                pe.wait_ge(S["w_loaded"], 80)
                for j, group in enumerate(banks):
                    for n, g in enumerate(group):
                        last = nc.tensor.transpose(ps[:, 2 + j, n * 128:(n + 1) * 128], g[0], identf[:])
                    last.then_inc(S["wT_ps"], 1)
                pe.wait_ge(S["bias_in"], 32)
                pe.wait_ge(S["antib_r"], 1)
                pe.wait_ge(S["lines_sb"], 4)
                for i in range(H // 2):
                    pair = slice(2 * i, 2 * i + 2)
                    if i >= 2:
                        pe.wait_ge(S["biasT_r"], i - 1)
                        pe.wait_ge(S["biasN_r"], i - 1)
                    nc.tensor.matmul(ps[0:TT, 6 + i % 2, 0:2 * N], anti[0:TT], flipT[0:TT, pair], start=True, stop=True
                                     ).then_inc(S["flipT_ps"], 1)
                    nc.tensor.matmul(ps[0:TT, i % 2, 0:2 * N], antib[0:TT], flipN[0:TT, pair], start=True, stop=True
                                     ).then_inc(S["flipN_ps"], 1)
        pw.close()

        xin = sba("xin", [128, 2, D])
        xh, xl = sba("xh", [128, T], F16), sba("xl", [128, T], F16)
        u = sba("u", [128, 2, C])
        r1 = sba("r1", [128, 2, C])
        v1 = sba("v1", [128, 2, C])
        h = sba("h", [128, 2, C])
        hall = sba("hall", [128, B, 2 * C])
        bns, bns2 = sba("bns", [128, 2, 6]), sba("bns2", [128, 2, 6])
        mv, mv2 = sba("mv", [128, 2, 2]), sba("mv2", [128, 2, 2])
        ve, ve2 = sba("ve", [128, 2]), sba("ve2", [128, 2])
        rstd, rstd2 = sba("rstd", [128, 2]), sba("rstd2", [128, 2])
        nb, nb2 = sba("nb", [128, 2]), sba("nb2", [128, 2])
        xn, xn2 = sba("xn", [128, 2, C]), sba("xn2", [128, 2, C])
        xnh, xnl = sba("xnh", [128, KT, N], F16), sba("xnl", [128, KT, N], F16)
        mx = sba("mx", [128, 2, H])
        sbr = sba("sbr", [128, 4, 2 * N])
        pt = sba("pt", [128, 2, 3, 2 * N])
        osb = sba("osb", [128, G, N])
        rc = sba("rc", [128, 2, H])
        on = sba("on", [128, 2, C])
        onh, onl = sba("onh", [128, KT, N], F16), sba("onl", [128, KT, N], F16)

        OB, MB = 4, 6

        def pieces(kind, off, first, end):
            return [(kind, off, n) for n in range(first, end)]

        P2, P1 = pieces("P2", 0, 0, 12), pieces("P1", 1, 0, 12)
        PE_ORDER = [P2[0], ("k", 1, 0), ("k", 1, 1), P2[1], ("conv", 2, 0), ("PV", -1, 3), P2[2], P2[3],
                    ("conv", 2, 1), P2[4], ("conv", 2, 2), P2[5], ("OT0", -1, 0), ("conv", 2, 3), ("conv", 2, 4),
                    ("PV", 0, 0), P1[0], ("OT1", -1, 0), P1[1], ("conv", 2, 5), P1[2], P1[3],
                    ("onT", -1, 0), P1[4], ("v", 1, 0), P1[5], P1[6], ("wo", -1, 0), P1[7],
                    ("wo", -1, 1), P1[8], ("v", 1, 1), P1[9], P1[10], ("xT", 3, 0), P1[11], ("PV", 0, 1), ("xnT", 2, 0),
                    P2[6], P2[7], P2[8], ("mT", 1, 0), ("q", 2, 0), P2[9], ("x2T", -1, 0), P2[10], ("q", 2, 1),
                    P2[11], ("PV", 0, 2)]
        DVE_ORDER = [P2[0], P2[1], ("kl", 1), P2[2], P2[3], P2[4], P2[5], ("on", -1, 0), P1[0], ("on", -1, 1),
                     P1[1], ("u", 2), P1[2], P1[3], P1[4], ("onl", -1), P1[5], P1[6],
                     ("stats", 2), P1[7], ("h2", -1), P1[8], P1[9], ("stats2", -1), P1[10], ("xl", 3), P1[11],
                     ("xnl", 2), P2[6], P2[7], P2[8], P2[9], P2[10], ("ax", -1), ("ql", 2), P2[11]]
        ACT_ORDER = [P2[0], ("kh", 1), P2[1], ("osb", -1, 3), P2[2], P2[3], P2[4], P2[5], ("osb", 0, 0),
                     ("relu", 2), ("onh", -1), ("xn", 2), ("va", 1), ("xh", 3), ("xnh", 2), ("osb", 0, 1), ("xn2", -1),
                     P2[6], ("mneg", 1), P2[7], P2[8], ("x2", -1), P2[9], ("qh", 2), P2[10], ("osb", 0, 2), P2[11]]
        FF_BANKS = len(ff_banks)
        FF_DVE = {(-2, ("u", 2)): [("ffabs", 0)], (-2, ("stats", 2)): [("ffdq", 0, 0)],
                  (-2, ("xnl", 2)): [("ffdq", 0, 1)], (-1, ("kl", 1)): [("ffdq", 0, 2), ("ffpow", 0)]}
        FF_ACT = {(-1, ("relu", 2)): [("ffhi", 0, j) for j in range(6)],
                  (-1, ("xn", 2)): [("ffhi", 0, j) for j in range(6, FF_BANKS - 1)],
                  (-1, ("va", 1)): [("ffhi", 0, FF_BANKS - 1)]}
        FF_PE = {(-1, P1[2]): [("ffT", 0, 0), ("ffT", 0, 1)]}
        for j in range(FF_BANKS):
            FF_DVE[-1, P1[j + 2]] = [("fflo", 0, j)]
            if j >= 2:
                FF_PE[-1, P1[j + 2]] = [("ffT", 0, j)]

        def step_order(order, ff, b):
            if not isinstance(b, int):
                return order
            todo = []
            for st in order:
                if runs(b, st[1]):
                    todo += [st] + ff.get((b, st), [])
            return todo

        MISC = [[("conv", "u_r", 1, 1, 2), ("v", "va_r", 1, 1, 1), ("xnT", "xnl_r", 1, 1, 2),
                 ("q", "ql_r", 1, 1, 2)],
                [("k", "kl_r", 1, 1, 1), ("OT0", "on_r", 2, 1, -1), ("OT1", "on_r", 2, 2, -1),
                 ("onT", "onl_r", 1, 1, -1), ("wo", "h2_r", 1, 1, -1), ("xT", "xl_r", 1, 1, 3),
                 ("mT", "mneg_r", 1, 1, 1), ("x2T", "x2_r", 1, 1, -1)]]
        misc_at = {m[0]: (r, i) for r, ring in enumerate(MISC) for i, m in enumerate(ring)}
        misc_bank = {name: MB + r for name, (r, i) in misc_at.items()}
        PIECES = [st for st in PE_ORDER if st[0] in ("P1", "P2")]
        score_bank = {(kind, n): i % 4 for i, (kind, off, n) in enumerate(PIECES)}

        def runs(b, off):
            return not isinstance(b, int) or 0 <= b + off < B

        def misc_free(pe, stage, b):
            r, i = misc_at[stage]
            i -= 1
            for back in range(5):
                while i >= 0:
                    _, name, per, n, off = MISC[r][i]
                    if runs(b - back if isinstance(b, int) else b, off):
                        return wait(pe, name, per * (b - back + off) + n)
                    i -= 1
                i += len(MISC[r])

        def score_free(pe, st, b):
            i = PIECES.index(st) - 4
            for back in range(5):
                while i >= 0:
                    kind, off, n = PIECES[i]
                    if runs(b - back if isinstance(b, int) else b, off):
                        return wait(pe, "sb_r" if kind == "P2" else "mx_r", 12 * (b - back + off) + n + 1)
                    i -= 4
                i += len(PIECES)

        def piece_heads(n):
            g, j = n // 3, n % 3
            if j == 2:
                return range(4 * g, 4 * g + 4), TT
            return range(4 * g + 2 * j, 4 * g + 2 * j + 2), N

        def three(out_ap, pairs):
            todo = []
            for (ah, al), (bh, bl) in pairs:
                todo += [(ah, bh), (al, bh), (ah, bl)]
            for i, (a, w) in enumerate(todo):
                last = nc.tensor.matmul(out_ap, a, w, start=(i == 0), stop=(i == len(todo) - 1))
            return last

        def pe_step(pe, b, par):
            odd = 1 - par
            for st in step_order(PE_ORDER, FF_PE, b):
                name, off, part = st
                c = b + off
                if name in misc_at:
                    bank = ps[:, misc_bank[name], :]
                if name == "ffT":
                    wait(pe, "wdq_w", part // (FF_BANKS // 3) + 1)
                    wait(pe, "ff_lo", part - 1)
                    for n, g in enumerate(ff_banks[part]):
                        last = nc.tensor.transpose(ps[:, OB + part % 2, n * 128:(n + 1) * 128], g[0], identf[:])
                    last.then_inc(S["ffT_ps"], 1)
                elif name == "xT":
                    wait(pe, "x_in", 16 * (c + 1))
                    misc_free(pe, name, b)
                    nc.tensor.transpose(bank[:, 0:128], xin[:, 0], identf[:])
                    nc.tensor.transpose(bank[:, 128:256], xin[:, 1], identf[:]).then_inc(S["xT_ps"], 1)
                elif name == "conv":
                    if part == 0:
                        wait(pe, "xh_r", c + 1)
                        wait(pe, "xl_r", c + 1)
                        misc_free(pe, name, b)
                    t = part // 3
                    products = []
                    for i in range(CTX):
                        rows = slice(t * TT + i, t * TT + i + TT)
                        products += [(xh[:, rows], wcT[:, 0, i, :]), (xl[:, rows], wcT[:, 0, i, :]),
                                     (xh[:, rows], wcT[:, 1, i, :])]
                    for i in range(part % 3 * 5, part % 3 * 5 + 5):
                        last = nc.tensor.matmul(bank[0:TT, t * C:(t + 1) * C], *products[i], start=(i == 0),
                                                stop=(i == 14))
                    if part == 5:
                        last.then_inc(S["conv_ps"], 1)
                elif name == "xnT":
                    wait(pe, "xn_r", 2 * (c + 1))
                    misc_free(pe, name, b)
                    for k in range(KT):
                        for t in range(2):
                            last = nc.tensor.transpose(bank[:, k * N + t * TT:k * N + (t + 1) * TT],
                                                       xn[0:TT, t, k * 128:(k + 1) * 128], identf[0:TT, 0:TT])
                    last.then_inc(S["xnT_ps"], 1)
                elif name in ("q", "k"):
                    w = wqT if name == "q" else wkT
                    if part == 0:
                        wait(pe, "xnh_r", c + 1)
                        wait(pe, "xnl_r", c + 1)
                        misc_free(pe, name, b)
                    cols = slice(part * 128, (part + 1) * 128)
                    todo = [(w[:, 0, k, cols], xnh[:, k]) for k in range(KT)]
                    todo += [(w[:, 0, k, cols], xnl[:, k]) for k in range(KT)]
                    todo += [(w[:, 1, k, cols], xnh[:, k]) for k in range(KT)]
                    for i, (a, v) in enumerate(todo):
                        last = nc.tensor.matmul(bank[:, part * N:(part + 1) * N], a, v, start=(i == 0),
                                                stop=(i == 5))
                    if part == 1:
                        last.then_inc(S[name + "_ps"], 1)
                elif name == "v":
                    if part == 0:
                        misc_free(pe, name, b)
                    rows = slice(part * TT, (part + 1) * TT)
                    last = three(bank[0:TT, part * C:(part + 1) * C],
                                 [((xnh[:, k, rows], xnl[:, k, rows]), (wvT[:, 0, k], wvT[:, 1, k]))
                                  for k in range(KT)])
                    if part == 1:
                        last.then_inc(S["v_ps"], 1)
                elif name == "P1":
                    if part == 0:
                        wait(pe, "stack_in", 96 * (c + 1))
                    score_free(pe, st, b)
                    heads, w = piece_heads(part)
                    qt = slice(0, TT) if w == TT else slice(TT, N)
                    dst = ps[0:TT, score_bank[name, part], 0:2 * N]
                    nc.tensor.matmul(dst, identb[0:TT, 0:TT], biasN[0:TT, heads[0]:heads[-1] + 1, N - w:N],
                                     start=True, stop=True)
                    for n, hd in enumerate(heads):
                        last = nc.tensor.matmul(dst[:, n * w:(n + 1) * w], qS[odd][0:48, hd, qt],
                                                kS[odd][0:48, hd, 0:w], start=False, stop=True,
                                                skip_group_check=True)
                    last.then_inc(S["p1_ps"], 1)
                elif name == "mT":
                    wait(pe, "mx_r", 12 * (c + 1))
                    misc_free(pe, name, b)
                    for t in range(2):
                        last = nc.tensor.matmul(bank[0:H, t * TT:(t + 1) * TT], mx[0:TT, t, :], identf[0:TT, 0:TT],
                                                start=True, stop=True)
                    last.then_inc(S["mT_ps"], 1)
                elif name == "P2":
                    if part == 0:
                        wait(pe, "mneg_in", 16 * (c + 1))
                    score_free(pe, st, b)
                    heads, w = piece_heads(part)
                    kt = slice(TT, N) if w == TT else slice(0, TT)
                    for n, hd in enumerate(heads):
                        last = nc.tensor.matmul(ps[0:TT, score_bank[name, part], n * w:(n + 1) * w],
                                                kS[par][0:49, hd, kt], qS[par][0:49, hd, N - w:N],
                                                start=True, stop=True)
                    last.then_inc(S["p2_ps"], 1)
                elif name == "PV":
                    g, vc = part, va[odd if off else par]
                    if isinstance(c, int) and c == 0:
                        wait(pe, "ff_lo", FF_BANKS)
                    wait(pe, "exp_r", 12 * c + 3 * (g + 1))
                    wait(pe, "va_r", c + 1)
                    wait(pe, "osb_r", 4 * c + g - 1)
                    p = pt[0:TT, g % 2]
                    for i in range(4):
                        nc.tensor.matmul(ps[32 * i:32 * i + 32, OB + g % 2, 0:N], vc[0:TT, 0, 4 * g + i, :],
                                         p[:, i // 2, (i % 2) * N:(i % 2) * N + N], start=True, stop=True,
                                         skip_group_check=True)
                    for i in range(4):
                        last = nc.tensor.matmul(ps[32 * i:32 * i + 32, OB + g % 2, TT:N],
                                                vc[0:TT, 1, 4 * g + i, :], p[:, 2, i * TT:(i + 1) * TT],
                                                start=False, stop=True, skip_group_check=True)
                    last.then_inc(S["pv_ps"], 1)
                elif name in ("OT0", "OT1"):
                    t = int(name[2])
                    wait(pe, "osb_r", 4 * (c + 1))
                    misc_free(pe, name, b)
                    for g in range(G):
                        last = nc.tensor.transpose(bank[0:TT, g * 128:(g + 1) * 128],
                                                   osb[:, g, t * TT:(t + 1) * TT], identf[:])
                    last.then_inc(S["oT_ps"], 1)
                elif name == "onT":
                    wait(pe, "on_r", 2 * (c + 1))
                    misc_free(pe, name, b)
                    for k in range(KT):
                        for t in range(2):
                            last = nc.tensor.transpose(bank[:, k * N + t * TT:k * N + (t + 1) * TT],
                                                       on[0:TT, t, k * 128:(k + 1) * 128], identf[0:TT, 0:TT])
                    last.then_inc(S["onT_ps"], 1)
                elif name == "wo":
                    if part == 0:
                        wait(pe, "onh_r", c + 1)
                        wait(pe, "onl_r", c + 1)
                        misc_free(pe, name, b)
                    rows = slice(part * TT, (part + 1) * TT)
                    last = three(bank[0:TT, part * C:(part + 1) * C],
                                 [((onh[:, k, rows], onl[:, k, rows]), (woT[:, 0, k], woT[:, 1, k]))
                                  for k in range(KT)])
                    if part == 1:
                        last.then_inc(S["wo_ps"], 1)
                elif name == "x2T":
                    wait(pe, "xn2_r", 2 * (c + 1))
                    misc_free(pe, name, b)
                    for k in range(KT):
                        for t in range(2):
                            last = nc.tensor.transpose(bank[:, k * N + t * TT:k * N + (t + 1) * TT],
                                                       xn2[0:TT, t, k * 128:(k + 1) * 128], identf[0:TT, 0:TT])
                    last.then_inc(S["x2T_ps"], 1)

        def misc(stage):
            return ps[:, misc_bank[stage], :]

        def whole(ap):
            return ap[:].rearrange("p k n -> p (k n)")

        def hall_of(c):
            return hall[0:TT, c, :] if isinstance(c, int) else hall[0:TT, bass.ds(c, 1), :].rearrange("p a n -> p (a n)")

        def x2t_of(c):
            return x2t[:, c] if isinstance(c, int) else x2t[:, bass.ds(c, 1)].rearrange("p a k n -> p (a k) n")

        def dve_step(dve, b, par):
            for st in step_order(DVE_ORDER, FF_DVE, b):
                name, off = st[0], st[1]
                c = b + off
                if name == "ffabs":
                    dve.wait_ge(S["ff_in"], 48)
                    for i in range(3):
                        nc.vector.tensor_reduce(ff_s[:, i], ff_n[:, i].rearrange("p (a b) -> p a b", b=BLOCK), X,
                                                ALU.max, apply_absolute_value=True).then_inc(S["wabs"], 1)
                    for i in range(3):
                        dve.wait_ge(S["wabs"], i + 1)
                        nc.vector.tensor_reduce(wam[:, 5 + i:6 + i], ff_s[:, i], X, ALU.max
                                                ).then_inc(S["wamax"], 1)
                    dve.wait_ge(S["wamax"], 8)
                    nc.vector.tensor_scalar(ff_s, ff_s, 1.0 / WQMAX, FLOOR, ALU.mult, ALU.max
                                            ).then_inc(S["wdq_s"], 1)
                    dve.wait_ge(S["wdq_s"], 1)
                    nc.vector.reciprocal(ff_r, ff_s).then_inc(S["wdq_s"], 1)
                elif name == "ffdq":
                    i = st[2]
                    v = ff_n[:, i].rearrange("p (a b) -> p a b", b=BLOCK)
                    vi = ff_i[:, i].rearrange("p (a b) -> p a b", b=BLOCK)
                    dve.wait_ge(S["wdq_s"], 2)
                    nc.vector.tensor_tensor(vi, v, ff_r[:, i].unsqueeze(2).broadcast_to([128, NB, BLOCK]), ALU.mult
                                            ).then_inc(S["wdq_i"], 1)
                    dve.wait_ge(S["wdq_i"], i + 1)
                    nc.vector.tensor_tensor(v, vi, ff_s[:, i].unsqueeze(2).broadcast_to([128, NB, BLOCK]), ALU.mult
                                            ).then_inc(S["wdq_w"], 1)
                elif name == "ffpow":
                    power(dve, slice(5, 8), 2)
                elif name == "fflo":
                    group = ff_banks[st[2]]
                    dve.wait_ge(S["ff_hi"], st[2] + 1)
                    nc.vector.scalar_tensor_tensor(bank_dst(group, 1)[0], ps[:, OB + st[2] % 2, :],
                                                   winv[:, group[0][4]:group[0][4] + 1], bank_dst(group, 0)[0],
                                                   ALU.mult, ALU.subtract).then_inc(S["ff_lo"], 1)
                elif name == "P2":
                    n = st[2]
                    heads, w = piece_heads(n)
                    wait(dve, "p2_ps", 12 * c + n + 1)
                    wait(dve, "exp_r", 12 * c + n - 3)
                    nc.vector.tensor_tensor(sbr[0:TT, n % 4].rearrange("p (h w) -> p h w", w=w),
                                            ps[0:TT, score_bank[name, n], 0:2 * N].rearrange("p (h w) -> p h w", w=w),
                                            biasT[0:TT, heads[0]:heads[-1] + 1, 0:w], ALU.add).then_inc(S["sb_r"], 1)
                elif name == "P1":
                    n = st[2]
                    heads, w = piece_heads(n)
                    wait(dve, "p1_ps", 12 * c + n + 1)
                    if n == 0:
                        wait(dve, "mT_ps", c)
                    nc.vector.tensor_reduce(mx[0:TT, 0 if w == TT else 1, heads[0]:heads[-1] + 1],
                                            ps[0:TT, score_bank[name, n], 0:2 * N].rearrange("p (h w) -> p h w", w=w),
                                            X, ALU.max).then_inc(S["mx_r"], 1)
                elif name == "xl":
                    wait(dve, "xh_r", c + 1)
                    wait(dve, "conv_ps", c)
                    nc.vector.tensor_tensor(xl[:], misc("xT")[:, 0:T], xh[:], ALU.subtract).then_inc(S["xl_r"], 1)
                elif name == "u":
                    wait(dve, "conv_ps", c + 1)
                    wait(dve, "relu_r", c)
                    nc.vector.scalar_tensor_tensor(
                        u[0:TT], misc("conv")[0:TT].rearrange("p (t c) -> p t c", t=2), wscale[0:TT, 0:1],
                        bc[0:TT, 0:1, :].broadcast_to([TT, 2, C]), ALU.mult, ALU.add).then_inc(S["u_r"], 1)
                elif name in ("stats", "stats2"):
                    if name == "stats":
                        src, m, s6, sfx, ready = h, mv, bns, "", "h_r"
                    else:
                        src, m, s6, sfx, ready = hall_of(c).rearrange("p (t c) -> p t c", t=2), mv2, bns2, "2", "h2_r"
                    unregistered(dve, c)
                    wait(dve, ready, c + 1)
                    wait(dve, f"nb{sfx}_r", c)
                    for t in range(2):
                        nc.vector.bn_stats(s6[0:TT, t], src[0:TT, t]).then_inc(S[f"bns{sfx}_r"], 1)
                    for t in range(2):
                        count = valued(dve, 2 * c + t + 1)
                        unregistered(dve, c)
                        wait(dve, f"bns{sfx}_r", count)
                        nc.vector.bn_aggr(m[0:TT, t], s6[0:TT, t]).then_inc(S[f"mv{sfx}_r"], 1)
                elif name == "xnl":
                    wait(dve, "xnh_r", c + 1)
                    wait(dve, "v_ps", c)
                    nc.vector.tensor_tensor(whole(xnl), misc("xnT")[:, 0:2 * N], whole(xnh), ALU.subtract
                                            ).then_inc(S["xnl_r"], 1)
                elif name in ("ql", "kl"):
                    hi, lo, col = (qh, ql, 0) if name == "ql" else (kh, kl, 1)
                    wait(dve, name[0] + "h_r", c + 1)
                    wait(dve, "stack_in", 96 * c)
                    nc.vector.scalar_tensor_tensor(
                        lo[:, :, 0:N], misc(name[0])[:, 0:2 * N].rearrange("p (m n) -> p m n", m=2),
                        qks[:, col:col + 1], hi[:, :, 0:N], ALU.mult, ALU.subtract).then_inc(S[name + "_r"], 1)
                elif name == "on":
                    t = st[2]
                    src = misc(f"OT{t}")[0:TT].rearrange("p (h e) -> p h e", e=32)
                    wait(dve, "oT_ps", 2 * c + t + 1)
                    wait(dve, "onT_ps", c)
                    nc.vector.reciprocal(rc[0:TT, t], src[:, :, DH]).then_inc(S["rc_r"], 1)
                    wait(dve, "rc_r", 2 * c + t + 1)
                    nc.vector.tensor_tensor(on[0:TT, t].rearrange("p (h e) -> p h e", e=DH), src[:, :, 0:DH],
                                            rc[0:TT, t].unsqueeze(2).broadcast_to([TT, H, DH]), ALU.mult
                                            ).then_inc(S["on_r"], 1)
                elif name == "onl":
                    wait(dve, "onh_r", c + 1)
                    wait(dve, "wo_ps", c)
                    nc.vector.tensor_tensor(whole(onl), misc("onT")[:, 0:2 * N], whole(onh), ALU.subtract
                                            ).then_inc(S["onl_r"], 1)
                elif name == "h2":
                    wait(dve, "wo_ps", c + 1)
                    wait(dve, "hb_r", c + 1)
                    nc.vector.scalar_tensor_tensor(hall_of(c), misc("wo")[0:TT], wscale[0:TT, W_O:W_O + 1], hall_of(c),
                                                   ALU.mult, ALU.add).then_inc(S["h2_r"], 1)
                elif name == "ax":
                    wait(dve, "x2_r", c + 1)
                    dst = amax_x[:, c:c + 1] if isinstance(c, int) else amax_x[:, bass.ds(c, 1)]
                    nc.vector.tensor_reduce(dst, x2t_of(c), mybir.AxisListType.XY, ALU.max, apply_absolute_value=True
                                            ).then_inc(S["ax_r"], 1)

        def act_step(act, b, par):
            odd = 1 - par
            for st in step_order(ACT_ORDER, FF_ACT, b):
                name, off = st[0], st[1]
                c = b + off
                if name == "ffhi":
                    group = ff_banks[st[2]]
                    act.wait_ge(S["winv_s"], 2)
                    act.wait_ge(S["ffT_ps"], st[2] + 1)
                    nc.scalar.activation(bank_dst(group, 0)[0], ps[:, OB + st[2] % 2, :], ACT.Copy,
                                         scale=winv[:, group[0][4]:group[0][4] + 1]).then_inc(S["ff_hi"], 1)
                elif name == "P2":
                    n = st[2]
                    wait(act, "sb_r", 12 * c + n + 1)
                    wait(act, "pv_ps", 4 * c + n // 3 - 1)
                    nc.scalar.activation(pt[0:TT, n // 3 % 2, n % 3], sbr[0:TT, n % 4], ACT.Exp
                                         ).then_inc(S["exp_r"], 1)
                elif name == "osb":
                    g = st[2]
                    wait(act, "pv_ps", 4 * c + g + 1)
                    if g == 0:
                        wait(act, "oT_ps", 2 * c)
                    nc.scalar.activation(osb[:, g], ps[:, OB + g % 2, 0:N], ACT.Copy).then_inc(S["osb_r"], 1)
                elif name == "xh":
                    wait(act, "xT_ps", c + 1)
                    wait(act, "conv_ps", c)
                    nc.scalar.activation(xh[:], misc("xT")[:, 0:T], ACT.Copy).then_inc(S["xh_r"], 1)
                elif name == "relu":
                    wait(act, "u_r", c + 1)
                    wait(act, "v1_r", c)
                    nc.scalar.activation(r1[0:TT], u[0:TT], ACT.Relu).then_inc(S["relu_r"], 1)
                elif name in ("xn", "xn2"):
                    if name == "xn":
                        src, dst, r, o, sfx, read = h, xn, rstd, nb, "", "xnT_ps"
                    else:
                        src, dst, r, o, sfx, read = (hall_of(c).rearrange("p (t c) -> p t c", t=2), xn2, rstd2, nb2, "2",
                                                     "x2T_ps")
                    wait(act, f"nb{sfx}_r", c + 1)
                    wait(act, read, c)
                    for t in range(2):
                        nc.scalar.activation(dst[0:TT, t], src[0:TT, t], ACT.Identity, bias=o[0:TT, t:t + 1],
                                             scale=r[0:TT, t:t + 1]).then_inc(S[f"xn{sfx}_r"], 1)
                elif name == "mneg":
                    wait(act, "mT_ps", c + 1)
                    wait(act, "mneg_in", 16 * c)
                    nc.scalar.activation(mneg[:, 0:N], misc("mT")[0:H, 0:N], ACT.Copy, scale=-1.0
                                         ).then_inc(S["mneg_r"], 1)
                elif name == "xnh":
                    wait(act, "xnT_ps", c + 1)
                    wait(act, "v_ps", c)
                    nc.scalar.activation(whole(xnh), misc("xnT")[:, 0:2 * N], ACT.Copy).then_inc(S["xnh_r"], 1)
                elif name in ("qh", "kh"):
                    hi, col = (qh, 0) if name == "qh" else (kh, 1)
                    wait(act, name[0] + "_ps", c + 1)
                    wait(act, "stack_in", 96 * c)
                    nc.scalar.activation(hi[:, :, 0:N], misc(name[0])[:, 0:2 * N].rearrange("p (m n) -> p m n", m=2),
                                         ACT.Copy, scale=qks[:, col:col + 1]).then_inc(S[name + "_r"], 1)
                elif name == "va":
                    wait(act, "v_ps", c + 1)
                    wait(act, "pv_ps", 4 * (c - 1))
                    nc.scalar.activation(va[odd][0:TT, :, :, 0:DH],
                                         misc("v")[0:TT].rearrange("p (t h e) -> p t h e", t=2, h=H), ACT.Copy,
                                         scale=wscale[0:TT, W_V:W_V + 1]).then_inc(S["va_r"], 1)
                elif name == "onh":
                    wait(act, "onT_ps", c + 1)
                    wait(act, "wo_ps", c)
                    nc.scalar.activation(whole(onh), misc("onT")[:, 0:2 * N], ACT.Copy).then_inc(S["onh_r"], 1)
                elif name == "x2":
                    wait(act, "x2T_ps", c + 1)
                    nc.scalar.activation(x2t_of(c), misc("x2T")[:, 0:2 * N].rearrange("p (k n) -> p k n", k=KT),
                                         ACT.Copy).then_inc(S["x2_r"], 1)

        def pool_norm(pool, c, m, v, r, o, sfx):
            wait(pool, f"mv{sfx}_r", 2 * (c + 1))
            wait(pool, f"xn{sfx}_r", 2 * c)
            nc.gpsimd.tensor_tensor(v[0:TT], m[0:TT, :, 1], epsc[0:TT], ALU.add).then_inc(S[f"ve{sfx}_r"], 1)
            nc.gpsimd.tensor_tensor(o[0:TT], m[0:TT, :, 0], minus[0:TT], ALU.mult).then_inc(S[f"nm{sfx}_r"], 1)
            wait(pool, f"ve{sfx}_r", c + 1)
            nc.gpsimd.tensor_tensor(r[0:TT], v[0:TT], nhalf[0:TT], ALU.pow).then_inc(S[f"rstd{sfx}_r"], 1)
            wait(pool, f"rstd{sfx}_r", c + 1)
            wait(pool, f"nm{sfx}_r", c + 1)
            nc.gpsimd.tensor_tensor(o[0:TT], o[0:TT], r[0:TT], ALU.mult).then_inc(S[f"nb{sfx}_r"], 1)

        def pool_step(pool, b, par):
            if runs(b, 2):
                c = b + 2
                wait(pool, "relu_r", c + 1)
                wait(pool, "h_r", c)
                nc.gpsimd.tensor_tensor(v1[0:TT], r1[0:TT], bc[0:TT, 1:2, :].broadcast_to([TT, 2, C]), ALU.mult
                                        ).then_inc(S["v1_r"], 1)
                wait(pool, "v1_r", c + 1)
                wait(pool, "xn_r", 2 * c)
                wait(pool, "hb_r", c)
                nc.gpsimd.tensor_tensor(h[0:TT], v1[0:TT], bc[0:TT, 2:3, :].broadcast_to([TT, 2, C]), ALU.add
                                        ).then_inc(S["h_r"], 1)
            if runs(b, 2):
                pool_norm(pool, c, mv, ve, rstd, nb, "")
                wait(pool, "h_r", c + 1)
                hc = hall_of(c).rearrange("p (t c) -> p t c", t=2)
                nc.gpsimd.tensor_tensor(hc, h[0:TT], bc[0:TT, 3:4, :].broadcast_to([TT, 2, C]), ALU.add
                                        ).then_inc(S["hb_r"], 1)
            if isinstance(b, int) and b == -2:
                wait(pool, "wamax", 8)
                nc.gpsimd.partition_all_reduce(wal[:, 5:8], wam[:, 5:8], 128, ABSMAX).then_inc(S["wall"], 1)
            if runs(b, -1):
                pool_norm(pool, b - 1, mv2, ve2, rstd2, nb2, "2")

        def load_x(sp, c):
            unregistered(sp, c)
            wait(sp, "xT_ps", c)
            src = x[c] if isinstance(c, int) else x[bass.ds(c, 1)].rearrange("a t d -> (a t) d")
            sp.dma_start(xin[:], src.rearrange("(a p) d -> p a d", p=128)).then_inc(S["x_in"], 16)

        def sp_step(sp, b, par):
            odd = 1 - par
            if runs(b, 1):
                c = b + 1
                for nm, dst, parts in (("q", qS[odd], ((qh, (0, 2)), (ql, (1,)))),
                                       ("k", kS[odd], ((kh, (0, 1)), (kl, (2,))))):
                    done = valued(sp, 12 * (c - 1))
                    for (src, rows), ready in zip(parts, ("h_r", "l_r")):
                        wait(sp, nm + ready, c + 1)
                        if ready == "h_r":
                            wait(sp, "p2_ps", done)
                        for i in rows:
                            sp.dma_start(dst[16 * i:16 * i + DH], src[:]).then_inc(S["stack_in"], 16)
            if runs(b, 3):
                load_x(sp, b + 3)
            if runs(b, -1):
                c = b - 1
                unregistered(sp, c)
                wait(sp, "h2_r", c + 1)
                if isinstance(c, int):
                    sp.dma_start(res.ap()[c], hall[0:TT, c, :]).then_inc(S["spilled"], 16)
                else:
                    sp.dma_start(res.ap()[bass.ds(c, 1)].rearrange("a p n -> (a p) n"),
                                 hall[0:TT, bass.ds(c, 1), :].rearrange("p a n -> p (a n)")).then_inc(S["spilled"], 16)
            if runs(b, 1):
                c = b + 1
                wait(sp, "mneg_r", c + 1)
                sp.dma_start(qS[odd][48:49], mneg[:]).then_inc(S["mneg_in"], 16)

        INIT = 2 + 2 + 4 + 1 + 1 + 2

        with nc.Block() as block:
            @block.tensor
            def _(pe):
                pe.wait_ge(S["dve_init"], INIT)
                for b in range(-3, 2):
                    pe_step(pe, b, b % 2)
                with pe.Fori(1, 6) as k:
                    for par in range(2):
                        pe_step(pe, 2 * k + par, par)
                for b in range(12, 17):
                    pe_step(pe, b, b % 2)

            @block.vector
            def _(dve):
                dve.wait_ge(S["dve_init"], INIT)
                for b in range(-3, 2):
                    dve_step(dve, b, b % 2)
                with dve.Fori(1, 6) as k:
                    for par in range(2):
                        dve_step(dve, 2 * k + par, par)
                for b in range(12, 17):
                    dve_step(dve, b, b % 2)

            @block.scalar
            def _(act):
                act.wait_ge(S["dve_init"], INIT)
                for b in range(-3, 2):
                    act_step(act, b, b % 2)
                with act.Fori(1, 6) as k:
                    for par in range(2):
                        act_step(act, 2 * k + par, par)
                for b in range(12, 17):
                    act_step(act, b, b % 2)

            @block.gpsimd
            def _(pool):
                for b in range(-3, 2):
                    pool_step(pool, b, b % 2)
                with pool.Fori(1, 6) as k:
                    for par in range(2):
                        pool_step(pool, 2 * k + par, par)
                for b in range(12, 17):
                    pool_step(pool, b, b % 2)

            @block.sync
            def _(sp):
                sp.wait_ge(S["dve_init"], INIT)
                sp_step(sp, -3, 1)
                for i, w in enumerate(ff_dram):
                    sp.dma_start(ff_view(i), w).then_inc(S["ff_in"], 16)
                for b in range(-2, 2):
                    sp_step(sp, b, b % 2)
                with sp.Fori(1, 6) as k:
                    for par in range(2):
                        sp_step(sp, 2 * k + par, par)
                for b in range(12, 17):
                    sp_step(sp, b, b % 2)
                sp.wait_ge(S["spilled"], 16 * B)
        pa.close()

        gat = sb("gat", [128, 2 * CH, UW])
        amax = sb("amax", [128, 4, 2 * CH])
        scalars = """ax pax ag pag au pau ap pap ao pao t least_g least_u least_p least_o
            step_x inv_x unit_g unit_u step_g inv_g size_g step_u inv_u size_u unit_p step_p inv_p size_p
            unit_o step_o inv_o size_o size_y""".split()
        sc = sb("sc", [128, len(scalars)])
        col = {n: sc[:, i:i + 1] for i, n in enumerate(scalars)}
        done = [0]

        def small(dve, ins):
            done[0] += 1
            ins.then_inc(S["sc_r"], 1)
            dve.wait_ge(S["sc_r"], done[0])

        def least(dve, unit, to):
            small(dve, nc.vector.reciprocal(col["t"], col[unit]))
            small(dve, nc.vector.tensor_scalar(col[to], col["t"], FLOOR, None, ALU.mult))

        def step_of(dve, name, least_step, s, inv):
            small(dve, nc.vector.tensor_scalar(col[s], col[name], 1.0 / QMAX, least_step, ALU.mult, ALU.max))
            small(dve, nc.vector.reciprocal(col[inv], col[s]))

        def times(dve, to, a, b):
            small(dve, nc.vector.tensor_tensor(col[to], col[a], b, ALU.mult))

        def over_partitions(pool, n, src, dst):
            pool.wait_ge(S["ared"], n)
            nc.gpsimd.partition_all_reduce(col[dst], col[src], 128, ABSMAX).then_inc(S["par"], 1)

        def unit(u):
            return gat[:, bass.ds(u, 1), :].rearrange("p a n -> p (a n)")

        def amax_at(i, u):
            return amax[:, i, bass.ds(u, 1)]

        XC = 2 * KT * N
        xf = x2t[:].rearrange("p b k n -> p (b k n)")
        xq = xf.bitcast(F16)

        def product(w, c, hf):
            for j in range(3):
                m = slice((3 * hf + j) * 128, (3 * hf + j + 1) * 128)
                i = 0
                for wp, xp in ((0, 0), (0, 1), (1, 0)):
                    for k in range(KT):
                        rhs = xq[:, bass.ds(c * 2 * XC + xp * XC + k * 2 * N, 2 * N)]
                        last = nc.tensor.matmul(ps[:, 3 * hf + j, 0:2 * N], w[:, wp, k, m], rhs,
                                                start=(i == 0), stop=(i == 5))
                        i += 1
            return last

        def banks_of(hf):
            return ps[:, 3 * hf:3 * hf + 3, 0:2 * N]

        def three_rows(ap):
            return ap.rearrange("p (j n) -> p j n", j=3)

        pf = ctx.enter_context(ExitStack())
        raw = [sb(f"raw{i}", [128, UW], F32, pf) for i in range(2)]
        gq = [sb(f"gq{i}", [128, UW], I16, pf) for i in range(2)]
        sig = [sb(f"sig{i}", [128, UW], F32, pf) for i in range(2)]
        sq = [sb(f"sq{i}", [128, UW], I32, pf) for i in range(2)]
        g2 = [sb(f"g2{i}", [128, UW], I16, pf) for i in range(2)]
        xi = sb("xi", [128, XC], I16, pf)

        def turn(i):
            return CH - 1 if isinstance(i, int) else i - 1

        scalars_at = {}

        with nc.Block() as block:
            @block.vector
            def _(dve):
                nc.vector.tensor_reduce(col["ax"], amax_x[:], X, ALU.max).then_inc(S["ared"], 1)
                wait(dve, "par", 1)
                step_of(dve, "pax", FLOOR, "step_x", "inv_x")

                def integers(c):
                    wait(dve, "xq_r", c)
                    nc.vector.tensor_scalar(xi[:].rearrange("p (k b n) -> p k b n", k=KT, b=2),
                                            x2t[:, bass.ds(2 * c, 2)].rearrange("p b k n -> p k b n"),
                                            col["inv_x"], None, ALU.mult).then_inc(S["xi_r"], 1)
                    wait(dve, "xqh_r", c + 1)
                    nc.vector.tensor_tensor(xq[:, bass.ds(c * 2 * XC + XC, XC)], xi[:],
                                            xq[:, bass.ds(c * 2 * XC, XC)], ALU.subtract).then_inc(S["xq_r"], 1)

                def largest(c):
                    for hf in range(2):
                        wait(dve, f"g_r{hf}", c + 1)
                        nc.vector.tensor_reduce(amax_at(0, 2 * c + hf), unit(2 * c + hf), X, ALU.max,
                                                apply_absolute_value=True).then_inc(S["ag_r"], 1)

                integers(0)
                times(dve, "unit_g", "step_x", wscale[:, W_GATE:W_GATE + 1])
                times(dve, "unit_u", "step_x", wscale[:, W_UP:W_UP + 1])
                least(dve, "unit_g", "least_g")
                least(dve, "unit_u", "least_u")
                def body(c):
                    integers(c + 1)
                    largest(c)

                from_zero(dve, CH - 1, body)
                largest(CH - 1)
                wait(dve, "ag_r", 2 * CH)
                nc.vector.tensor_reduce(col["ag"], amax[:, 0], X, ALU.max).then_inc(S["ared"], 1)
                wait(dve, "par", 2)
                step_of(dve, "pag", col["least_g"], "step_g", "inv_g")
                times(dve, "size_g", "step_g", col["unit_g"])
                scalars_at[2] = done[0]
                small(dve, nc.vector.tensor_scalar(col["unit_p"], col["size_g"], 1.0 / 65536, None, ALU.mult))
                least(dve, "unit_p", "least_p")

                def body(c):
                    for hf in range(2):
                        wait(dve, f"raw_r{hf}", c + 1)
                        nc.vector.tensor_reduce(amax_at(1, 2 * c + hf), raw[hf][:], X, ALU.max,
                                                apply_absolute_value=True).then_inc(S[f"au_r{hf}"], 1)
                        wait(dve, f"sq_r{hf}", c + 1)
                        wait(dve, f"gq_r{hf}", c + 1)
                        nc.vector.scalar_tensor_tensor(unit(2 * c + hf), sq[hf][:], 65535.0, gq[hf][:], ALU.min,
                                                       ALU.mult).then_inc(S[f"p_r{hf}"], 1)
                        wait(dve, f"p_r{hf}", c + 1)
                        nc.vector.tensor_reduce(amax_at(2, 2 * c + hf), unit(2 * c + hf), X, ALU.max,
                                                apply_absolute_value=True).then_inc(S["ap_r"], 1)

                from_zero(dve, CH, body)
                for hf in range(2):
                    wait(dve, f"au_r{hf}", CH)
                wait(dve, "ap_r", 2 * CH)
                nc.vector.tensor_reduce(col["au"], amax[:, 1], X, ALU.max).then_inc(S["ared"], 1)
                nc.vector.tensor_reduce(col["ap"], amax[:, 2], X, ALU.max).then_inc(S["ared"], 1)
                wait(dve, "par", 4)
                step_of(dve, "pau", col["least_u"], "step_u", "inv_u")
                step_of(dve, "pap", col["least_p"], "step_p", "inv_p")
                scalars_at[3] = done[0]
                times(dve, "size_u", "step_u", col["unit_u"])
                times(dve, "size_p", "step_p", col["unit_p"])
                times(dve, "unit_o", "size_u", col["size_p"])
                least(dve, "unit_o", "least_o")

                def body(i):
                    for hf in range(2):
                        wait(dve, f"uq_r{hf}", i + 1)
                        wait(dve, f"g2_r{hf}", i + 1)
                        nc.vector.tensor_tensor(unit(2 * turn(i) + hf), g2[hf][:], gq[hf][:], ALU.mult
                                                ).then_inc(S[f"o_r{hf}"], 1)
                    for hf in range(2):
                        wait(dve, f"o_r{hf}", i + 1)
                        nc.vector.tensor_reduce(amax_at(3, 2 * turn(i) + hf), unit(2 * turn(i) + hf), X, ALU.max,
                                                apply_absolute_value=True).then_inc(S["ao_r"], 1)

                from_zero(dve, CH, body)
                wait(dve, "ao_r", 2 * CH)
                nc.vector.tensor_reduce(col["ao"], amax[:, 3], X, ALU.max).then_inc(S["ared"], 1)
                wait(dve, "par", 5)
                step_of(dve, "pao", col["least_o"], "step_o", "inv_o")

            @block.tensor
            def _(pe):
                def body(c):
                    for hf in range(2):
                        wait(pe, "xq_r", c + 1)
                        wait(pe, f"g_r{hf}", c)
                        product(wgT, c, hf).then_inc(S[f"g_ps{hf}"], 1)

                from_zero(pe, CH, body)
                for hf in range(2):
                    wait(pe, f"g_r{hf}", CH)
                    product(wuT, 0, hf).then_inc(S[f"u_ps{hf}"], 1)

                def body(c):
                    for hf in range(2):
                        wait(pe, f"raw_r{hf}", c)
                        product(wuT, c, hf).then_inc(S[f"u_ps{hf}"], 1)

                with pe.Fori(1, CH) as c:
                    body(c)

            @block.scalar
            def _(act):
                def high(c):
                    wait(act, "xi_r", c + 1)
                    nc.scalar.activation(xq[:, bass.ds(c * 2 * XC, XC)], xi[:], ACT.Copy).then_inc(S["xqh_r"], 1)

                def keep(c):
                    for hf in range(2):
                        wait(act, f"g_ps{hf}", c + 1)
                        nc.scalar.activation(three_rows(unit(2 * c + hf)), banks_of(hf), ACT.Copy
                                             ).then_inc(S[f"g_r{hf}"], 1)

                high(0)
                def body(c):
                    high(c + 1)
                    keep(c)

                from_zero(act, CH - 1, body)
                keep(CH - 1)

                def body(c):
                    for hf in range(2):
                        wait(act, f"u_ps{hf}", c + 1)
                        wait(act, f"au_r{hf}", c)
                        wait(act, f"raw_out{hf}", 16 * c)
                        nc.scalar.activation(three_rows(raw[hf][:]), banks_of(hf), ACT.Copy
                                             ).then_inc(S[f"raw_r{hf}"], 1)
                        if isinstance(c, int) and hf == 0:
                            wait(act, "sc_r", scalars_at[2])
                        wait(act, f"p_r{hf}", c)
                        nc.scalar.activation(gq[hf][:], unit(2 * c + hf), ACT.Copy, scale=col["inv_g"]
                                             ).then_inc(S[f"gq_r{hf}"], 1)
                        wait(act, f"gq_r{hf}", c + 1)
                        wait(act, f"sq_r{hf}", c)
                        nc.scalar.activation(sig[hf][:], gq[hf][:], ACT.Sigmoid, scale=col["size_g"]
                                             ).then_inc(S[f"sig_r{hf}"], 1)

                from_zero(act, CH, body)

                def body(i):
                    for hf in range(2):
                        if isinstance(i, int) and hf == 0:
                            wait(act, "sc_r", scalars_at[3])
                        wait(act, f"o_r{hf}", i)
                        nc.scalar.activation(g2[hf][:], unit(2 * turn(i) + hf), ACT.Copy, scale=col["inv_p"]
                                             ).then_inc(S[f"g2_r{hf}"], 1)

                from_zero(act, CH, body)

            @block.gpsimd
            def _(pool):
                over_partitions(pool, 1, "ax", "pax")
                over_partitions(pool, 2, "ag", "pag")

                def body(c):
                    for hf in range(2):
                        count = valued(pool, c + 1)
                        unregistered(pool, c)
                        wait(pool, f"sig_r{hf}", count)
                        wait(pool, f"p_r{hf}", c)
                        nc.gpsimd.tensor_scalar(sq[hf][:], sig[hf][:], 65536.0, 0.0, ALU.mult, ALU.add
                                                ).then_inc(S[f"sq_r{hf}"], 1)

                from_zero(pool, CH, body)
                over_partitions(pool, 3, "au", "pau")
                over_partitions(pool, 4, "ap", "pap")

                def body(i):
                    for hf in range(2):
                        if not isinstance(i, int):
                            count = valued(pool, 16 * i)
                            unregistered(pool, i)
                            wait(pool, f"raw_in{hf}", count)
                        if isinstance(i, int) and hf == 0:
                            wait(pool, "sc_r", scalars_at[3])
                        wait(pool, f"o_r{hf}", i)
                        nc.gpsimd.tensor_scalar(gq[hf][:], raw[hf][:], col["inv_u"], 0.0, ALU.mult, ALU.add
                                                ).then_inc(S[f"uq_r{hf}"], 1)

                from_zero(pool, CH, body)
                over_partitions(pool, 5, "ao", "pao")

            @block.sync
            def _(sp):
                def body(c):
                    for hf in range(2):
                        wait(sp, f"raw_r{hf}", c + 1)
                        sp.dma_start(up_raw.ap()[bass.ds(c, 1), hf].rearrange("a p n -> (a p) n"), raw[hf][:]
                                     ).then_inc(S[f"raw_out{hf}"], 16)

                from_zero(sp, CH - 1, body)
                for hf in range(2):
                    wait(sp, f"raw_out{hf}", 16 * (CH - 1))

                with sp.Fori(1, CH) as i:
                    for hf in range(2):
                        wait(sp, f"uq_r{hf}", i)
                        sp.dma_start(raw[hf][:], up_raw.ap()[bass.ds(turn(i), 1), hf].rearrange("a p n -> (a p) n")
                                     ).then_inc(S[f"raw_in{hf}"], 16)
        pf.close()

        oq = sb("oq", [128, MT, 2 * N], I16)
        oh = [sb(f"oh{i}", [128, MT, 2 * N], F16) for i in range(2)]
        ol = [sb(f"ol{i}", [128, MT, 2 * N], F16) for i in range(2)]
        hin = [sb(f"hin{i}", [128, 2 * C]) for i in range(4)]
        y = [sb(f"y{i}", [128, 2 * C]) for i in range(4)]

        def flat(t, hf):
            return t[:, 3 * hf:3 * hf + 3].rearrange("p m n -> p (m n)")

        with nc.Block() as block:
            @block.scalar
            def _(act):
                def body(k):
                    for par in range(2):
                        c = 2 * k + par
                        wait(act, "ol_r", 2 * c)
                        for hf in range(2):
                            nc.scalar.activation(flat(oq, hf), unit(2 * c + hf), ACT.Copy, scale=col["inv_o"]
                                                 ).then_inc(S["oq_r"], 1)
                            wait(act, "oq_r", 2 * c + hf + 1)
                            if hf == 0:
                                for bb in range(2):
                                    wait(act, f"dn_ps{2 * par + bb}", k)
                            nc.scalar.activation(flat(oh[par], hf), flat(oq, hf), ACT.Copy).then_inc(S["oh_r"], 1)

                from_zero(act, CH // 2, body)

            @block.vector
            def _(dve):
                def low(k, par):
                    c = 2 * k + par
                    for hf in range(2):
                        wait(dve, "oh_r", 2 * c + hf + 1)
                        if hf == 0:
                            for bb in range(2):
                                wait(dve, f"dn_ps{2 * par + bb}", k)
                        nc.vector.tensor_tensor(flat(ol[par], hf), flat(oq, hf), flat(oh[par], hf), ALU.subtract
                                                ).then_inc(S["ol_r"], 1)

                def finish(k, par):
                    for bb in range(2):
                        s = 2 * par + bb
                        wait(dve, f"dn_ps{s}", k + 1)
                        wait(dve, f"h_in{s}", 16 * (k + 1))
                        wait(dve, f"y_out{s}", 16 * k)
                        nc.vector.scalar_tensor_tensor(y[s][0:TT], ps[0:TT, s, :], col["size_y"][0:TT],
                                                       hin[s][0:TT], ALU.mult, ALU.add).then_inc(S[f"y_r{s}"], 1)

                low(0, 0)
                times(dve, "size_o", "step_o", col["unit_o"])
                times(dve, "size_y", "size_o", wscale[:, W_DOWN:W_DOWN + 1])
                def body(k):
                    low(k, 1)
                    finish(k, 0)
                    low(k + 1, 0)
                    finish(k, 1)

                from_zero(dve, CH // 2 - 1, body)
                low(CH // 2 - 1, 1)
                finish(CH // 2 - 1, 0)
                finish(CH // 2 - 1, 1)

            @block.tensor
            def _(pe):
                def body(k):
                    for par in range(2):
                        wait(pe, "ol_r", 2 * (2 * k + par) + 1)
                        for bb in range(2):
                            s = 2 * par + bb
                            wait(pe, f"y_r{s}", k)
                            for t in range(2):
                                rows = slice(bb * N + t * TT, bb * N + (t + 1) * TT)
                                for m in range(MT):
                                    if m == MT // 2 and bb == 0 and t == 0:
                                        wait(pe, "ol_r", 2 * (2 * k + par) + 2)
                                    for i, (o, w) in enumerate(((oh, 0), (ol, 0), (oh, 1))):
                                        last = nc.tensor.matmul(ps[0:TT, s, t * C:(t + 1) * C], o[par][:, m, rows],
                                                                wdT[:, w, m], start=(m == 0 and i == 0),
                                                                stop=(m == MT - 1 and i == 2))
                            last.then_inc(S[f"dn_ps{s}"], 1)

                from_zero(pe, CH // 2, body)

            @block.sync
            def _(sp):
                def load(k, s):
                    sp.dma_start(hin[s][0:TT], res.ap()[bass.ds(4 * k + s, 1)].rearrange("a p n -> (a p) n")
                                 ).then_inc(S[f"h_in{s}"], 16)

                def store(k, s):
                    count = valued(sp, k + 1)
                    dst = out[bass.ds(4 * k + s, 1)].rearrange("a (t p) c -> p (a t) c", p=TT)
                    unregistered(sp, k)
                    wait(sp, f"y_r{s}", count)
                    sp.dma_start(dst, y[s][0:TT].rearrange("p (t c) -> p t c", t=2)).then_inc(S[f"y_out{s}"], 16)

                for s in range(4):
                    load(0, s)
                def body(k):
                    for s in range(4):
                        store(k, s)
                        load(k + 1, s)

                from_zero(sp, CH // 2 - 1, body)
                for s in range(4):
                    store(CH // 2 - 1, s)
                for s in range(4):
                    wait(sp, f"y_out{s}", 16 * (CH // 2))


def kernel(x, L0_tok_W, L0_tok_b, L0_tok_gamma, L0_tok_beta, L0_tok_running_mean, L0_tok_running_var, L0_attn_Wq,
           L0_attn_Wk, L0_attn_Wv, L0_attn_Wo, L0_attn_bo, L0_attn_rel_emb, L0_ffn_w_gate, L0_ffn_w_up,
           L0_ffn_w_down):
    import concourse.bacc as bacc
    from concourse.bass_utils import run_bass_kernel_spmd

    nc = bacc.Bacc("TRN2", target_bir_lowering=False, num_devices=1)
    given = dict(x=x, cw=L0_tok_W, cb=L0_tok_b, gamma=L0_tok_gamma, beta=L0_tok_beta, rmean=L0_tok_running_mean,
                 rvar=L0_tok_running_var, wq=L0_attn_Wq, wk=L0_attn_Wk, wv=L0_attn_Wv, wo=L0_attn_Wo, bo=L0_attn_bo,
                 rel=L0_attn_rel_emb, wg=L0_ffn_w_gate, wu=L0_ffn_w_up, wd=L0_ffn_w_down, hot=bucket_onehot())
    arrays, args = {}, {}
    for name, a in given.items():
        arrays["in_" + name] = np.ascontiguousarray(a)
        args[name] = nc.dram_tensor("in_" + name, arrays["in_" + name].shape, F32, kind="ExternalInput").ap()
    out = nc.dram_tensor("out", (B, N, C), F32, kind="ExternalOutput").ap()
    audio_tower(nc, out=out, **args)
    r = run_bass_kernel_spmd(nc, [arrays], core_ids=[0])
    return r.results[0]["out"]
```
